# Optimizing a Trainium2 kernel written in Bass

```python
import numpy as np
import jax
import jax.numpy as jnp

def _softmax(x, axis=-1):
    return jax.nn.softmax(x, axis=axis)

def _gelu(x):
    return jax.nn.gelu(x, approximate=True)

def _silu(x):
    return jax.nn.silu(x)

def _sigmoid(x):
    return jax.nn.sigmoid(x)

def _layernorm(x, axis=-1, eps=1e-05):
    m = jnp.mean(x, axis=axis, keepdims=True)
    v = jnp.var(x, axis=axis, keepdims=True)
    return (x - m) / jnp.sqrt(v + eps)

def _scatter_add(tgt, idx, src, axis=0):
    return tgt.at[idx].add(src)

def _segment_sum(src, seg, n):
    return jax.ops.segment_sum(src, seg, n)
kernel_name = 'mk_audio_tower_d4_tok_audfeat1024_r4_0fc6c4'

def setup_inputs(seed: int=0):
    np.random.seed(seed)
    _w = jnp.asarray

    def _rec_inputs():
        import jax
        import jax.numpy as jnp
        _rk = jax.random.key(seed)
        x = -0.000123307 + 1.00004 * jax.random.normal(jax.random.fold_in(_rk, 1), (32, 375, 80), jnp.float32)
        return x
    x = _rec_inputs()

    def _L0_tok_setup():
        import jax, jax.numpy as jnp
        import numpy as np
        NUM_FRAMES = 8
        STRIDE = 4
        BN_EPS = 1e-05
        key = jax.random.key(seed)
        ks = jax.random.split(key, 7)
        B, L, D = (32, 1024, 80)
        H1, H2 = (256, 256)
        x = jax.random.normal(ks[0], (B, L, D), dtype=jnp.float32)
        W1 = jax.random.normal(ks[1], (D * NUM_FRAMES, H1), dtype=jnp.float32) * (1.0 / np.sqrt(D * NUM_FRAMES))
        b1 = jax.random.normal(ks[2], (H1,), dtype=jnp.float32) * 0.01
        W2 = jax.random.normal(ks[3], (H1, H2), dtype=jnp.float32) * (1.0 / np.sqrt(H1))
        b2 = jax.random.normal(ks[4], (H2,), dtype=jnp.float32) * 0.01
        gamma = 1.0 + 0.1 * jax.random.normal(ks[5], (H2,), dtype=jnp.float32)
        beta = 0.1 * jax.random.normal(ks[6], (H2,), dtype=jnp.float32)
        return {'x': x, 'W1': W1, 'b1': b1, 'W2': W2, 'b2': b2, 'gamma': gamma, 'beta': beta}
    _L0_tok_all = _L0_tok_setup()
    _L0_tok_in = {k: v for k, v in _L0_tok_all.items() if k in ('W1', 'b1', 'W2', 'b2', 'gamma', 'beta')}
    del _L0_tok_all

    def _L0_attn_setup():
        import jax, jax.numpy as jnp
        import numpy as np
        H = 256
        NH = 16
        HD = H // NH
        B, S = (2, 512)
        key = jax.random.key(seed)
        ks = jax.random.split(key, 6)
        std = 0.02
        x = jax.random.normal(ks[0], (B, S, H), dtype=jnp.float32)
        w_qkv = jax.random.normal(ks[1], (3 * H, H), dtype=jnp.float32) * std
        b_qkv = jnp.zeros((3 * H,), dtype=jnp.float32)
        ln_g = jnp.ones((H,), dtype=jnp.float32)
        ln_b = jnp.zeros((H,), dtype=jnp.float32)
        w_ent = jax.random.normal(ks[2], (1, H), dtype=jnp.float32) * std
        b_ent = jnp.zeros((1,), dtype=jnp.float32)
        w_out = jax.random.normal(ks[3], (H, H), dtype=jnp.float32) * std
        b_out = jnp.zeros((H,), dtype=jnp.float32)
        return {'x': x, 'ln_g': ln_g, 'ln_b': ln_b, 'w_qkv': w_qkv, 'b_qkv': b_qkv, 'w_ent': w_ent, 'b_ent': b_ent, 'w_out': w_out, 'b_out': b_out}
    _L0_attn_all = _L0_attn_setup()
    _L0_attn_in = {k: v for k, v in _L0_attn_all.items() if k in ('ln_g', 'ln_b', 'w_qkv', 'b_qkv', 'w_ent', 'b_ent', 'w_out', 'b_out')}
    del _L0_attn_all

    def _L0_ffn_setup():
        import jax, jax.numpy as jnp
        import numpy as np
        EPS = 1e-05
        key = jax.random.key(seed)
        kx, kw, kb = jax.random.split(key, 3)
        B, S, K, N = (8, 2048, 256, 256)
        x = jax.random.normal(kx, (B, S, K), dtype=jnp.float32)
        W = jax.random.normal(kw, (N, K), dtype=jnp.float32) * 0.02
        weight_scale = jnp.maximum(jnp.max(jnp.abs(W), axis=1, keepdims=True) / 127.0, EPS)
        weight_int8 = jnp.clip(jnp.round(W / weight_scale), -128, 127).astype(jnp.int8)
        bias = jax.random.normal(kb, (N,), dtype=jnp.float32) * 0.01
        return {'x': x, 'weight_int8': weight_int8, 'weight_scale': weight_scale, 'bias': bias}
    _L0_ffn_all = _L0_ffn_setup()
    _L0_ffn_in = {k: v for k, v in _L0_ffn_all.items() if k in ('weight_int8', 'weight_scale', 'bias')}
    del _L0_ffn_all

    def _L1_attn_setup():
        import jax, jax.numpy as jnp
        import numpy as np
        key = jax.random.key(seed)
        ks = jax.random.split(key, 5)
        B, T, C = (2, 512, 256)
        x = jax.random.normal(ks[0], (B, T, C), dtype=jnp.float32)
        Wqkv = jax.random.normal(ks[1], (C, 3 * C), dtype=jnp.float32) * C ** (-0.5)
        bqkv = jax.random.normal(ks[2], (3 * C,), dtype=jnp.float32) * 0.02
        Wproj = jax.random.normal(ks[3], (C, C), dtype=jnp.float32) * C ** (-0.5)
        bproj = jax.random.normal(ks[4], (C,), dtype=jnp.float32) * 0.02
        return {'x': x, 'Wqkv': Wqkv, 'bqkv': bqkv, 'Wproj': Wproj, 'bproj': bproj}
    _L1_attn_all = _L1_attn_setup()
    _L1_attn_in = {k: v for k, v in _L1_attn_all.items() if k in ('Wqkv', 'bqkv', 'Wproj', 'bproj')}
    del _L1_attn_all

    def _L1_ffn_setup():
        import jax, jax.numpy as jnp
        import numpy as np
        B, N, D = (4, 512, 256)
        SPARSITY = 0.01
        key = jax.random.key(seed)
        k1, k2, k3 = jax.random.split(key, 3)
        x = jax.random.normal(k1, (B, N, D), dtype=jnp.float32)
        spatial = jax.random.normal(k2, (D, D), dtype=jnp.float32) * 0.02
        freq = jnp.fft.fft(spatial, axis=-1)
        k = int(D * SPARSITY)
        mag = jnp.abs(freq)
        kth = jax.lax.top_k(mag, k)[0][:, -1:]
        w_sparse = jnp.where(mag >= kth, freq, 0.0 + 0j)
        bias = jax.random.normal(k3, (D,), dtype=jnp.float32) * 0.01
        return {'x': x, 'w_freq_real': jnp.real(w_sparse).astype(jnp.float32), 'w_freq_imag': jnp.imag(w_sparse).astype(jnp.float32), 'bias': bias}
    _L1_ffn_all = _L1_ffn_setup()
    _L1_ffn_in = {k: v for k, v in _L1_ffn_all.items() if k in ('w_freq_real', 'w_freq_imag', 'bias')}
    del _L1_ffn_all

    def _L2_attn_setup():
        import jax, jax.numpy as jnp
        import numpy as np
        import math
        N_EMBD = 256
        N_HEAD = 16
        HEAD_DIM = N_EMBD // N_HEAD // 2
        DEPTH = 1
        LAMBDA_INIT = 0.8 - 0.6 * math.exp(-0.3 * (DEPTH - 1))
        EPS = 1e-05
        key = jax.random.key(seed)
        ks = jax.random.split(key, 8)
        B, T, C = (4, 256, N_EMBD)
        x = jax.random.normal(ks[0], (B, T, C), dtype=jnp.float32)
        w_attn = jax.random.normal(ks[1], (C, 3 * C), dtype=jnp.float32) * (1.0 / math.sqrt(C))
        w_proj = jax.random.normal(ks[2], (C, C), dtype=jnp.float32) * (1.0 / math.sqrt(C))
        lambda_q1 = jax.random.normal(ks[3], (HEAD_DIM,), dtype=jnp.float32) * 0.1
        lambda_q2 = jax.random.normal(ks[4], (HEAD_DIM,), dtype=jnp.float32) * 0.1
        lambda_k1 = jax.random.normal(ks[5], (HEAD_DIM,), dtype=jnp.float32) * 0.1
        lambda_k2 = jax.random.normal(ks[6], (HEAD_DIM,), dtype=jnp.float32) * 0.1
        gamma = jnp.ones((2 * HEAD_DIM,), dtype=jnp.float32)
        return {'x': x, 'w_attn': w_attn, 'w_proj': w_proj, 'lambda_q1': lambda_q1, 'lambda_q2': lambda_q2, 'lambda_k1': lambda_k1, 'lambda_k2': lambda_k2, 'gamma': gamma}
    _L2_attn_all = _L2_attn_setup()
    _L2_attn_in = {k: v for k, v in _L2_attn_all.items() if k in ('w_attn', 'w_proj', 'lambda_q1', 'lambda_q2', 'lambda_k1', 'lambda_k2', 'gamma')}
    del _L2_attn_all

    def _L2_ffn_setup():
        import jax, jax.numpy as jnp
        import numpy as np
        B, T, D, F, E, TOP_K = (4, 1024, 256, 1024, 8, 2)
        key = jax.random.key(seed)
        kx, kr, k1, k2 = jax.random.split(key, 4)
        x = jax.random.normal(kx, (B, T, D), dtype=jnp.float32)
        Wr = jax.random.normal(kr, (D, E), dtype=jnp.float32) * 0.02
        W1 = jax.random.normal(k1, (E, D, F), dtype=jnp.float32) * 0.02
        W2 = jax.random.normal(k2, (E, F, D), dtype=jnp.float32) * 0.02
        return {'x': x, 'Wr': Wr, 'W1': W1, 'W2': W2}
    _L2_ffn_all = _L2_ffn_setup()
    _L2_ffn_in = {k: v for k, v in _L2_ffn_all.items() if k in ('Wr', 'W1', 'W2')}
    del _L2_ffn_all

    def _L3_attn_setup():
        import jax, jax.numpy as jnp
        import numpy as np
        B_, L_, D_MODEL = (4, 512, 256)
        EXPAND, D_STATE, D_CONV = (2, 16, 4)
        D_IN = EXPAND * D_MODEL
        DT_RANK = D_MODEL // 16
        LN_EPS = 1e-05

        def _mamba(x, W_in, conv_w, conv_b, W_x, W_dt, b_dt, A_log, D):
            Bb, L, _ = x.shape
            xz = x @ W_in
            x_in, z = (xz[..., :D_IN], xz[..., D_IN:])
            xp = jnp.pad(x_in, ((0, 0), (D_CONV - 1, 0), (0, 0)))
            xc = conv_b
            for k in range(D_CONV):
                xc = xc + xp[:, k:k + L, :] * conv_w[:, k]
            xc = jax.nn.silu(xc)
            dbc = xc @ W_x
            dt = dbc[..., :DT_RANK]
            Bm = dbc[..., DT_RANK:DT_RANK + D_STATE]
            Cm = dbc[..., DT_RANK + D_STATE:]
            delta = jax.nn.softplus(dt @ W_dt + b_dt)
            A = -jnp.exp(A_log)
            u_t = jnp.swapaxes(xc, 0, 1)
            d_t = jnp.swapaxes(delta, 0, 1)
            B_t = jnp.swapaxes(Bm, 0, 1)
            C_t = jnp.swapaxes(Cm, 0, 1)

            def step(h, inp):
                u, d, b, c = inp
                dA = jnp.exp(d[..., None] * A)
                h = h * dA + (d * u)[..., None] * b[:, None, :]
                y = jnp.einsum('bds,bs->bd', h, c)
                return (h, y)
            h0 = jnp.zeros((Bb, D_IN, D_STATE), dtype=x.dtype)
            _, ys = jax.lax.scan(step, h0, (u_t, d_t, B_t, C_t))
            y = jnp.swapaxes(ys, 0, 1) + xc * D
            y = y * jax.nn.silu(z)
            return y @ (W_in[:0, :0] if False else None) if False else y
        key = jax.random.key(seed)
        ks = jax.random.split(key, 8)
        s = 0.02
        x = jax.random.normal(ks[0], (B_, L_, D_MODEL), dtype=jnp.float32)
        W_in = jax.random.normal(ks[1], (D_MODEL, 2 * D_IN), dtype=jnp.float32) * s
        conv_w = jax.random.normal(ks[2], (D_IN, D_CONV), dtype=jnp.float32) * 0.1
        conv_b = jnp.zeros((D_IN,), dtype=jnp.float32)
        W_x = jax.random.normal(ks[3], (D_IN, DT_RANK + 2 * D_STATE), dtype=jnp.float32) * s
        W_dt = jax.random.normal(ks[4], (DT_RANK, D_IN), dtype=jnp.float32) * s
        b_dt = jnp.log(jnp.expm1(jnp.full((D_IN,), 0.01, dtype=jnp.float32)))
        A_log = jnp.log(jnp.broadcast_to(jnp.arange(1, D_STATE + 1, dtype=jnp.float32), (D_IN, D_STATE)))
        Dp = jnp.ones((D_IN,), dtype=jnp.float32)
        W_out = jax.random.normal(ks[5], (D_IN, D_MODEL), dtype=jnp.float32) * s
        gamma = jnp.ones((D_MODEL,), dtype=jnp.float32)
        beta = jnp.zeros((D_MODEL,), dtype=jnp.float32)
        return dict(x=x, W_in=W_in, conv_w=conv_w, conv_b=conv_b, W_x=W_x, W_dt=W_dt, b_dt=b_dt, A_log=A_log, D=Dp, W_out=W_out, gamma=gamma, beta=beta)
    _L3_attn_all = _L3_attn_setup()
    _L3_attn_in = {k: v for k, v in _L3_attn_all.items() if k in ('W_in', 'conv_w', 'conv_b', 'W_x', 'W_dt', 'b_dt', 'A_log', 'D', 'W_out', 'gamma', 'beta')}
    del _L3_attn_all

    def _L3_ffn_setup():
        import jax, jax.numpy as jnp
        import numpy as np
        E, TOPK, R = (8, 2, 16)
        D, H, GH = (256, 16, 64)
        HD = D // H
        SCALE = HD ** (-0.5)

        def _svd_moe(x, Wm, U, S, V, b, idx, gates):
            main = jnp.einsum('bsd,od->bso', x, Wm)
            Ug, Sg, Vg = (U[idx], S[idx], V[idx])
            xv = jnp.einsum('bsd,bkrd->bksr', x, Vg)
            xvs = xv * Sg[:, :, None, :]
            eo = jnp.einsum('bksr,bkor->bkso', xvs, Ug)
            expert = jnp.einsum('bkso,bk->bso', eo, gates)
            return main + expert + b
        key = jax.random.key(seed)
        ks = jax.random.split(key, 32)
        B, S = (32, 257)
        inp = {'hidden_states': jax.random.normal(ks[0], (B, S, D), jnp.float32)}
        inp['gw1'] = jax.random.normal(ks[1], (GH, D), jnp.float32) * 0.02
        inp['gb1'] = jnp.zeros((GH,), jnp.float32)
        inp['gw2'] = jax.random.normal(ks[2], (E, GH), jnp.float32) * 0.02
        inp['gb2'] = jnp.zeros((E,), jnp.float32)
        i = 3
        for p in ('q', 'k', 'v', 'o'):
            inp[p + 'Wm'] = jax.random.normal(ks[i], (D, D), jnp.float32) * 0.02
            i += 1
            inp[p + 'U'] = jax.random.normal(ks[i], (E, D, R), jnp.float32) * 0.02
            i += 1
            inp[p + 'S'] = jax.random.normal(ks[i], (E, R), jnp.float32) * 0.1
            i += 1
            inp[p + 'V'] = jax.random.normal(ks[i], (E, R, D), jnp.float32) * 0.02
            i += 1
            inp[p + 'b'] = jnp.zeros((D,), jnp.float32)
        return inp
    _L3_ffn_all = _L3_ffn_setup()
    _L3_ffn_in = {k: v for k, v in _L3_ffn_all.items() if k in ('gw1', 'gb1', 'gw2', 'gb2', 'qWm', 'qU', 'qS', 'qV', 'qb', 'kWm', 'kU', 'kS', 'kV', 'kb', 'vWm', 'vU', 'vS', 'vV', 'vb', 'oWm', 'oU', 'oS', 'oV', 'ob')}
    del _L3_ffn_all
    return {'x': x, 'L0_tok_W1': _L0_tok_in['W1'], 'L0_tok_b1': _L0_tok_in['b1'], 'L0_tok_W2': _L0_tok_in['W2'], 'L0_tok_b2': _L0_tok_in['b2'], 'L0_tok_gamma': _L0_tok_in['gamma'], 'L0_tok_beta': _L0_tok_in['beta'], 'L0_attn_ln_g': _L0_attn_in['ln_g'], 'L0_attn_ln_b': _L0_attn_in['ln_b'], 'L0_attn_w_qkv': _L0_attn_in['w_qkv'], 'L0_attn_b_qkv': _L0_attn_in['b_qkv'], 'L0_attn_w_ent': _L0_attn_in['w_ent'], 'L0_attn_b_ent': _L0_attn_in['b_ent'], 'L0_attn_w_out': _L0_attn_in['w_out'], 'L0_attn_b_out': _L0_attn_in['b_out'], 'L0_ffn_weight_int8': _L0_ffn_in['weight_int8'], 'L0_ffn_weight_scale': _L0_ffn_in['weight_scale'], 'L0_ffn_bias': _L0_ffn_in['bias'], 'L1_attn_Wqkv': _L1_attn_in['Wqkv'], 'L1_attn_bqkv': _L1_attn_in['bqkv'], 'L1_attn_Wproj': _L1_attn_in['Wproj'], 'L1_attn_bproj': _L1_attn_in['bproj'], 'L1_ffn_w_freq_real': _L1_ffn_in['w_freq_real'], 'L1_ffn_w_freq_imag': _L1_ffn_in['w_freq_imag'], 'L1_ffn_bias': _L1_ffn_in['bias'], 'L2_attn_w_attn': _L2_attn_in['w_attn'], 'L2_attn_w_proj': _L2_attn_in['w_proj'], 'L2_attn_lambda_q1': _L2_attn_in['lambda_q1'], 'L2_attn_lambda_q2': _L2_attn_in['lambda_q2'], 'L2_attn_lambda_k1': _L2_attn_in['lambda_k1'], 'L2_attn_lambda_k2': _L2_attn_in['lambda_k2'], 'L2_attn_gamma': _L2_attn_in['gamma'], 'L2_ffn_Wr': _L2_ffn_in['Wr'], 'L2_ffn_W1': _L2_ffn_in['W1'], 'L2_ffn_W2': _L2_ffn_in['W2'], 'L3_attn_W_in': _L3_attn_in['W_in'], 'L3_attn_conv_w': _L3_attn_in['conv_w'], 'L3_attn_conv_b': _L3_attn_in['conv_b'], 'L3_attn_W_x': _L3_attn_in['W_x'], 'L3_attn_W_dt': _L3_attn_in['W_dt'], 'L3_attn_b_dt': _L3_attn_in['b_dt'], 'L3_attn_A_log': _L3_attn_in['A_log'], 'L3_attn_D': _L3_attn_in['D'], 'L3_attn_W_out': _L3_attn_in['W_out'], 'L3_attn_gamma': _L3_attn_in['gamma'], 'L3_attn_beta': _L3_attn_in['beta'], 'L3_ffn_gw1': _L3_ffn_in['gw1'], 'L3_ffn_gb1': _L3_ffn_in['gb1'], 'L3_ffn_gw2': _L3_ffn_in['gw2'], 'L3_ffn_gb2': _L3_ffn_in['gb2'], 'L3_ffn_qWm': _L3_ffn_in['qWm'], 'L3_ffn_qU': _L3_ffn_in['qU'], 'L3_ffn_qS': _L3_ffn_in['qS'], 'L3_ffn_qV': _L3_ffn_in['qV'], 'L3_ffn_qb': _L3_ffn_in['qb'], 'L3_ffn_kWm': _L3_ffn_in['kWm'], 'L3_ffn_kU': _L3_ffn_in['kU'], 'L3_ffn_kS': _L3_ffn_in['kS'], 'L3_ffn_kV': _L3_ffn_in['kV'], 'L3_ffn_kb': _L3_ffn_in['kb'], 'L3_ffn_vWm': _L3_ffn_in['vWm'], 'L3_ffn_vU': _L3_ffn_in['vU'], 'L3_ffn_vS': _L3_ffn_in['vS'], 'L3_ffn_vV': _L3_ffn_in['vV'], 'L3_ffn_vb': _L3_ffn_in['vb'], 'L3_ffn_oWm': _L3_ffn_in['oWm'], 'L3_ffn_oU': _L3_ffn_in['oU'], 'L3_ffn_oS': _L3_ffn_in['oS'], 'L3_ffn_oV': _L3_ffn_in['oV'], 'L3_ffn_ob': _L3_ffn_in['ob']}

def reference(x, L0_tok_W1, L0_tok_b1, L0_tok_W2, L0_tok_b2, L0_tok_gamma, L0_tok_beta, L0_attn_ln_g, L0_attn_ln_b, L0_attn_w_qkv, L0_attn_b_qkv, L0_attn_w_ent, L0_attn_b_ent, L0_attn_w_out, L0_attn_b_out, L0_ffn_weight_int8, L0_ffn_weight_scale, L0_ffn_bias, L1_attn_Wqkv, L1_attn_bqkv, L1_attn_Wproj, L1_attn_bproj, L1_ffn_w_freq_real, L1_ffn_w_freq_imag, L1_ffn_bias, L2_attn_w_attn, L2_attn_w_proj, L2_attn_lambda_q1, L2_attn_lambda_q2, L2_attn_lambda_k1, L2_attn_lambda_k2, L2_attn_gamma, L2_ffn_Wr, L2_ffn_W1, L2_ffn_W2, L3_attn_W_in, L3_attn_conv_w, L3_attn_conv_b, L3_attn_W_x, L3_attn_W_dt, L3_attn_b_dt, L3_attn_A_log, L3_attn_D, L3_attn_W_out, L3_attn_gamma, L3_attn_beta, L3_ffn_gw1, L3_ffn_gb1, L3_ffn_gw2, L3_ffn_gb2, L3_ffn_qWm, L3_ffn_qU, L3_ffn_qS, L3_ffn_qV, L3_ffn_qb, L3_ffn_kWm, L3_ffn_kU, L3_ffn_kS, L3_ffn_kV, L3_ffn_kb, L3_ffn_vWm, L3_ffn_vU, L3_ffn_vS, L3_ffn_vV, L3_ffn_vb, L3_ffn_oWm, L3_ffn_oU, L3_ffn_oS, L3_ffn_oV, L3_ffn_ob):
    import jax
    import jax.numpy as jnp

    def _L0_tok_ref(x, W1, b1, W2, b2, gamma, beta):
        import jax, jax.numpy as jnp
        import numpy as np
        NUM_FRAMES = 8
        STRIDE = 4
        BN_EPS = 1e-05
        B, L, D = x.shape
        remove_top = L - NUM_FRAMES
        if remove_top < 0:
            pad = -remove_top
        else:
            pad = STRIDE - remove_top % STRIDE
        xp = jnp.pad(x, ((0, 0), (0, pad), (0, 0)))
        Lp = L + pad
        num_slices = 1 + (Lp - NUM_FRAMES) // STRIDE
        idx = np.arange(num_slices)[:, None] * STRIDE + np.arange(NUM_FRAMES)[None, :]
        win = xp[:, idx, :].reshape(B, num_slices, NUM_FRAMES * D)
        h = jax.nn.relu(jnp.einsum('bsk,kh->bsh', win, W1) + b1)
        h = jax.nn.relu(jnp.einsum('bsk,kh->bsh', h, W2) + b2)
        mean = jnp.mean(h, axis=(0, 1))
        var = jnp.var(h, axis=(0, 1))
        out = (h - mean) * jax.lax.rsqrt(var + BN_EPS) * gamma + beta
        return out

    def _L0_attn_ref(x, ln_g, ln_b, w_qkv, b_qkv, w_ent, b_ent, w_out, b_out):
        import jax, jax.numpy as jnp
        import numpy as np
        H = 256
        NH = 16
        HD = H // NH
        B, S = (2, 512)
        b, s, h = x.shape
        scale = 1.0 / jnp.sqrt(jnp.float32(HD))
        TEMP = 0.1
        mu = jnp.mean(x, axis=-1, keepdims=True)
        var = jnp.mean(jnp.square(x - mu), axis=-1, keepdims=True)
        xn = (x - mu) / jnp.sqrt(var + 1e-06) * ln_g + ln_b
        qkv = xn @ w_qkv.T + b_qkv
        qkv = qkv.reshape(b, s, 3, NH, HD).transpose(2, 0, 3, 1, 4)
        q, k, v = (qkv[0], qkv[1], qkv[2])
        scores = jnp.einsum('bhqd,bhkd->bhqk', q, k) * scale
        causal = jnp.tril(jnp.ones((s, s), dtype=bool))
        scores = jnp.where(causal[None, None], scores, -jnp.inf)
        probs = jax.nn.softmax(scores / TEMP, axis=-1)
        gate = jax.nn.sigmoid(xn @ w_ent.T + b_ent)
        gate = jnp.clip(gate, 0.1, 2.0)[:, None, None, :, 0]
        probs = probs * gate
        out = jnp.einsum('bhqk,bhkd->bhqd', probs, v)
        out = out.transpose(0, 2, 1, 3).reshape(b, s, h)
        return (out @ w_out.T + b_out) * 0.1

    def _L0_ffn_ref(x, weight_int8, weight_scale, bias):
        import jax, jax.numpy as jnp
        import numpy as np
        EPS = 1e-05
        B, S, K = x.shape
        x2 = x.reshape(-1, K)
        x_scale = jnp.maximum(jnp.abs(x2).max() / 127.0, EPS)
        x_int8 = jnp.clip(jnp.round(x2 / x_scale), -128, 127).astype(jnp.int8)
        acc_i32 = jax.lax.dot_general(x_int8, weight_int8.T, dimension_numbers=(((1,), (0,)), ((), ())), preferred_element_type=jnp.int32)
        out = acc_i32.astype(jnp.float32) * x_scale * weight_scale.T
        out = out + bias
        return out.reshape(B, S, -1)

    def _L1_attn_ref(x, Wqkv, bqkv, Wproj, bproj):
        import jax, jax.numpy as jnp
        import numpy as np
        B, T, C = x.shape
        n_head = 16
        hd = C // n_head
        x_proj = x @ Wqkv + bqkv
        q = x_proj[:, :, :C].reshape(B, n_head, T, hd)
        k = x_proj[:, :, C:2 * C].reshape(B, n_head, T, hd)
        v = x_proj[:, :, 2 * C:].reshape(B, n_head, T, hd)
        att = jnp.einsum('bhtd,bhsd->bhts', q, k) * (1.0 / jnp.sqrt(jnp.float32(hd)))
        causal = jnp.tril(jnp.ones((T, T), dtype=bool))
        att = jnp.where(causal, att, jnp.float32(-jnp.inf))
        att = jax.nn.softmax(att, axis=-1)
        y = att @ v
        y = jnp.transpose(y, (0, 2, 1, 3)).reshape(B, T, C)
        return y @ Wproj + bproj

    def _L1_ffn_ref(x, w_freq_real, w_freq_imag, bias):
        import jax, jax.numpy as jnp
        import numpy as np
        B, N, D = (4, 512, 256)
        SPARSITY = 0.01
        w = jax.lax.complex(w_freq_real, w_freq_imag)
        x_freq = jnp.fft.fft(x, axis=-1)
        y_freq = jnp.einsum('bnd,do->bno', x_freq, w)
        y = jnp.real(jnp.fft.ifft(y_freq, axis=-1))
        return y + bias

    def _L2_attn_ref(x, w_attn, w_proj, lambda_q1, lambda_q2, lambda_k1, lambda_k2, gamma):
        import jax, jax.numpy as jnp
        import numpy as np
        import math
        N_EMBD = 256
        N_HEAD = 16
        HEAD_DIM = N_EMBD // N_HEAD // 2
        DEPTH = 1
        LAMBDA_INIT = 0.8 - 0.6 * math.exp(-0.3 * (DEPTH - 1))
        EPS = 1e-05
        B, T, C = x.shape
        H, hd = (N_HEAD, HEAD_DIM)
        qkv = x @ w_attn
        q, k, v = jnp.split(qkv, 3, axis=-1)
        q = q.reshape(B, T, 2 * H, hd).transpose(0, 2, 1, 3)
        k = k.reshape(B, T, 2 * H, hd).transpose(0, 2, 1, 3)
        v = v.reshape(B, T, H, 2 * hd).transpose(0, 2, 1, 3)
        q = q * hd ** (-0.5)
        att = jnp.einsum('bhtd,bhsd->bhts', q, k) * (1.0 / math.sqrt(hd))
        causal = jnp.tril(jnp.ones((T, T), dtype=bool))
        att = jnp.where(causal, att, -jnp.inf)
        att = jax.nn.softmax(att, axis=-1)
        lam1 = jnp.exp(jnp.sum(lambda_q1 * lambda_k1))
        lam2 = jnp.exp(jnp.sum(lambda_q2 * lambda_k2))
        lambda_full = lam1 - lam2 + LAMBDA_INIT
        att = att.reshape(B, H, 2, T, T)
        att = att[:, :, 0] - lambda_full * att[:, :, 1]
        out = jnp.einsum('bhts,bhsd->bhtd', att, v)
        rms = jax.lax.rsqrt(jnp.mean(out * out, axis=-1, keepdims=True) + EPS)
        out = out * rms * gamma
        out = (1.0 - LAMBDA_INIT) * out
        out = out.transpose(0, 2, 1, 3).reshape(B, T, C)
        return out @ w_proj

    def _L2_ffn_ref(x, Wr, W1, W2):
        import jax, jax.numpy as jnp
        import numpy as np
        B, T, D, F, E, TOP_K = (4, 1024, 256, 1024, 8, 2)
        b, t, d = x.shape
        n_experts = W1.shape[0]
        xf = x.reshape(-1, d)
        logits = xf @ Wr
        probs = jax.nn.softmax(logits, axis=-1)
        weights, indices = jax.lax.top_k(probs, TOP_K)
        out = jnp.zeros_like(xf)
        for e in range(n_experts):
            h = jax.nn.gelu(xf @ W1[e], approximate=False) @ W2[e]
            coeff = jnp.sum(jnp.where(indices == e, weights, 0.0), axis=-1)
            out = out + coeff[:, None] * h
        return out.reshape(b, t, d)

    def _L3_attn_ref(x, W_in, conv_w, conv_b, W_x, W_dt, b_dt, A_log, D, W_out, gamma, beta):
        import jax, jax.numpy as jnp
        import numpy as np
        B_, L_, D_MODEL = (4, 512, 256)
        EXPAND, D_STATE, D_CONV = (2, 16, 4)
        D_IN = EXPAND * D_MODEL
        DT_RANK = D_MODEL // 16
        LN_EPS = 1e-05

        def _mamba(x, W_in, conv_w, conv_b, W_x, W_dt, b_dt, A_log, D):
            Bb, L, _ = x.shape
            xz = x @ W_in
            x_in, z = (xz[..., :D_IN], xz[..., D_IN:])
            xp = jnp.pad(x_in, ((0, 0), (D_CONV - 1, 0), (0, 0)))
            xc = conv_b
            for k in range(D_CONV):
                xc = xc + xp[:, k:k + L, :] * conv_w[:, k]
            xc = jax.nn.silu(xc)
            dbc = xc @ W_x
            dt = dbc[..., :DT_RANK]
            Bm = dbc[..., DT_RANK:DT_RANK + D_STATE]
            Cm = dbc[..., DT_RANK + D_STATE:]
            delta = jax.nn.softplus(dt @ W_dt + b_dt)
            A = -jnp.exp(A_log)
            u_t = jnp.swapaxes(xc, 0, 1)
            d_t = jnp.swapaxes(delta, 0, 1)
            B_t = jnp.swapaxes(Bm, 0, 1)
            C_t = jnp.swapaxes(Cm, 0, 1)

            def step(h, inp):
                u, d, b, c = inp
                dA = jnp.exp(d[..., None] * A)
                h = h * dA + (d * u)[..., None] * b[:, None, :]
                y = jnp.einsum('bds,bs->bd', h, c)
                return (h, y)
            h0 = jnp.zeros((Bb, D_IN, D_STATE), dtype=x.dtype)
            _, ys = jax.lax.scan(step, h0, (u_t, d_t, B_t, C_t))
            y = jnp.swapaxes(ys, 0, 1) + xc * D
            y = y * jax.nn.silu(z)
            return y @ (W_in[:0, :0] if False else None) if False else y
        y = _mamba(x, W_in, conv_w, conv_b, W_x, W_dt, b_dt, A_log, D) @ W_out
        h = x + y
        mu = jnp.mean(h, axis=-1, keepdims=True)
        var = jnp.mean(jnp.square(h - mu), axis=-1, keepdims=True)
        return (h - mu) / jnp.sqrt(var + LN_EPS) * gamma + beta

    def _L3_ffn_ref(hidden_states, gw1, gb1, gw2, gb2, qWm, qU, qS, qV, qb, kWm, kU, kS, kV, kb, vWm, vU, vS, vV, vb, oWm, oU, oS, oV, ob):
        import jax, jax.numpy as jnp
        import numpy as np
        E, TOPK, R = (8, 2, 16)
        D, H, GH = (256, 16, 64)
        HD = D // H
        SCALE = HD ** (-0.5)

        def _svd_moe(x, Wm, U, S, V, b, idx, gates):
            main = jnp.einsum('bsd,od->bso', x, Wm)
            Ug, Sg, Vg = (U[idx], S[idx], V[idx])
            xv = jnp.einsum('bsd,bkrd->bksr', x, Vg)
            xvs = xv * Sg[:, :, None, :]
            eo = jnp.einsum('bksr,bkor->bkso', xvs, Ug)
            expert = jnp.einsum('bkso,bk->bso', eo, gates)
            return main + expert + b
        B, S, _ = hidden_states.shape
        pooled = hidden_states.mean(axis=1)
        h = jax.nn.relu(pooled @ gw1.T + gb1)
        logits = h @ gw2.T + gb2
        top_vals, top_idx = jax.lax.top_k(logits, TOPK)
        gates = jax.nn.softmax(top_vals, axis=-1)
        q = _svd_moe(hidden_states, qWm, qU, qS, qV, qb, top_idx, gates) * SCALE
        k = _svd_moe(hidden_states, kWm, kU, kS, kV, kb, top_idx, gates)
        v = _svd_moe(hidden_states, vWm, vU, vS, vV, vb, top_idx, gates)

        def shp(t):
            return t.reshape(B, S, H, HD).transpose(0, 2, 1, 3)
        q, k, v = (shp(q), shp(k), shp(v))
        attn = jax.nn.softmax(jnp.einsum('bhsd,bhtd->bhst', q, k), axis=-1)
        ctx = jnp.einsum('bhst,bhtd->bhsd', attn, v)
        ctx = ctx.transpose(0, 2, 1, 3).reshape(B, S, D)
        out = _svd_moe(ctx, oWm, oU, oS, oV, ob, top_idx, gates)
        return out
    h = _L0_tok_ref(x, L0_tok_W1, L0_tok_b1, L0_tok_W2, L0_tok_b2, L0_tok_gamma, L0_tok_beta)
    h = h + _L0_attn_ref(_layernorm(h, axis=-1), L0_attn_ln_g, L0_attn_ln_b, L0_attn_w_qkv, L0_attn_b_qkv, L0_attn_w_ent, L0_attn_b_ent, L0_attn_w_out, L0_attn_b_out)
    h = h + _L0_ffn_ref(_layernorm(h, axis=-1), L0_ffn_weight_int8, L0_ffn_weight_scale, L0_ffn_bias)
    h = h + _L1_attn_ref(_layernorm(h, axis=-1), L1_attn_Wqkv, L1_attn_bqkv, L1_attn_Wproj, L1_attn_bproj)
    h = h + _L1_ffn_ref(_layernorm(h, axis=-1), L1_ffn_w_freq_real, L1_ffn_w_freq_imag, L1_ffn_bias)
    h = h + _L2_attn_ref(_layernorm(h, axis=-1), L2_attn_w_attn, L2_attn_w_proj, L2_attn_lambda_q1, L2_attn_lambda_q2, L2_attn_lambda_k1, L2_attn_lambda_k2, L2_attn_gamma)
    h = h + _L2_ffn_ref(_layernorm(h, axis=-1), L2_ffn_Wr, L2_ffn_W1, L2_ffn_W2)
    h = h + _L3_attn_ref(_layernorm(h, axis=-1), L3_attn_W_in, L3_attn_conv_w, L3_attn_conv_b, L3_attn_W_x, L3_attn_W_dt, L3_attn_b_dt, L3_attn_A_log, L3_attn_D, L3_attn_W_out, L3_attn_gamma, L3_attn_beta)
    h = h + _L3_ffn_ref(_layernorm(h, axis=-1), L3_ffn_gw1, L3_ffn_gb1, L3_ffn_gw2, L3_ffn_gb2, L3_ffn_qWm, L3_ffn_qU, L3_ffn_qS, L3_ffn_qV, L3_ffn_qb, L3_ffn_kWm, L3_ffn_kU, L3_ffn_kS, L3_ffn_kV, L3_ffn_kb, L3_ffn_vWm, L3_ffn_vU, L3_ffn_vS, L3_ffn_vV, L3_ffn_vb, L3_ffn_oWm, L3_ffn_oU, L3_ffn_oS, L3_ffn_oV, L3_ffn_ob)
    return h

_drawn_inputs = setup_inputs


def setup_inputs(seed=0):
    import zlib

    import numpy as np

    out = dict(_drawn_inputs(seed))
    spreads = {'L0_attn_ln_g': (1.0, 0.6),
     'L0_attn_ln_b': (0.0, 0.8),
     'L0_attn_b_qkv': (0.0, 0.8),
     'L0_attn_b_out': (0.0, 0.363),
     'L2_attn_gamma': (1.0, 0.2),
     'L3_attn_conv_b': (0.0, 0.8),
     'L3_attn_b_dt': (-4.600166320800781, 0.6),
     'L3_attn_D': (1.0, 0.6),
     'L3_attn_gamma': (1.0, 0.2),
     'L3_attn_beta': (0.0, 0.1),
     'L3_ffn_gb1': (0.0, 0.8),
     'L3_ffn_gb2': (0.0, 0.8),
     'L3_ffn_qb': (0.0, 0.8),
     'L3_ffn_kb': (0.0, 0.8),
     'L3_ffn_vb': (0.0, 0.609),
     'L3_ffn_ob': (0.0, 0.1)}
    factors = {'L0_tok_b1': 3.818,
     'L0_tok_b2': 4.055,
     'L0_attn_w_qkv': 8.0,
     'L0_attn_w_ent': 8.0,
     'L0_attn_w_out': 8.0,
     'L0_ffn_bias': 2.816,
     'L1_attn_bqkv': 4.522,
     'L1_ffn_bias': 3.364,
     'L2_attn_lambda_q1': 8.0,
     'L2_attn_lambda_q2': 8.0,
     'L2_attn_lambda_k1': 8.0,
     'L2_attn_lambda_k2': 4.719,
     'L2_ffn_Wr': 3.64,
     'L2_ffn_W1': 3.198,
     'L2_ffn_W2': 3.131,
     'L3_attn_W_in': 8.0,
     'L3_attn_conv_w': 8.0,
     'L3_attn_W_x': 8.0,
     'L3_attn_W_dt': 8.0,
     'L3_attn_A_log': 8.0,
     'L3_attn_W_out': 8.0,
     'L3_ffn_gw1': 8.0,
     'L3_ffn_gw2': 8.0,
     'L3_ffn_qWm': 8.0,
     'L3_ffn_qU': 8.0,
     'L3_ffn_qS': 8.0,
     'L3_ffn_qV': 8.0,
     'L3_ffn_kWm': 8.0,
     'L3_ffn_kU': 8.0,
     'L3_ffn_kS': 8.0,
     'L3_ffn_kV': 8.0,
     'L3_ffn_vWm': 3.133,
     'L3_ffn_vU': 8.0,
     'L3_ffn_vS': 8.0,
     'L3_ffn_vV': 8.0,
     'L3_ffn_oU': 8.0,
     'L3_ffn_oS': 8.0,
     'L3_ffn_oV': 8.0}
    for name, (base, spread) in spreads.items():
        noise = np.random.default_rng([zlib.crc32(name.encode()), seed]).standard_normal(out[name].shape)
        drawn = base * np.exp(spread * noise) if base else spread * noise
        out[name] = jnp.asarray(drawn.astype(out[name].dtype))
    for name, factor in factors.items():
        out[name] = (out[name] * factor).astype(out[name].dtype)
    return out
```

```python
import math
from contextlib import ExitStack

import numpy as np
import concourse.bass as bass
from concourse import mybir

F32 = mybir.dt.float32
BF16 = mybir.dt.bfloat16
I8 = mybir.dt.int8
ACT = mybir.ActivationFunctionType
ALU = mybir.AluOpType
AX = mybir.AxisListType

P = 128
B = 32
FRAMES, BANDS = 375, 80
STRIDE, WINDOW = 4, 8
T = 93
D = 256
DC = D // P
GU = 4
G = B // GU
GT = GU * T
HEADS, HD = 16, 16
MASKED = -1.0e30
ROUND = 1.5 * 2.0 ** 23


class Chain:

    def __init__(self, eng, sem, base=0):
        self.eng, self.sem, self.base = eng, sem, base

    def link(self, ins):
        self.base = self.base + 1
        ins.then_inc(self.sem, 1)
        self.eng.wait_ge(self.sem, self.base)


class Scope:

    def __init__(self, nc, name):
        self.nc, self.name, self.stack, self.semaphores = nc, name, ExitStack(), []

    def __enter__(self):
        return self

    def __exit__(self, *a):
        self.stack.__exit__(*a)
        if self.semaphores:
            self.nc.clear_and_free_semaphores(self.semaphores)
            self.nc.all_engine_barrier()

    def sb(self, name, shape, dt=F32):
        return self.stack.enter_context(self.nc.sbuf_tensor(f"{self.name}_{name}", shape, dt))

    def ps(self, name, shape, dt=F32):
        return self.stack.enter_context(self.nc.psum_tensor(f"{self.name}_{name}", shape, dt))

    def sem(self, name):
        self.semaphores.append(self.nc.alloc_semaphore(f"{self.name}_{name}"))
        return self.semaphores[-1]



def constants(nc, top, shared):
    shared["ident"] = ident = top.sb("ident", [P, P])
    shared["ident16"] = ident16 = top.sb("ident16", [P, P], BF16)
    shared["minus_half"] = minus_half = top.sb("minus_half", [P, B])
    with Scope(nc, "const") as s:
        filled = s.sem("filled")
        with nc.Block() as block:
            @block.gpsimd
            def _(pool):
                pool.memset(ident[:, :], 0.0).then_inc(filled, 1)
                pool.memset(minus_half[:, :], -0.5).then_inc(filled, 1)
                pool.wait_ge(filled, 2)
                pool.affine_select(out=ident[:, :], in_=ident[:, :], compare_op=ALU.not_equal, fill=1.0, base=0,
                                   pattern=[[-1, P]], channel_multiplier=1).then_inc(filled, 1)

            @block.vector
            def _(dve):
                dve.wait_ge(filled, 3)
                dve.tensor_copy(ident16[:, :], ident[:, :]).then_inc(filled, 1)
                dve.wait_ge(filled, 4)



def tokenizer(nc, shared, dram):
    hidden, ident, minus_half = shared["hidden"], shared["ident"], shared["minus_half"]
    BLOCK = STRIDE * BANDS
    NBLK = T + 1
    rows = [P, P, BLOCK - 2 * P]
    with Scope(nc, "tok") as s:
        frames = s.sb("frames", [P, 3, B, NBLK])
        w1 = s.sb("w1", [P, 2, 3, D])
        w2 = s.sb("w2", [P, DC, D])
        cols = s.sb("cols", [P, 4, DC])
        hid1 = s.sb("hid1", [P, DC, GT])
        hid2 = s.sb("hid2", [P, DC, B * T])
        normal = s.sb("normal", [P, DC, GT])
        stat = s.sb("stat", [P, DC, G, 6])
        agg = s.sb("agg", [P, DC, 2])
        fold = s.sb("fold", [P, 4, DC])
        ps1 = s.ps("ps1", [P, 2, 512])
        ps2 = s.ps("ps2", [P, 2, 512])
        pst = s.ps("pst", [P, 2, 512])
        w_loaded = s.sem("w_loaded")
        cols_loaded = s.sem("cols_loaded")
        frames_loaded = [s.sem(f"frames_loaded{i}") for i in range(4)]
        first_done = s.sem("first_done")
        first_relu = s.sem("first_relu")
        second_done = s.sem("second_done")
        second_relu = s.sem("second_relu")
        step = s.sem("step")
        shifted = s.sem("shifted")
        rooted = s.sem("rooted")
        folded = s.sem("folded")
        normed = s.sem("normed")
        turned = s.sem("turned")
        placed = s.sem("placed")
        with nc.Block() as block:
            @block.sync
            def _(sync):
                for half in range(2):
                    for c in range(3):
                        sync.dma_start(w1[0:rows[c], half, c, :],
                                       dram["tok_W1"][half, c * P:c * P + rows[c], :]).then_inc(w_loaded, 16)
                sync.dma_start(w2[:, :, :], dram["tok_W2"].rearrange("(c p) n -> p c n", p=P)).then_inc(w_loaded, 16)
                for n, name in enumerate(("tok_b1", "tok_b2", "tok_gamma", "tok_beta")):
                    sync.dma_start(cols[:, n, :], dram[name + "_col"]).then_inc(cols_loaded, 16)

            @block.scalar
            def _(act):
                for part in range(4):
                    for c in range(3):
                        act.dma_start(frames[0:rows[c], c, 8 * part:8 * part + 8, :],
                                      dram["frames"][c * P:c * P + rows[c], 8 * part:8 * part + 8, :]
                                      ).then_inc(frames_loaded[part], 16)
                act.wait_ge(cols_loaded, 64)
                with act.Fori(0, G) as g:
                    for c in range(DC):
                        act.wait_ge(first_done, 2 * g + c + 1)
                        act.activation(hid1[:, c, :], ps1[:, c, 0:GT], ACT.Relu,
                                       bias=cols[:, 0, c:c + 1]).then_inc(first_relu, 1)
                    for c in range(DC):
                        act.wait_ge(second_done, 2 * g + c + 1)
                        act.activation(hid2[:, c, bass.ds(g * GT, GT)], ps2[:, c, 0:GT], ACT.Relu,
                                       bias=cols[:, 1, c:c + 1]).then_inc(second_relu, 1)
                act.wait_ge(folded, 1)
                with act.Fori(0, G) as g:
                    act.wait_ge(turned, 4 * g)
                    for c in range(DC):
                        act.activation(normal[:, c, :], hid2[:, c, bass.ds(g * GT, GT)], ACT.Identity,
                                       bias=fold[:, 3, c:c + 1], scale=fold[:, 2, c:c + 1]).then_inc(normed, 1)

            @block.tensor
            def _(pe):
                pe.wait_ge(w_loaded, 7 * 16)
                for part in range(4):
                    pe.wait_ge(frames_loaded[part], 48)
                with pe.Fori(0, G) as g:
                    for m in range(DC):
                        pe.wait_ge(first_relu, 2 * g)
                        for n in range(6):
                            half, c = n // 3, n % 3
                            mm = pe.matmul(ps1[:, m, 0:GT], w1[0:rows[c], half, c, m * P:(m + 1) * P],
                                           frames[0:rows[c], c, bass.ds(g * GU, GU), half:half + T],
                                           start=(n == 0), stop=(n == 5))
                        mm.then_inc(first_done, 1)
                    pe.wait_ge(first_relu, 2 * g + 2)
                    pe.wait_ge(second_relu, 2 * g)
                    for m in range(DC):
                        for c in range(DC):
                            mm = pe.matmul(ps2[:, m, 0:GT], w2[:, c, m * P:(m + 1) * P], hid1[:, c, :],
                                           start=(c == 0), stop=(c == DC - 1))
                        mm.then_inc(second_done, 1)
                with pe.Fori(0, G) as g:
                    pe.wait_ge(normed, 2 * g + 2)
                    for u in range(GU):
                        if u >= 2:
                            pe.wait_ge(placed, 4 * g + u - 1)
                        else:
                            pe.wait_ge(placed, 4 * g)
                        for c in range(DC):
                            mm = pe.transpose(pst[0:T, u % 2, c * P:(c + 1) * P], normal[:, c, u * T:(u + 1) * T],
                                              ident[:, :])
                        mm.then_inc(turned, 1)

            @block.vector
            def _(dve):
                with dve.Fori(0, G) as g:
                    for c in range(DC):
                        dve.wait_ge(second_relu, 2 * g + c + 1)
                        dve.bn_stats(stat[:, c, g, :], hid2[:, c, bass.ds(g * GT, GT)]).then_inc(step, 1)
                dve.wait_ge(step, 2 * G)
                steps = Chain(dve, step, 2 * G)
                for c in range(DC):
                    steps.link(dve.bn_aggr(agg[:, c, :], stat[:, c, :, :]))
                dve.tensor_scalar(fold[:, 0, :], agg[:, :, 1], 1e-5, None, ALU.add).then_inc(shifted, 1)
                dve.wait_ge(rooted, 1)
                dve.wait_ge(cols_loaded, 64)
                steps.link(dve.tensor_tensor(fold[:, 2, :], fold[:, 1, :], cols[:, 2, :], ALU.mult))
                steps.link(dve.tensor_tensor(fold[:, 0, :], agg[:, :, 0], fold[:, 2, :], ALU.mult))
                dve.tensor_tensor(fold[:, 3, :], cols[:, 3, :], fold[:, 0, :], ALU.subtract).then_inc(folded, 1)
                with dve.Fori(0, G) as g:
                    for u in range(GU):
                        dve.wait_ge(turned, 4 * g + u + 1)
                        dve.tensor_copy(hidden[0:T, 4 * g + u, :], pst[0:T, u % 2, 0:D]).then_inc(placed, 1)

            @block.gpsimd
            def _(pool):
                pool.wait_ge(shifted, 1)
                pool.tensor_tensor(fold[:, 1, :], fold[:, 0, :], minus_half[:, 0:DC], ALU.pow).then_inc(rooted, 1)



class Norm:

    def __init__(self, s, prefix=""):
        self.stat = s.sb(prefix + "stat", [P, B, 6])
        self.tmp = s.sb(prefix + "stat_tmp", [P, 4, B])
        self.mean = s.sb(prefix + "mean", [P, B])
        self.rstd = s.sb(prefix + "rstd", [P, B])
        self.xn = s.sb(prefix + "xn", [P, GU, D])
        self.xT = s.sb(prefix + "xT", [P, DC, GT])
        self.measured = s.sem(prefix + "measured")
        self.step = s.sem(prefix + "norm_step")
        self.spread = s.sem(prefix + "spread")
        self.rooted = s.sem(prefix + "rooted")
        self.normed = s.sem(prefix + "normed")
        self.turned = s.sem(prefix + "turned")
        self.xT_ready = s.sem(prefix + "xT_ready")


def norm_statistics_dve(dve, n, source, eps):
    with dve.Fori(0, B) as b:
        dve.bn_stats(n.stat[0:T, b, :], source[0:T, b, :]).then_inc(n.measured, 1)
    dve.wait_ge(n.measured, B)
    mean_e, m2_e, mean_o, m2_o = (n.stat[0:T, :, k] for k in (1, 2, 4, 5))
    t = [n.tmp[0:T, k, :] for k in range(4)]
    steps = Chain(dve, n.step)
    dve.tensor_tensor(t[0], mean_e, mean_o, ALU.add).then_inc(n.step, 1)
    dve.tensor_tensor(t[1], mean_e, mean_o, ALU.subtract).then_inc(n.step, 1)
    dve.tensor_tensor(t[2], m2_e, m2_o, ALU.add).then_inc(n.step, 1)
    steps.base = 3
    dve.wait_ge(n.step, 3)
    dve.tensor_scalar(n.mean[0:T, :], t[0], 0.5, None, ALU.mult).then_inc(n.step, 1)
    dve.tensor_tensor(t[3], t[1], t[1], ALU.mult).then_inc(n.step, 1)
    dve.tensor_scalar(t[2], t[2], 1.0 / D, eps, ALU.mult, ALU.add).then_inc(n.step, 1)
    dve.wait_ge(n.step, 6)
    dve.scalar_tensor_tensor(t[0], t[3], 0.25, t[2], ALU.mult, ALU.add).then_inc(n.spread, 1)
    dve.wait_ge(n.rooted, 1)


def norm_root_pool(pool, n, minus_half):
    pool.wait_ge(n.spread, 1)
    pool.tensor_tensor(n.rstd[0:T, :], n.tmp[0:T, 0, :], minus_half[0:T, :], ALU.pow).then_inc(n.rooted, 1)


def norm_group_dve(dve, n, g, source):
    dve.wait_ge(n.turned, GU * g)
    for u in range(GU):
        b = GU * g + u
        dve.tensor_scalar(n.xn[0:T, u, :], source[0:T, b, :], n.mean[0:T, bass.ds(b, 1)], n.rstd[0:T, bass.ds(b, 1)],
                          ALU.subtract, ALU.mult).then_inc(n.normed, 1)


def norm_group_pe(pe, n, g, banks, ident):
    for u in range(GU):
        pe.wait_ge(n.normed, GU * g + u + 1)
        for c in range(DC):
            mm = pe.transpose(banks[:, c, u * T:(u + 1) * T], n.xn[0:T, u, c * P:(c + 1) * P], ident[0:T, 0:T])
        mm.then_inc(n.turned, 1)


def norm_group_act(act, n, g, banks, scale=None, shift=None):
    act.wait_ge(n.turned, GU * g + GU)
    for c in range(DC):
        act.activation(n.xT[:, c, :], banks[:, c, 0:GT], ACT.Identity,
                       bias=0.0 if shift is None else shift[:, c:c + 1],
                       scale=1.0 if scale is None else scale[:, c:c + 1]).then_inc(n.xT_ready, 1)



class Attention:

    def __init__(self, s, maps, causal, exp_scale):
        self.maps, self.causal, self.exp_scale = maps, causal, exp_scale
        self.width = D // maps
        self.variants = 32 // self.width
        self.units = maps // 4
        self.banks_o = maps // HEADS
        self.q = s.sb("q", [P, DC, self.variants, GT])
        self.k = s.sb("k", [P, DC, GT])
        self.v = s.sb("v", [P, GU, HEADS, HD + 1])
        self.only = s.sb("only", [P, self.variants])
        self.sel = s.sb("sel", [P, maps, T], BF16)
        self.negmax = s.sb("negmax", [P, maps])
        self.split_width = 2 * maps if maps == HEADS else 2 * maps + 2
        self.split = s.sb("split", [P, self.split_width], BF16)
        self.maxT = s.sb("maxT", [P, T], BF16)
        self.probs = s.sb("probs", [P, 4, GT])
        self.rden = s.sb("rden", [P, self.banks_o, HEADS])
        self.ctx = s.sb("ctx", [P, 2, D])
        self.ctxT = s.sb("ctxT", [P, DC, T])
        if causal:
            self.mask_q = s.sb("mask_q", [P, 4, T], BF16)
            self.mask_k = s.sb("mask_k", [P, 4, T], BF16)
        self.ps_s = s.ps("scores", [P, 2, 512])
        self.ps_t = s.ps("scoresT", [P, 2, 512])
        self.ps_o = s.ps("outputs", [P, 2, 512])
        self.ps_g = s.ps("general", [P, 2, 512])
        self.const_ready = s.sem("att_const")
        self.q_done = s.sem("q_done")
        self.k_done = s.sem("k_done")
        self.v_done = s.sem("v_done")
        self.q_ready = s.sem("q_ready")
        self.k_ready = s.sem("k_ready")
        self.v_ready = s.sem("v_ready")
        self.v_gated = None
        self.ranks_ready = None
        self.scored = s.sem("scored")
        self.maxed = s.sem("maxed")
        self.split_ready = s.sem("split_ready")
        self.max_turned = s.sem("max_turned")
        self.maxT_ready = s.sem("maxT_ready")
        self.scoredT = s.sem("scoredT")
        self.probs_ready = s.sem("probs_ready")
        self.weighed = s.sem("weighed")
        self.ctx_ready = s.sem("ctx_ready")
        self.ctx_turned = s.sem("ctx_turned")
        self.ctxT_ready = s.sem("ctxT_ready")
        self.out_done = s.sem("out_done")
        self.added = s.sem("added")
        self.step = s.sem("att_step")

    def unit(self, g, u, w):
        return (GU * g + u) * self.units + w

    def place(self, w, j):
        if self.variants == 4:
            c, r, v = w // 4, w % 4, j
        else:
            c, r, v = j // 2, w, j % 2
        return c, 32 * r, v, (4 * c + r) * self.variants + v


def attention_constants_pool(pool, a):
    pool.memset(a.sel[:, :, :], 0.0).then_inc(a.const_ready, 1)
    pool.memset(a.v[:, :, :, HD:HD + 1], 1.0).then_inc(a.const_ready, 1)
    pool.memset(a.maxT[:, :], 0.0).then_inc(a.const_ready, 1)
    pool.memset(a.split[:, :], 0.0).then_inc(a.const_ready, 1)
    pool.wait_ge(a.const_ready, 4)
    for part in range(2):
        pool.affine_select(out=a.sel[:, :, :], in_=a.sel[:, :, :], compare_op=ALU.not_equal, fill=1.0,
                           base=-part * a.maps, pattern=[[-1, a.maps], [0, T]],
                           channel_multiplier=1).then_inc(a.const_ready, 1)
        pool.wait_ge(a.const_ready, 5 + part)
    if a.causal:
        for m in (a.mask_q, a.mask_k):
            pool.memset(m[:, :, :], 0.0).then_inc(a.const_ready, 1)
        pool.wait_ge(a.const_ready, 8)
        for m, sign in ((a.mask_q, -1), (a.mask_k, 1)):
            pool.affine_select(out=m[:, :, :], in_=m[:, :, :], compare_op=ALU.is_ge, fill=MASKED, base=0,
                               pattern=[[0, 4], [sign, T]], channel_multiplier=-sign).then_inc(a.const_ready, 1)


def attention_constants_dve(dve, a, ident):
    rows = ident[:, :].rearrange("p (q v e) -> p v q e", q=4, v=a.variants)
    dve.tensor_reduce(a.only[:, :], rows, AX.XY, ALU.add).then_inc(a.step, 1)
    dve.sem_inc(a.maxed, 2)
    dve.sem_inc(a.probs_ready, 2)
    dve.sem_inc(a.weighed, 4)
    dve.sem_inc(a.ctx_ready, 3 - a.banks_o)


def attention_constants_ready(a):
    return 10 if a.causal else 6


def attention_pe(pe, a, g, ident, ident16, w_out, before_out=None, extra_out=None):

    def scores(u, w):
        n = a.unit(g, u, w)
        if u == 0 and w == 0:
            pe.wait_ge(a.q_ready, 2 * g + 2)
            pe.wait_ge(a.k_ready, 2 * g + 2)
        pe.wait_ge(a.maxed, n + 1)
        bank = a.ps_s[0:T, w % 2, :]
        if a.causal:
            pe.matmul(bank[:, 0:GT], ident16[0:T, 0:T], a.mask_q[0:T, :, :], start=True, stop=False,
                      skip_group_check=True)
        for j in range(4):
            c, r, v, _ = a.place(w, j)
            mm = pe.matmul(bank[:, j * T:(j + 1) * T], a.q[r:r + 32, c, v, u * T:(u + 1) * T],
                           a.k[r:r + 32, c, u * T:(u + 1) * T], start=not a.causal, stop=True,
                           skip_group_check=True)
        mm.then_inc(a.scored, 1)

    def turn_max(u):
        pe.wait_ge(a.split_ready, GU * g + u + 1)
        if u:
            pe.wait_ge(a.added, GU * g + u - 1)
        pe.transpose(a.ps_g[0:a.split_width, 0, :].bitcast(BF16)[:, 0:T], a.split[0:T, :],
                     ident16[0:T, 0:T]).then_inc(a.max_turned, 1)

    def scores_t(u, w):
        n = a.unit(g, u, w)
        if w == 0:
            pe.wait_ge(a.maxT_ready, GU * g + u + 1)
        pe.wait_ge(a.probs_ready, n + 1)
        bank = a.ps_t[0:T, w % 2, :]
        if a.causal:
            pe.matmul(bank[:, 0:GT], ident16[0:T, 0:T], a.mask_k[0:T, :, :], start=True, stop=False,
                      skip_group_check=True)
        for j in range(4):
            c, r, v, _ = a.place(w, j)
            pe.matmul(bank[:, j * T:(j + 1) * T], a.sel[:, 4 * w + j, :], a.maxT[:, :],
                      start=(j == 0 and not a.causal), stop=False, skip_group_check=True)
            mm = pe.matmul(bank[:, j * T:(j + 1) * T], a.k[r:r + 32, c, u * T:(u + 1) * T],
                           a.q[r:r + 32, c, v, u * T:(u + 1) * T], start=False, stop=True, skip_group_check=True)
        mm.then_inc(a.scoredT, 1)

    def weigh(u, w):
        n = a.unit(g, u, w)
        if w == 0:
            pe.wait_ge(a.v_ready if a.v_gated is None else a.v_gated, GU * g + GU)
            pe.wait_ge(a.ctx_ready, GU * g + u + 1)
        pe.wait_ge(a.probs_ready, n + 3)
        for j in range(4):
            m = a.place(w, j)[3]
            if a.banks_o == 1:
                h, bank = m, u % 2
            else:
                h, bank = m // 2, m % 2
            mm = pe.matmul(a.ps_o[0:T, bank, h * (HD + 1):(h + 1) * (HD + 1)], a.probs[0:T, w % 4, j * T:(j + 1) * T],
                           a.v[0:T, u, h, :], start=True, stop=True, skip_group_check=True)
        mm.then_inc(a.weighed, 1)

    def turn_ctx(u):
        pe.wait_ge(a.ctx_ready, 3 - a.banks_o + GU * g + u + 1)
        pe.wait_ge(a.ctxT_ready, GU * g + u)
        if a.ranks_ready is not None:
            pe.wait_ge(a.ranks_ready, GU * g + u)
        for c in range(DC):
            mm = pe.transpose(a.ps_g[:, 1, c * T:(c + 1) * T], a.ctx[0:T, u % 2, c * P:(c + 1) * P], ident[0:T, 0:T])
        mm.then_inc(a.ctx_turned, 1)

    def project(u):
        pe.wait_ge(a.ctxT_ready, GU * g + u + 1)
        pe.wait_ge(a.added, GU * g + u)
        if u < GU - 1:
            pe.wait_ge(a.maxT_ready, GU * g + u + 2)
        if before_out is not None:
            before_out(u)
        for c in range(DC):
            mm = pe.matmul(a.ps_g[0:T, 0, 0:D], a.ctxT[:, c, :], w_out[:, c, :], start=(c == 0),
                           stop=(c == DC - 1 and extra_out is None))
        if extra_out is not None:
            mm = extra_out(u)
        mm.then_inc(a.out_done, 1)

    for w in range(a.units):
        scores(0, w)
    for u in range(GU):
        turn_max(u)
        for w in range(a.units):
            scores_t(u, w)
            if u + 1 < GU:
                scores(u + 1, w)
            if w:
                weigh(u, w - 1)
            if u and w == 1:
                turn_ctx(u - 1)
            if u and w == a.units - 1:
                project(u - 1)
        weigh(u, a.units - 1)
    turn_ctx(GU - 1)
    project(GU - 1)


def attention_act(act, a, g, ctx_scale=None, extra=None):

    def exp(u, w):
        n = a.unit(g, u, w)
        act.wait_ge(a.scoredT, n + 1)
        act.wait_ge(a.weighed, n + 1)
        act.activation(a.probs[0:T, w % 4, :], a.ps_t[0:T, w % 2, 0:GT], ACT.Exp,
                       scale=a.exp_scale).then_inc(a.probs_ready, 1)

    def ctx_t(u):
        act.wait_ge(a.ctx_turned, GU * g + u + 1)
        act.wait_ge(a.out_done, GU * g + u)
        if ctx_scale is None:
            act.activation(a.ctxT[:, :, :], a.ps_g[:, 1, 0:DC * T], ACT.Copy).then_inc(a.ctxT_ready, 1)
        else:
            act.activation(a.ctxT[:, :, :], a.ps_g[:, 1, 0:DC * T], ACT.Copy,
                           scale=ctx_scale).then_inc(a.ctxT_ready, 1)

    for u in range(GU):
        for w in range(a.units):
            exp(u, w)
            if u and w == 1:
                ctx_t(u - 1)
        if u and extra is not None:
            extra(u - 1)
    ctx_t(GU - 1)
    if extra is not None:
        extra(GU - 1)


def attention_dve(dve, a, g, steps, context, add):

    def maxima(u):
        for w in range(a.units):
            dve.wait_ge(a.scored, a.unit(g, u, w) + 1)
            dve.tensor_reduce(a.negmax[0:T, 4 * w:4 * w + 4],
                              a.ps_s[0:T, w % 2, 0:GT].rearrange("p (j t) -> p j t", j=4), AX.X, ALU.max,
                              negate=True).then_inc(a.maxed, 1)
        dve.wait_ge(a.maxed, 2 + a.unit(g, u, a.units))
        dve.wait_ge(a.max_turned, GU * g + u)
        steps.link(dve.tensor_copy(a.split[0:T, 0:a.maps], a.negmax[0:T, :]))
        dve.tensor_tensor(a.split[0:T, a.maps:2 * a.maps], a.negmax[0:T, :], a.split[0:T, 0:a.maps],
                          ALU.subtract).then_inc(a.split_ready, 1)
        dve.wait_ge(a.split_ready, GU * g + u + 1)

    def max_t(u):
        dve.wait_ge(a.max_turned, GU * g + u + 1)
        dve.wait_ge(a.scoredT, a.unit(g, u, 0))
        dve.tensor_copy(a.maxT[0:2 * a.maps, :], a.ps_g[0:2 * a.maps, 0, :].bitcast(BF16)[:, 0:T]).then_inc(a.maxT_ready, 1)

    maxima(0)
    max_t(0)
    for u in range(GU):
        if u + 1 < GU:
            maxima(u + 1)
        if u:
            add(u - 1)
        if u + 1 < GU:
            max_t(u + 1)
        dve.wait_ge(a.weighed, 4 + a.unit(g, u, a.units))
        context(u)
    add(GU - 1)


class GroupSteps:

    def __init__(self, eng, sem, base, per):
        self.eng, self.sem, self.base, self.per = eng, sem, base, per

    def begin(self, g):
        self.g, self.n = g, 0
        return self

    def link(self, ins):
        self.n += 1
        ins.then_inc(self.sem, 1)
        self.eng.wait_ge(self.sem, self.g * self.per + (self.base + self.n))

    def end(self):
        assert self.n == self.per, (self.n, self.per)


def load_rows(eng, tile, vector, sem, rows=T):
    eng.dma_start(tile, vector.partition_broadcast(rows)).then_inc(sem, 16)


def project_group_pe(pe, a, n, g, w_qkv, v_cols, extra_q=None):
    pe.wait_ge(n.xT_ready, 2 * g + 2)
    for what, (done, free) in enumerate(((a.q_done, n.xT_ready), (a.k_done, a.q_ready))):
        for m in range(DC):
            pe.wait_ge(free, 2 * g + m + 1)
            for c in range(DC):
                mm = pe.matmul(a.ps_g[:, m, 0:GT], w_qkv[:, c, what * D + m * P:what * D + (m + 1) * P],
                               n.xT[:, c, :], start=(c == 0), stop=(c == DC - 1))
            mm.then_inc(done, 1)
    for u in range(GU):
        if u < 2:
            pe.wait_ge(a.k_ready, 2 * g + u + 1)
        else:
            pe.wait_ge(a.v_ready, GU * g + u - 1)
        for c in range(DC):
            mm = pe.matmul(a.ps_g[0:T, u % 2, 0:v_cols], n.xT[:, c, u * T:(u + 1) * T],
                           w_qkv[:, c, 2 * D:2 * D + v_cols], start=(c == 0), stop=(c == DC - 1))
        mm.then_inc(a.v_done, 1)


def queries_keys_act(act, a, g, q_bias, k_bias):
    act.wait_ge(a.scoredT, a.unit(g, 0, 0))
    for m in range(DC):
        act.wait_ge(a.q_done, 2 * g + m + 1)
        for v in range(a.variants):
            ins = act.activation(a.q[:, m, v, :], a.ps_g[:, m, 0:GT], ACT.Identity,
                                 bias=0.0 if q_bias is None else q_bias[:, v, m:m + 1], scale=a.only[:, v:v + 1])
        ins.then_inc(a.q_ready, 1)
    for m in range(DC):
        act.wait_ge(a.k_done, 2 * g + m + 1)
        act.activation(a.k[:, m, :], a.ps_g[:, m, 0:GT], ACT.Identity,
                       bias=0.0 if k_bias is None else k_bias[:, m:m + 1]).then_inc(a.k_ready, 1)



def gated_attention(nc, shared, dram):
    hidden, ident, ident16, minus_half = (shared[k] for k in ("hidden", "ident", "ident16", "minus_half"))
    TEMPERATURE, OUT_SCALE = 0.1, 0.1
    with Scope(nc, "gattn") as s:
        outer = Norm(s, "outer_")
        n = Norm(s)
        a = Attention(s, HEADS, True, 1.0 / (math.sqrt(HD) * TEMPERATURE))
        x1 = s.sb("x1", [P, B, D])
        w_qkv = s.sb("w_qkv", [P, DC, 3 * D + 1])
        w_out = s.sb("w_out", [P, DC, D])
        ln = s.sb("ln", [P, 2, DC])
        qk_bias = s.sb("qk_bias", [P, 2, DC])
        q_bias = s.sb("q_bias", [P, a.variants, DC])
        v_bias = s.sb("v_bias", [P, D])
        o_bias = s.sb("o_bias", [P, D])
        b_ent = s.sb("b_ent", [P, 1])
        gate = s.sb("gate", [P, 3, GU])
        summed = s.sb("summed", [P, D])
        w_loaded, x1_ready, bias_ready, gate_in, gate_exp = (
            s.sem(k) for k in ("w_loaded", "x1_ready", "bias_ready", "gate_in", "gate_exp"))
        a.v_gated = s.sem("v_gated")
        LOADS = 9
        with nc.Block() as block:
            @block.sync
            def _(sync):
                sync.dma_start(w_qkv[:, :, 0:3 * D], dram["L0_attn_w_qkv"].rearrange("(c p) n -> p c n", p=P)
                               ).then_inc(w_loaded, 16)
                for c in range(DC):
                    sync.dma_start(w_qkv[:, c, 3 * D:], dram["L0_attn_w_ent"][c * P:(c + 1) * P, :]).then_inc(w_loaded, 16)
                sync.dma_start(w_out[:, :, :], dram["L0_attn_w_out"].rearrange("(c p) n -> p c n", p=P)
                               ).then_inc(w_loaded, 16)
                sync.dma_start(ln[:, 0, :], dram["L0_attn_ln_g_col"]).then_inc(w_loaded, 16)
                sync.dma_start(ln[:, 1, :], dram["L0_attn_ln_b_col"]).then_inc(w_loaded, 16)
                sync.dma_start(qk_bias[:, :, :], dram["L0_attn_b_qkv_col"][:, 0:4].rearrange("p (a c) -> p a c", a=2)
                               ).then_inc(w_loaded, 16)
                load_rows(sync, v_bias[0:T, :], dram["L0_attn_b_qkv"][2 * D:3 * D], w_loaded)
                load_rows(sync, o_bias[0:T, :], dram["L0_attn_b_out"], w_loaded)
                load_rows(sync, b_ent[0:T, :], dram["L0_attn_b_ent"], w_loaded)

            @block.gpsimd
            def _(pool):
                attention_constants_pool(pool, a)
                norm_root_pool(pool, outer, minus_half)
                norm_root_pool(pool, n, minus_half)

            @block.scalar
            def _(act):
                act.wait_ge(w_loaded, 16 * (LOADS + 1))
                act.wait_ge(bias_ready, a.variants)
                with act.Fori(0, G) as g:
                    act.wait_ge(a.v_done, GU * g)
                    norm_group_act(act, n, g, a.ps_g, scale=ln[:, 0, :], shift=ln[:, 1, :])
                    queries_keys_act(act, a, g, q_bias, qk_bias[:, 1, :])
                    act.wait_ge(gate_in, g + 1)
                    act.activation(gate[0:T, 1, :], gate[0:T, 0, :], ACT.Exp, scale=-1.0).then_inc(gate_exp, 1)
                    attention_act(act, a, g)

            @block.tensor
            def _(pe):
                pe.wait_ge(w_loaded, 16 * (LOADS + 1))
                pe.wait_ge(a.const_ready, attention_constants_ready(a))
                with pe.Fori(0, G) as g:
                    pe.wait_ge(a.added, GU * g)
                    pe.wait_ge(a.ctxT_ready, GU * g)
                    norm_group_pe(pe, n, g, a.ps_g, ident)
                    project_group_pe(pe, a, n, g, w_qkv, D + 1)
                    attention_pe(pe, a, g, ident, ident16, w_out)

            @block.vector
            def _(dve):
                attention_constants_dve(dve, a, ident)
                norm_statistics_dve(dve, outer, hidden, 1e-5)
                with dve.Fori(0, B) as b:
                    dve.tensor_scalar(x1[0:T, b, :], hidden[0:T, b, :], outer.mean[0:T, bass.ds(b, 1)],
                                      outer.rstd[0:T, bass.ds(b, 1)], ALU.subtract, ALU.mult).then_inc(x1_ready, 1)
                dve.wait_ge(x1_ready, B)
                norm_statistics_dve(dve, n, x1, 1e-6)
                dve.wait_ge(w_loaded, 16 * (LOADS + 1))
                dve.wait_ge(a.const_ready, 4)
                dve.wait_ge(a.step, 1)
                for v in range(a.variants):
                    dve.tensor_scalar(q_bias[:, v, :], qk_bias[:, 0, :], a.only[:, v:v + 1], None,
                                      ALU.mult).then_inc(bias_ready, 1)
                steps = GroupSteps(dve, a.step, 1, 19)
                with dve.Fori(0, G) as g:
                    steps.begin(g)
                    norm_group_dve(dve, n, g, x1)
                    dve.wait_ge(a.weighed, 4 + a.unit(g, 0, 0))
                    for u in range(GU):
                        dve.wait_ge(a.v_done, GU * g + u + 1)
                        steps.link(dve.tensor_tensor(gate[0:T, 0, u:u + 1], a.ps_g[0:T, u % 2, D:D + 1], b_ent[0:T, :],
                                                     ALU.add))
                        dve.tensor_tensor(a.v[0:T, u, :, 0:HD],
                                          a.ps_g[0:T, u % 2, 0:D].rearrange("p (h e) -> p h e", h=HEADS),
                                          v_bias[0:T, :].rearrange("p (h e) -> p h e", h=HEADS),
                                          ALU.add).then_inc(a.v_ready, 1)
                    dve.sem_inc(gate_in, 1)
                    dve.wait_ge(gate_exp, g + 1)
                    steps.link(dve.tensor_scalar(gate[0:T, 1, :], gate[0:T, 1, :], 1.0, None, ALU.add))
                    steps.link(dve.reciprocal(gate[0:T, 2, :], gate[0:T, 1, :]))
                    steps.link(dve.tensor_scalar(gate[0:T, 2, :], gate[0:T, 2, :], 0.1, 2.0, ALU.max, ALU.min))
                    for u in range(GU):
                        dve.tensor_scalar(a.v[0:T, u, :, 0:HD], a.v[0:T, u, :, 0:HD], gate[0:T, 2, u:u + 1], None,
                                          ALU.mult).then_inc(a.v_gated, 1)

                    def context(u):
                        outputs = a.ps_o[0:T, u % 2, 0:HEADS * (HD + 1)].rearrange("p (h e) -> p h e", h=HEADS)
                        steps.link(dve.reciprocal(a.rden[0:T, 0, :], outputs[:, :, HD]))
                        dve.tensor_tensor(a.ctx[0:T, u % 2, :].rearrange("p (h e) -> p h e", h=HEADS),
                                          outputs[:, :, 0:HD], a.rden[0:T, 0, :].unsqueeze(2).broadcast_to([T, HEADS, HD]),
                                          ALU.mult).then_inc(a.ctx_ready, 1)

                    def add(u):
                        dve.wait_ge(a.out_done, GU * g + u + 1)
                        steps.link(dve.tensor_tensor(summed[0:T, :], a.ps_g[0:T, 0, 0:D], o_bias[0:T, :], ALU.add))
                        dve.scalar_tensor_tensor(hidden[0:T, GU * g + u, :], summed[0:T, :], OUT_SCALE,
                                                 hidden[0:T, GU * g + u, :], ALU.mult, ALU.add).then_inc(a.added, 1)

                    attention_dve(dve, a, g, steps, context, add)
                    steps.end()



def quantised_linear(nc, shared, dram):
    hidden, ident, ident16, minus_half = (shared[k] for k in ("hidden", "ident", "ident16", "minus_half"))
    TE = T + 1
    with Scope(nc, "quant") as s:
        n = Norm(s)
        x1 = s.sb("x1", [P, B, D])
        w_int = s.sb("w_int", [P, DC, D // 4], mybir.dt.int32)
        w = s.sb("w", [P, DC, D], BF16)
        w_scale = s.sb("w_scale", [P, D])
        bias = s.sb("bias", [P, D])
        largest = s.sb("largest", [P, B])
        most = s.sb("most", [P, 2])
        x_scale = s.sb("x_scale", [P, 2])
        xs = s.sb("xs", [P, 2, D])
        xq = s.sb("xq", [P, 2, D], BF16)
        xqT = s.sb("xqT", [P, 2, DC * TE], BF16)
        scaled = s.sb("scaled", [P, 2, D])
        ps_t = s.ps("turned", [P, 2, 512])
        ps_y = s.ps("product", [P, 2, 512])
        w_loaded, w_ready, x1_ready, found, most_ready, step, rounded, xq_turned, xqT_ready, multiplied, added = (
            s.sem(k) for k in ("w_loaded", "w_ready", "x1_ready", "found", "most_ready", "step", "rounded", "xq_turned",
                               "xqT_ready", "multiplied", "added"))
        with nc.Block() as block:
            @block.sync
            def _(sync):
                sync.dma_start(w_int[:, :, :], dram["L0_ffn_weight_int8"].rearrange("(c p) n -> p c n", p=P)
                               ).then_inc(w_loaded, 16)
                load_rows(sync, w_scale[0:T, :], dram["L0_ffn_weight_scale"].rearrange("n a -> (n a)"), w_loaded)
                load_rows(sync, bias[0:T, :], dram["L0_ffn_bias"], w_loaded)

            @block.gpsimd
            def _(pool):
                pool.memset(most[:, :], 0.0).then_inc(most_ready, 1)
                norm_root_pool(pool, n, minus_half)
                pool.wait_ge(found, 1)
                pool.partition_all_reduce(most[:, 1:2], most[:, 0:1], P, bass.bass_isa.ReduceOp.max).then_inc(most_ready, 1)

            @block.scalar
            def _(act):
                with act.Fori(0, B // 2) as i:
                    for j in range(2):
                        act.wait_ge(xq_turned, 2 * i + j + 1)
                        act.wait_ge(multiplied, 2 * i)
                        act.activation(xqT[:, j, :], ps_t[:, j, :].bitcast(BF16)[:, 0:DC * TE],
                                       ACT.Copy).then_inc(xqT_ready, 1)

            @block.tensor
            def _(pe):
                pe.wait_ge(w_ready, 1)
                with pe.Fori(0, B // 2) as i:
                    for j in range(2):
                        pe.wait_ge(rounded, 2 * i + j + 1)
                        pe.wait_ge(xqT_ready, 2 * i)
                        for c in range(DC):
                            mm = pe.transpose(ps_t[:, j, :].bitcast(BF16)[:, c * TE:c * TE + T],
                                              xq[0:T, j, c * P:(c + 1) * P], ident16[0:T, 0:T])
                        mm.then_inc(xq_turned, 1)
                    for j in range(2):
                        pe.wait_ge(xqT_ready, 2 * i + j + 1)
                        pe.wait_ge(added, 2 * i)
                        for c in range(DC):
                            mm = pe.matmul(ps_y[0:T, j, 0:D], xqT[:, j, c * TE:c * TE + T], w[:, c, :],
                                           start=(c == 0), stop=(c == DC - 1))
                        mm.then_inc(multiplied, 1)

            @block.vector
            def _(dve):
                norm_statistics_dve(dve, n, hidden, 1e-5)
                with dve.Fori(0, B) as b:
                    dve.tensor_scalar(x1[0:T, b, :], hidden[0:T, b, :], n.mean[0:T, bass.ds(b, 1)],
                                      n.rstd[0:T, bass.ds(b, 1)], ALU.subtract, ALU.mult).then_inc(x1_ready, 1)
                    dve.wait_ge(x1_ready, b + 1)
                    dve.tensor_reduce(largest[0:T, bass.ds(b, 1)], x1[0:T, b, :], AX.X, ALU.max,
                                      apply_absolute_value=True).then_inc(step, 1)
                dve.wait_ge(w_loaded, 48)
                for c in range(DC):
                    ins = dve.tensor_copy(w[:, c, :], w_int[:, c, :].bitcast(I8))
                ins.then_inc(w_ready, 1)
                dve.wait_ge(step, B)
                dve.wait_ge(most_ready, 1)
                dve.tensor_reduce(most[0:T, 0:1], largest[0:T, :], AX.X, ALU.max).then_inc(found, 1)
                dve.wait_ge(most_ready, 2)
                steps = Chain(dve, step, B)
                steps.link(dve.tensor_scalar(x_scale[:, 0:1], most[:, 1:2], 1.0 / 127.0, 1e-5, ALU.mult, ALU.max))
                steps.link(dve.reciprocal(x_scale[:, 1:2], x_scale[:, 0:1]))
                steps = GroupSteps(dve, step, B + 2, 8)
                with dve.Fori(0, B // 2) as i:
                    steps.begin(i)
                    dve.wait_ge(xq_turned, 2 * i)
                    for j in range(2):
                        x = xs[0:T, j, :]
                        steps.link(dve.tensor_scalar(x, x1[0:T, 2 * i + j, :], x_scale[0:T, 1:2], -128.0, ALU.mult, ALU.max))
                        steps.link(dve.tensor_scalar(x, x, 127.0, ROUND, ALU.min, ALU.add))
                        dve.tensor_scalar(xq[0:T, j, :], x, ROUND, None, ALU.subtract).then_inc(rounded, 1)
                    for j in range(2):
                        y = scaled[0:T, j, :]
                        dve.wait_ge(multiplied, 2 * i + j + 1)
                        steps.link(dve.scalar_tensor_tensor(y, ps_y[0:T, j, 0:D], x_scale[0:T, 0:1], w_scale[0:T, :],
                                                            ALU.mult, ALU.mult))
                        steps.link(dve.tensor_tensor(y, y, bias[0:T, :], ALU.add))
                        dve.tensor_tensor(hidden[0:T, 2 * i + j, :], hidden[0:T, 2 * i + j, :], y,
                                          ALU.add).then_inc(added, 1)
                    steps.end()



def frequency_linear(nc, shared, dram):
    hidden, ident, minus_half = (shared[k] for k in ("hidden", "ident", "minus_half"))
    with Scope(nc, "freq") as s:
        n = Norm(s)
        dft = s.sb("dft", [P, 2, DC, D])
        minus_sin = s.sb("minus_sin", [P, DC, D])
        back = s.sb("back", [P, 2, DC, D])
        w_freq = s.sb("w_freq", [P, 2, DC, D])
        folded = s.sb("folded", [P, 2, DC, D])
        m = s.sb("m", [P, DC, D])
        bias = s.sb("bias", [P, D])
        summed = s.sb("summed", [P, 2, D])
        ps_t = s.ps("turned", [P, 2, 512])
        ps_y = s.ps("product", [P, 2, 512])
        w_loaded, prepared, fold_done, fold_ready, y_done, step, added = (
            s.sem(k) for k in ("w_loaded", "prepared", "fold_done", "fold_ready", "y_done", "step", "added"))
        with nc.Block() as block:
            @block.sync
            def _(sync):
                for k in range(2):
                    sync.dma_start(dft[:, k, :, :], dram["dft"][k].rearrange("(c p) n -> p c n", p=P)).then_inc(w_loaded, 16)
                for k, name in enumerate(("L1_ffn_w_freq_real", "L1_ffn_w_freq_imag")):
                    sync.dma_start(w_freq[:, k, :, :], dram[name].rearrange("(c p) n -> p c n", p=P)).then_inc(w_loaded, 16)
                load_rows(sync, bias[0:T, :], dram["L1_ffn_bias"], w_loaded)

            @block.gpsimd
            def _(pool):
                norm_root_pool(pool, n, minus_half)

            @block.scalar
            def _(act):
                act.wait_ge(w_loaded, 80)
                act.activation(minus_sin[:, :, :], dft[:, 1, :, :], ACT.Copy, scale=-1.0).then_inc(prepared, 1)
                act.activation(back[:, 0, :, :], dft[:, 0, :, :], ACT.Copy, scale=1.0 / D).then_inc(prepared, 1)
                act.activation(back[:, 1, :, :], dft[:, 1, :, :], ACT.Copy, scale=-1.0 / D).then_inc(prepared, 1)
                for k in range(4):
                    act.wait_ge(fold_done, k + 1)
                    act.activation(folded[:, k // 2, k % 2, :], ps_y[:, k % 2, 0:D], ACT.Copy).then_inc(fold_ready, 1)
                for k in range(2):
                    act.wait_ge(fold_done, 5 + k)
                    act.activation(m[:, k, :], ps_y[:, k, 0:D], ACT.Copy).then_inc(fold_ready, 1)
                with act.Fori(0, G) as g:
                    act.wait_ge(y_done, GU * g)
                    norm_group_act(act, n, g, ps_t)

            @block.tensor
            def _(pe):
                pe.wait_ge(w_loaded, 80)
                pe.wait_ge(prepared, 3)
                for k, terms in enumerate((((0, dft[:, 0]), (1, dft[:, 1])), ((1, dft[:, 0]), (0, minus_sin)))):
                    for row in range(DC):
                        if k:
                            pe.wait_ge(fold_ready, row + 1)
                        for t, (part, right) in enumerate(terms):
                            for c in range(DC):
                                mm = pe.matmul(ps_y[:, row, 0:D], w_freq[:, part, c, row * P:(row + 1) * P], right[:, c, :],
                                               start=(t == 0 and c == 0), stop=(t == 1 and c == DC - 1))
                        mm.then_inc(fold_done, 1)
                pe.wait_ge(fold_ready, 4)
                for row in range(DC):
                    for t in range(2):
                        for c in range(DC):
                            mm = pe.matmul(ps_y[:, row, 0:D], folded[:, t, c, row * P:(row + 1) * P], back[:, t, c, :],
                                           start=(t == 0 and c == 0), stop=(t == 1 and c == DC - 1))
                    mm.then_inc(fold_done, 1)
                pe.wait_ge(fold_ready, 6)
                with pe.Fori(0, G) as g:
                    pe.wait_ge(n.xT_ready, 2 * g)
                    norm_group_pe(pe, n, g, ps_t, ident)
                    pe.wait_ge(n.xT_ready, 2 * g + 2)
                    for u in range(GU):
                        if u < 2:
                            pe.wait_ge(added, GU * g)
                        else:
                            pe.wait_ge(added, GU * g + u - 1)
                        for c in range(DC):
                            mm = pe.matmul(ps_y[0:T, u % 2, 0:D], n.xT[:, c, u * T:(u + 1) * T], m[:, c, :],
                                           start=(c == 0), stop=(c == DC - 1))
                        mm.then_inc(y_done, 1)

            @block.vector
            def _(dve):
                norm_statistics_dve(dve, n, hidden, 1e-5)
                dve.wait_ge(w_loaded, 80)
                steps = GroupSteps(dve, step, 0, GU)
                with dve.Fori(0, G) as g:
                    steps.begin(g)
                    norm_group_dve(dve, n, g, hidden)
                    for u in range(GU):
                        dve.wait_ge(y_done, GU * g + u + 1)
                        steps.link(dve.tensor_tensor(summed[0:T, u % 2, :], ps_y[0:T, u % 2, 0:D], bias[0:T, :], ALU.add))
                        dve.tensor_tensor(hidden[0:T, GU * g + u, :], hidden[0:T, GU * g + u, :], summed[0:T, u % 2, :],
                                          ALU.add).then_inc(added, 1)
                    steps.end()



def reshaped_projection(nc, shared, dram):
    hidden, ident, minus_half = (shared[k] for k in ("hidden", "ident", "minus_half"))
    with Scope(nc, "rproj") as s:
        n = Norm(s)
        w_qkv = s.sb("w_qkv", [P, DC, 3 * D])
        bias = s.sb("bias", [P, 3 * D])
        rows = s.sb("rows", [P, 2, 3, D])
        ps_t = s.ps("xturned", [P, 2, 512])
        ps_y = s.ps("product", [P, 2, 2, 512])
        w_loaded, y_done, y_copied = (s.sem(k) for k in ("w_loaded", "y_done", "y_copied"))
        stored = [s.sem(f"stored{j}") for j in range(2)]
        qkv = shared["qkv"]
        with nc.Block() as block:
            @block.sync
            def _(sync):
                sync.dma_start(w_qkv[:, :, :], dram["L1_attn_Wqkv"].rearrange("(c p) n -> p c n", p=P)).then_inc(w_loaded, 16)
                load_rows(sync, bias[0:T, :], dram["L1_attn_bqkv"], w_loaded)
                with sync.Fori(0, B // 2) as i:
                    for j in range(2):
                        sync.wait_ge(y_copied, 4 * i + 2 * j + 2)
                        sync.dma_start(qkv[bass.ds(2 * i + j, 1), :, :, :].rearrange("b a t d -> t (b a) d"),
                                       rows[0:T, j, :, :]).then_inc(stored[j], 16)
                for j in range(2):
                    sync.wait_ge(stored[j], 16 * (B // 2))

            @block.gpsimd
            def _(pool):
                norm_root_pool(pool, n, minus_half)

            @block.scalar
            def _(act):
                with act.Fori(0, G) as g:
                    act.wait_ge(y_done, GU * g)
                    norm_group_act(act, n, g, ps_t)

            @block.tensor
            def _(pe):
                pe.wait_ge(w_loaded, 32)
                with pe.Fori(0, G) as g:
                    pe.wait_ge(n.xT_ready, 2 * g)
                    norm_group_pe(pe, n, g, ps_t, ident)
                    pe.wait_ge(n.xT_ready, 2 * g + 2)
                    for u in range(GU):
                        if u < 2:
                            pe.wait_ge(y_copied, 2 * GU * g)
                        else:
                            pe.wait_ge(y_copied, 2 * (GU * g + u - 1))
                        for bank, (at, size) in enumerate(((0, 2 * D), (2 * D, D))):
                            for c in range(DC):
                                mm = pe.matmul(ps_y[0:T, u % 2, bank, 0:size], n.xT[:, c, u * T:(u + 1) * T],
                                               w_qkv[:, c, at:at + size], start=(c == 0), stop=(c == DC - 1))
                        mm.then_inc(y_done, 1)

            @block.vector
            def _(dve):
                norm_statistics_dve(dve, n, hidden, 1e-5)
                dve.wait_ge(w_loaded, 32)
                with dve.Fori(0, G) as g:
                    norm_group_dve(dve, n, g, hidden)
                    for u in range(GU):
                        dve.wait_ge(y_done, GU * g + u + 1)
                        if u < 2:
                            dve.wait_ge(stored[u], 32 * g)
                        else:
                            dve.wait_ge(stored[u % 2], 32 * g + 16)
                        dve.tensor_tensor(rows[0:T, u % 2, 0:2, :].rearrange("p a d -> p (a d)"), ps_y[0:T, u % 2, 0, 0:2 * D],
                                          bias[0:T, 0:2 * D], ALU.add).then_inc(y_copied, 1)
                        dve.tensor_tensor(rows[0:T, u % 2, 2, :], ps_y[0:T, u % 2, 1, 0:D], bias[0:T, 2 * D:],
                                          ALU.add).then_inc(y_copied, 1)


def reshaped_attention(nc, shared, dram):
    hidden, ident, ident16 = (shared[k] for k in ("hidden", "ident", "ident16"))
    with Scope(nc, "rattn") as s:
        a = Attention(s, HEADS, True, 1.0 / math.sqrt(HD))
        w_out = s.sb("w_out", [P, DC, D])
        o_bias = s.sb("o_bias", [P, D])
        heads = s.sb("heads", [P, 2, GU, 3, D])
        summed = s.sb("summed", [P, D])
        w_loaded = s.sem("w_loaded")
        heads_loaded = [s.sem(f"heads_loaded{j}") for j in range(2)]
        LOADS = 2
        source = shared["qkv"].rearrange("b a t d -> b a (t d)").rearrange("b a (h t e) -> b t a h e", h=HEADS, e=HD)
        with nc.Block() as block:
            @block.sync
            def _(sync):
                sync.dma_start(w_out[:, :, :], dram["L1_attn_Wproj"].rearrange("(c p) n -> p c n", p=P)).then_inc(w_loaded, 16)
                load_rows(sync, o_bias[0:T, :], dram["L1_attn_bproj"], w_loaded)
                with sync.Fori(0, G // 2) as i:
                    for j in range(2):
                        sync.wait_ge(a.v_ready, 2 * GU * i)
                        for u in range(GU):
                            for part in range(3):
                                sync.dma_start(heads[0:T, j, u, part, :].rearrange("p (h e) -> p h e", h=HEADS),
                                               source[bass.ds(2 * GU * i + GU * j + u, 1), :, part, :, :].rearrange(
                                                   "b t h e -> (b t) h e")).then_inc(heads_loaded[j], 16)

            @block.gpsimd
            def _(pool):
                attention_constants_pool(pool, a)

            @block.scalar
            def _(act):
                act.wait_ge(a.step, 1)
                with act.Fori(0, G // 2) as i:
                    for j in range(2):
                        g = 2 * i + j
                        queries_keys_act(act, a, g, None, None)
                        attention_act(act, a, g)

            @block.tensor
            def _(pe):
                pe.wait_ge(w_loaded, 16 * LOADS)
                pe.wait_ge(a.const_ready, attention_constants_ready(a))
                with pe.Fori(0, G // 2) as i:
                    for j in range(2):
                        g = 2 * i + j
                        pe.wait_ge(a.added, GU * g)
                        pe.wait_ge(a.ctxT_ready, GU * g)
                        pe.wait_ge(heads_loaded[j], 16 * 3 * GU * (i + 1))
                        for what, done in enumerate((a.q_done, a.k_done)):
                            for m in range(DC):
                                if what:
                                    pe.wait_ge(a.q_ready, 2 * g + m + 1)
                                for u in range(GU):
                                    mm = pe.transpose(a.ps_g[:, m, u * T:(u + 1) * T],
                                                      heads[0:T, j, u, what, m * P:(m + 1) * P], ident[0:T, 0:T])
                                mm.then_inc(done, 1)
                        pe.wait_ge(a.k_ready, 2 * g + 2)
                        attention_pe(pe, a, g, ident, ident16, w_out)

            @block.vector
            def _(dve):
                attention_constants_dve(dve, a, ident)
                dve.wait_ge(w_loaded, 16 * LOADS)
                dve.wait_ge(a.const_ready, 4)
                dve.wait_ge(a.step, 1)
                steps = GroupSteps(dve, a.step, 1, 12)
                with dve.Fori(0, G // 2) as i:
                    for j in range(2):
                        g = 2 * i + j
                        steps.begin(g)
                        dve.wait_ge(heads_loaded[j], 16 * 3 * GU * (i + 1))
                        dve.wait_ge(a.weighed, 4 + a.unit(g, 0, 0))
                        dve.wait_ge(a.k_done, 2 * g + 2)
                        for u in range(GU):
                            dve.tensor_copy(a.v[0:T, u, :, 0:HD], heads[0:T, j, u, 2, :].rearrange("p (h e) -> p h e", h=HEADS)
                                            ).then_inc(a.v_ready, 1)

                        def context(u):
                            outputs = a.ps_o[0:T, u % 2, 0:HEADS * (HD + 1)].rearrange("p (h e) -> p h e", h=HEADS)
                            steps.link(dve.reciprocal(a.rden[0:T, 0, :], outputs[:, :, HD]))
                            dve.tensor_tensor(a.ctx[0:T, u % 2, :].rearrange("p (h e) -> p h e", h=HEADS),
                                              outputs[:, :, 0:HD],
                                              a.rden[0:T, 0, :].unsqueeze(2).broadcast_to([T, HEADS, HD]),
                                              ALU.mult).then_inc(a.ctx_ready, 1)

                        def add(u):
                            dve.wait_ge(a.out_done, GU * g + u + 1)
                            steps.link(dve.tensor_tensor(summed[0:T, :], a.ps_g[0:T, 0, 0:D], o_bias[0:T, :], ALU.add))
                            dve.tensor_tensor(hidden[0:T, GU * g + u, :], hidden[0:T, GU * g + u, :], summed[0:T, :],
                                              ALU.add).then_inc(a.added, 1)

                        attention_dve(dve, a, g, steps, context, add)
                        steps.end()



def differential_attention(nc, shared, dram):
    hidden, ident, ident16, minus_half = (shared[k] for k in ("hidden", "ident", "ident16", "minus_half"))
    LAMBDA_INIT, EPS = 0.8 - 0.6 * math.exp(0.0), 1e-5
    MAPS = 2 * HEADS
    with Scope(nc, "dattn") as s:
        n = Norm(s)
        a = Attention(s, MAPS, True, 1.0 / (D // MAPS))
        w_qkv = s.sb("w_qkv", [P, DC, 3 * D])
        w_out = s.sb("w_out", [P, DC, D])
        lam = s.sb("lam", [P, 4, 8])
        lam_s = s.sb("lam_s", [P, 6])
        gamma = s.sb("gamma", [P, 2])
        diff = s.sb("diff", [P, 2, D])
        square = s.sb("square", [P, 3, HEADS])
        w_loaded, lam_summed, lam_exp, gamma_ready, ms_ready, rms_ready = (
            s.sem(k) for k in ("w_loaded", "lam_summed", "lam_exp", "gamma_ready", "ms_ready", "rms_ready"))
        LOADS = 6 + P // HD
        with nc.Block() as block:
            @block.sync
            def _(sync):
                sync.dma_start(w_qkv[:, :, :], dram["L2_attn_w_attn"].rearrange("(c p) n -> p c n", p=P)).then_inc(w_loaded, 16)
                sync.dma_start(w_out[:, :, :], dram["L2_attn_w_proj"].rearrange("(c p) n -> p c n", p=P)).then_inc(w_loaded, 16)
                for k, name in enumerate(("q1", "k1", "q2", "k2")):
                    load_rows(sync, lam[0:T, k, :], dram[f"L2_attn_lambda_{name}"], w_loaded)
                for k in range(P // HD):
                    sync.dma_start(gamma[k * HD:(k + 1) * HD, 0:1], dram["L2_attn_gamma"].rearrange("(e a) -> e a", a=1)
                                   ).then_inc(w_loaded, 16)

            @block.gpsimd
            def _(pool):
                attention_constants_pool(pool, a)
                norm_root_pool(pool, n, minus_half)
                with pool.Fori(0, G) as g:
                    for u in range(GU):
                        pool.wait_ge(ms_ready, GU * g + u + 1)
                        pool.tensor_tensor(square[0:T, 2, :], square[0:T, 1, :], minus_half[0:T, 0:HEADS],
                                           ALU.pow).then_inc(rms_ready, 1)

            @block.scalar
            def _(act):
                act.wait_ge(w_loaded, 16 * LOADS)
                act.activation(gamma[:, 1:2], gamma[:, 0:1], ACT.Copy, scale=1.0 - LAMBDA_INIT).then_inc(gamma_ready, 1)
                act.wait_ge(lam_summed, 2)
                act.activation(lam_s[0:T, 2:4], lam_s[0:T, 0:2], ACT.Exp).then_inc(lam_exp, 1)
                act.wait_ge(gamma_ready, 1)
                act.wait_ge(a.step, 1)
                with act.Fori(0, G) as g:
                    act.wait_ge(a.v_done, GU * g)
                    norm_group_act(act, n, g, a.ps_g)
                    queries_keys_act(act, a, g, None, None)
                    attention_act(act, a, g, ctx_scale=gamma[:, 1:2])

            @block.tensor
            def _(pe):
                pe.wait_ge(w_loaded, 16 * LOADS)
                pe.wait_ge(a.const_ready, attention_constants_ready(a))
                with pe.Fori(0, G) as g:
                    pe.wait_ge(a.added, GU * g)
                    pe.wait_ge(a.ctxT_ready, GU * g)
                    norm_group_pe(pe, n, g, a.ps_g, ident)
                    project_group_pe(pe, a, n, g, w_qkv, D)
                    attention_pe(pe, a, g, ident, ident16, w_out)

            @block.vector
            def _(dve):
                attention_constants_dve(dve, a, ident)
                norm_statistics_dve(dve, n, hidden, 1e-5)
                dve.wait_ge(w_loaded, 16 * LOADS)
                dve.wait_ge(a.const_ready, 4)
                dve.wait_ge(a.step, 1)
                steps = Chain(dve, a.step, 1)
                for k in range(2):
                    steps.link(dve.tensor_tensor(lam[0:T, 2 * k, :], lam[0:T, 2 * k, :], lam[0:T, 2 * k + 1, :], ALU.mult))
                    dve.tensor_reduce(lam_s[0:T, k:k + 1], lam[0:T, 2 * k, :], AX.X, ALU.add).then_inc(lam_summed, 1)
                dve.wait_ge(lam_exp, 1)
                steps.link(dve.tensor_tensor(lam_s[0:T, 4:5], lam_s[0:T, 3:4], lam_s[0:T, 2:3], ALU.subtract))
                steps.link(dve.tensor_scalar(lam_s[0:T, 5:6], lam_s[0:T, 4:5], LAMBDA_INIT, None, ALU.subtract))
                minus_lambda = lam_s[0:T, 5:6]
                steps = GroupSteps(dve, a.step, 5, GU * 7)
                with dve.Fori(0, G) as g:
                    steps.begin(g)
                    norm_group_dve(dve, n, g, hidden)
                    dve.wait_ge(a.weighed, 4 + a.unit(g, 0, 0))
                    for u in range(GU):
                        dve.wait_ge(a.v_done, GU * g + u + 1)
                        dve.tensor_copy(a.v[0:T, u, :, 0:HD],
                                        a.ps_g[0:T, u % 2, 0:D].rearrange("p (h e) -> p h e", h=HEADS)).then_inc(a.v_ready, 1)

                    def context(u):
                        first, second = (a.ps_o[0:T, k, 0:HEADS * (HD + 1)].rearrange("p (h e) -> p h e", h=HEADS)
                                         for k in range(2))
                        d0, d1 = (diff[0:T, k, :].rearrange("p (h e) -> p h e", h=HEADS) for k in range(2))
                        wide = lambda x: x.unsqueeze(2).broadcast_to([T, HEADS, HD])
                        dve.reciprocal(a.rden[0:T, 0, :], first[:, :, HD])
                        steps.link(dve.reciprocal(a.rden[0:T, 1, :], second[:, :, HD]))
                        steps.link(dve.tensor_scalar(a.rden[0:T, 1, :], a.rden[0:T, 1, :], minus_lambda, None, ALU.mult))
                        dve.tensor_tensor(d0, first[:, :, 0:HD], wide(a.rden[0:T, 0, :]), ALU.mult)
                        steps.link(dve.tensor_tensor(d1, second[:, :, 0:HD], wide(a.rden[0:T, 1, :]), ALU.mult))
                        steps.link(dve.tensor_tensor(d0, d0, d1, ALU.add))
                        steps.link(dve.tensor_tensor(d1, d0, d0, ALU.mult))
                        steps.link(dve.tensor_reduce(square[0:T, 0, :], d1, AX.X, ALU.add))
                        dve.tensor_scalar(square[0:T, 1, :], square[0:T, 0, :], 1.0 / HD, EPS, ALU.mult,
                                          ALU.add).then_inc(ms_ready, 1)
                        dve.wait_ge(rms_ready, GU * g + u + 1)
                        dve.tensor_tensor(a.ctx[0:T, u % 2, :].rearrange("p (h e) -> p h e", h=HEADS), d0,
                                          wide(square[0:T, 2, :]), ALU.mult).then_inc(a.ctx_ready, 1)

                    def add(u):
                        dve.wait_ge(a.out_done, GU * g + u + 1)
                        dve.tensor_tensor(hidden[0:T, GU * g + u, :], a.ps_g[0:T, 0, 0:D], hidden[0:T, GU * g + u, :],
                                          ALU.add).then_inc(a.added, 1)

                    attention_dve(dve, a, g, steps, context, add)
                    steps.end()

def layer1_attention(nc, shared, dram):
    shared["qkv"] = nc.dram_tensor("qkv_rows", (B, 3, T, D), F32, kind="Internal").ap()
    reshaped_projection(nc, shared, dram)
    reshaped_attention(nc, shared, dram)



def choose_two_dve(dve, s, steps, score, score2d, rows, wide_shape, restart, work, chosen):
    top, hit, rank, first = work["top"], work["hit"], work["rank"], work["first"]
    flat = lambda x: x[rows, :, :].rearrange("p b e -> p (b e)")
    left = score
    for k in range(2):
        steps.link(dve.tensor_reduce(top[rows, :], left[rows, :, :], AX.X, ALU.max))
        steps.link(dve.tensor_tensor(hit[rows, :, :], left[rows, :, :],
                                     top[rows, :].unsqueeze(2).broadcast_to(wide_shape), ALU.is_equal))
        steps.link(dve.tensor_tensor_scan(flat(rank), flat(restart), flat(hit), 0.0, ALU.mult, ALU.add))
        steps.link(dve.scalar_tensor_tensor(first[k][rows, :, :], rank[rows, :, :], 1.0, hit[rows, :, :],
                                            ALU.is_equal, ALU.mult))
        if k == 0:
            steps.link(dve.scalar_tensor_tensor(work["left"][rows, :, :], first[0][rows, :, :], MASKED,
                                                left[rows, :, :], ALU.mult, ALU.add))
            left = work["left"]
    steps.link(dve.tensor_tensor(chosen[rows, :, :], first[0][rows, :, :], first[1][rows, :, :], ALU.add))


def choice_buffers(s, sets, experts):
    work = {k: s.sb(f"choice_{k}", [P, sets, experts]) for k in ("hit", "rank", "left", "first0", "first1")}
    work["first"] = [work["first0"], work["first1"]]
    work["top"] = s.sb("choice_top", [P, sets])
    return work



def mixture(nc, shared, dram):
    hidden, ident, minus_half = (shared[k] for k in ("hidden", "ident", "minus_half"))
    E, F = 8, 1024
    FC = F // P
    with Scope(nc, "moe") as s:
        n = Norm(s)
        xT = s.sb("xT_all", [P, DC, B * T])
        w_router = s.sb("w_router", [P, DC, E])
        w1 = s.sb("w1", [P, 2, DC, F])
        w2 = s.sb("w2", [P, 2, FC, D])
        act1 = s.sb("act1", [P, FC, GT])
        logits = s.sb("logits", [P, B, E])
        prob = s.sb("prob", [P, B, E])
        chosen = s.sb("chosen", [P, B, E])
        weight = s.sb("weight", [P, B, E])
        restart = s.sb("restart", [P, B, E])
        total = s.sb("total", [P, 2, B])
        work = choice_buffers(s, B, E)
        ps_h = s.ps("hidden", [P, 4, 512])
        ps_y = s.ps("product", [P, 4, 512])
        (router_loaded, restart_ready, xT_kept, routed, logits_ready, step, prob_in, prob_exp, h_done, h_ready, y_done,
         y_added, expert_used, weight_ready) = (s.sem(k) for k in (
             "router_loaded", "restart_ready", "xT_kept", "routed", "logits_ready", "step", "prob_in", "prob_exp",
             "h_done", "h_ready", "y_done", "y_added", "expert_used", "weight_ready"))
        w_loaded = [s.sem(f"w_loaded{j}") for j in range(2)]
        with nc.Block() as block:
            @block.sync
            def _(sync):
                sync.dma_start(w_router[:, :, :], dram["L2_ffn_Wr"].rearrange("(c p) n -> p c n", p=P)).then_inc(router_loaded, 16)
                sync.sem_inc(expert_used, 2)
                with sync.Fori(0, E // 2) as i:
                    for j in range(2):
                        e = 2 * i + j
                        sync.wait_ge(expert_used, e + 1)
                        sync.dma_start(w1[:, j, :, :], dram["L2_ffn_W1"][bass.ds(e, 1), :, :].rearrange(
                            "e (c p) n -> p (e c) n", p=P)).then_inc(w_loaded[j], 16)
                        sync.dma_start(w2[:, j, :, :], dram["L2_ffn_W2"][bass.ds(e, 1), :, :].rearrange(
                            "e (c p) n -> p (e c) n", p=P)).then_inc(w_loaded[j], 16)

            @block.gpsimd
            def _(pool):
                pool.memset(restart[:, :, :], 1.0).then_inc(restart_ready, 1)
                pool.wait_ge(restart_ready, 1)
                pool.memset(restart[:, :, 0:1], 0.0).then_inc(restart_ready, 1)
                norm_root_pool(pool, n, minus_half)

            @block.scalar
            def _(act):
                with act.Fori(0, G) as g:
                    act.wait_ge(routed, GU * g)
                    norm_group_act(act, n, g, ps_h)
                    for c in range(DC):
                        act.activation(xT[:, c, bass.ds(g * GT, GT)], ps_h[:, c, 0:GT], ACT.Copy).then_inc(xT_kept, 1)
                act.wait_ge(prob_in, 1)
                act.activation(prob[0:T, :, :], logits[0:T, :, :], ACT.Exp).then_inc(prob_exp, 1)
                with act.Fori(0, E * G) as i:
                    act.wait_ge(y_done, GU * i)
                    for f in range(FC):
                        act.wait_ge(h_done, FC * i + f + 1)
                        act.activation(act1[:, f, :], ps_h[:, f % 4, 0:GT], ACT.Gelu).then_inc(h_ready, 1)

            @block.tensor
            def _(pe):
                pe.wait_ge(router_loaded, 16)
                with pe.Fori(0, G) as g:
                    pe.wait_ge(xT_kept, 2 * g)
                    norm_group_pe(pe, n, g, ps_h, ident)
                    pe.wait_ge(n.xT_ready, 2 * g + 2)
                    pe.wait_ge(logits_ready, g)
                    for u in range(GU):
                        for c in range(DC):
                            mm = pe.matmul(ps_y[0:T, 0, u * E:(u + 1) * E], n.xT[:, c, u * T:(u + 1) * T], w_router[:, c, :],
                                           start=(c == 0), stop=(c == DC - 1))
                        mm.then_inc(routed, 1)
                pe.wait_ge(xT_kept, 2 * G)
                pe.wait_ge(logits_ready, G)
                with pe.Fori(0, E // 2) as i:
                    for j in range(2):
                        with pe.Fori(0, G) as g:
                            r = (2 * i + j) * G + g
                            pe.wait_ge(w_loaded[j], 32 * (i + 1))
                            for f in range(FC):
                                if f < 4:
                                    pe.wait_ge(h_ready, FC * r)
                                else:
                                    pe.wait_ge(h_ready, FC * r + f - 3)
                                for c in range(DC):
                                    mm = pe.matmul(ps_h[:, f % 4, 0:GT], w1[:, j, c, f * P:(f + 1) * P],
                                                   xT[:, c, bass.ds(g * GT, GT)], start=(c == 0), stop=(c == DC - 1))
                                mm.then_inc(h_done, 1)
                            pe.wait_ge(h_ready, FC * r + FC)
                            pe.wait_ge(y_added, GU * r)
                            for u in range(GU):
                                for f in range(FC):
                                    mm = pe.matmul(ps_y[0:T, u, 0:D], act1[:, f, u * T:(u + 1) * T], w2[:, j, f, :],
                                                   start=(f == 0), stop=(f == FC - 1))
                                mm.then_inc(y_done, 1)

            @block.vector
            def _(dve):
                norm_statistics_dve(dve, n, hidden, 1e-5)
                with dve.Fori(0, G) as g:
                    norm_group_dve(dve, n, g, hidden)
                    dve.wait_ge(routed, GU * g + GU)
                    dve.tensor_copy(logits[0:T, bass.ds(GU * g, GU), :],
                                    ps_y[0:T, 0, 0:GU * E].rearrange("p (u e) -> p u e", e=E)).then_inc(logits_ready, 1)
                dve.wait_ge(logits_ready, G)
                dve.wait_ge(restart_ready, 2)
                rows, wide = slice(0, T), [T, B, E]
                steps = Chain(dve, step)
                steps.link(dve.tensor_reduce(total[rows, 0, :], logits[rows, :, :], AX.X, ALU.max))
                dve.tensor_tensor(logits[rows, :, :], logits[rows, :, :], total[rows, 0, :].unsqueeze(2).broadcast_to(wide),
                                  ALU.subtract).then_inc(prob_in, 1)
                dve.wait_ge(prob_exp, 1)
                steps.link(dve.tensor_reduce(total[rows, 0, :], prob[rows, :, :], AX.X, ALU.add))
                steps.link(dve.reciprocal(total[rows, 1, :], total[rows, 0, :]))
                steps.link(dve.tensor_tensor(prob[rows, :, :], prob[rows, :, :],
                                             total[rows, 1, :].unsqueeze(2).broadcast_to(wide), ALU.mult))
                choose_two_dve(dve, s, steps, prob, None, rows, wide, restart, work, chosen)
                steps.link(dve.tensor_tensor(weight[rows, :, :], prob[rows, :, :], chosen[rows, :, :], ALU.mult))
                with dve.Fori(0, E) as e:
                    with dve.Fori(0, G) as g:
                        for u in range(GU):
                            dve.wait_ge(y_done, (e * G + g) * GU + u + 1)
                            b = GU * g + u
                            dve.scalar_tensor_tensor(hidden[0:T, b, :], ps_y[0:T, u, 0:D],
                                                     weight[0:T, b, bass.ds(e, 1)], hidden[0:T, b, :],
                                                     ALU.mult, ALU.add).then_inc(y_added, 1)
                    dve.wait_ge(y_added, (e + 1) * B)
                    dve.sem_inc(expert_used, 1)



def state_space(nc, shared, dram):
    hidden, ident, minus_half = (shared[k] for k in ("hidden", "ident", "minus_half"))
    CH, N, TAPS, RANK = 512, 16, 4, 16
    CC = CH // P
    ROWS = RANK + 2 * N
    LN_EPS = 1e-5
    nodes = (np.cos(np.pi * (np.arange(64) + 0.5) / 64) + 1) / 18
    fit = np.polynomial.Chebyshev.fit(nodes, 2 * np.arctanh(np.sqrt(nodes)) / np.sqrt(nodes), 4, domain=[0, 1 / 9])
    ARTANH = [float(x) for x in fit.convert(kind=np.polynomial.Polynomial).coef]
    with Scope(nc, "ssm") as s:
        n = Norm(s)
        w_in = s.sb("w_in", [P, DC, 2 * CH])
        w_x = s.sb("w_x", [P, CC, ROWS])
        w_dt = s.sb("w_dt", [RANK, CH])
        w_out = s.sb("w_out", [P, CC, D])
        taps = s.sb("taps", [P, CC, TAPS])
        cols = s.sb("cols", [P, 3, CC])
        decay = s.sb("decay", [P, CC, N])
        gamma = s.sb("gamma", [P, D])
        beta = s.sb("beta", [P, D])
        x_in = s.sb("x_in", [P, CC, GT])
        conv = s.sb("conv", [P, CC, GT])
        xc = s.sb("xc", [P, CC, GT])
        gate = s.sb("gate", [P, CC, GT])
        dbc = s.sb("dbc", [ROWS, GT])
        pos = s.sb("pos", [P, CC, GT])
        mag = s.sb("mag", [P, CC, GT])
        delta = s.sb("delta", [P, CC, GT])
        du = s.sb("du", [P, CC, GT])
        ratio, square = du, conv
        bc = s.sb("bc", [P, 2, 2, 4, GT])
        dA = s.sb("dA", [P, 2, CC, GU, T])
        dBx = s.sb("dBx", [P, 2, CC, GT])
        state = s.sb("state", [P, 2, CC, GT])
        hC = s.sb("hC", [P, 2, CC, GT])
        yT = s.sb("yT", [P, CC, GT])
        res = s.sb("res", [P, GU, D])
        rstat = s.sb("rstat", [P, GU, 6])
        ragg = s.sb("ragg", [P, 3, GU])
        rroot = s.sb("rroot", [P, 2, GU])
        ps_a = s.ps("wide", [P, 4, 512])
        ps_b = s.ps("small", [P, 2, 512])
        names = ("w_loaded dA_zeroed decay_exp decay_ready xz_done xz_ready conv_ready xc_ready dbc_done dbc_ready dbc_stored "
                 "delta_done relu_ready sp_ready sp_step ratio_ready square_ready delta_ready du_ready dA_ready dbx_ready scanned hc_ready y_acc "
                 "y_taken yT_ready out_done out_read step spread2 rooted2").split()
        sem = {k: s.sem(k) for k in names}
        (w_loaded, dA_zeroed, decay_exp, decay_ready, xz_done, xz_ready, conv_ready, xc_ready, dbc_done, dbc_ready,
         dbc_stored, delta_done, relu_ready, sp_ready, sp_step, ratio_ready, square_ready, delta_ready, du_ready, dA_ready, dbx_ready, scanned,
         hc_ready, y_acc, y_taken, yT_ready, out_done, out_read, step, spread2, rooted2) = (sem[k] for k in names)
        bc_loaded = [s.sem(f"bc_loaded{j}") for j in range(2)]
        scratch = nc.dram_tensor("dbc_rows", (G, ROWS, GT), F32, kind="Internal").ap()
        LOADS = 11
        with nc.Block() as block:
            @block.sync
            def _(sync):
                for tile, name in ((w_in, "L3_attn_W_in"), (w_x, "L3_attn_W_x"), (w_out, "L3_attn_W_out"),
                                   (taps, "L3_attn_conv_w"), (decay, "L3_attn_A_log")):
                    sync.dma_start(tile[:, :, :], dram[name].rearrange("(c p) n -> p c n", p=P)).then_inc(w_loaded, 16)
                sync.dma_start(w_dt[:, :], dram["L3_attn_W_dt"]).then_inc(w_loaded, 16)
                for k, name in enumerate(("conv_b", "b_dt", "D")):
                    sync.dma_start(cols[:, k, :], dram[f"L3_attn_{name}_col"]).then_inc(w_loaded, 16)
                load_rows(sync, gamma[0:T, :], dram["L3_attn_gamma"], w_loaded)
                load_rows(sync, beta[0:T, :], dram["L3_attn_beta"], w_loaded)
                with sync.Fori(0, G) as g:
                    sync.wait_ge(dbc_ready, g + 1)
                    sync.dma_start(scratch[bass.ds(g, 1), :, :].rearrange("g r t -> (g r) t"), dbc[:, :]).then_inc(dbc_stored, 16)
                    sync.wait_ge(dbc_stored, 16 * (g + 1))
                    for q in range(N // 4):
                        sync.wait_ge(hc_ready, N * g + 4 * q + 4)
                        for k in range(2):
                            r = RANK + k * N + 4 * q
                            sync.dma_start(bc[:, q % 2, k, :, :].rearrange("p r t -> p (r t)"),
                                           scratch[bass.ds(g, 1), r:r + 4, :].rearrange("g r t -> (g r t)").partition_broadcast(P)
                                           ).then_inc(bc_loaded[q % 2], 16)

            @block.gpsimd
            def _(pool):
                pool.memset(dA[:, :, :, :, :], 0.0).then_inc(dA_zeroed, 1)
                norm_root_pool(pool, n, minus_half)
                with pool.Fori(0, G) as g:
                    pool.wait_ge(sp_ready, g + 1)
                    pool.tensor_tensor(delta[:, :, :], pos[:, :, :], mag[:, :, :], ALU.add).then_inc(delta_ready, 1)
                    pool.wait_ge(delta_ready, g + 1)
                    pool.tensor_tensor(du[:, :, :], delta[:, :, :], xc[:, :, :], ALU.mult).then_inc(du_ready, 1)
                    pool.wait_ge(du_ready, g + 1)
                    for k in range(N):
                        q = k // 4
                        pool.wait_ge(bc_loaded[q % 2], 64 * g + 32 * (q // 2 + 1))
                        pool.wait_ge(scanned, N * g + k + 1)
                        pool.tensor_tensor(dBx[:, k % 2, :, :], du[:, :, :],
                                           bc[:, q % 2, 0, k % 4, :].unsqueeze(1).broadcast_to([P, CC, GT]),
                                           ALU.mult).then_inc(dbx_ready, 1)
                    pool.wait_ge(spread2, g + 1)
                    pool.tensor_tensor(rroot[0:T, 1, :], rroot[0:T, 0, :], minus_half[0:T, 0:GU], ALU.pow).then_inc(rooted2, 1)

            @block.scalar
            def _(act):
                act.wait_ge(w_loaded, 16 * LOADS)
                act.activation(decay[:, :, :], decay[:, :, :], ACT.Exp).then_inc(decay_exp, 1)
                act.wait_ge(decay_ready, 1)
                act.wait_ge(dA_zeroed, 1)
                with act.Fori(0, G) as g:
                    act.wait_ge(xz_done, 8 * g)
                    norm_group_act(act, n, g, ps_b)
                    for m in range(2 * CC):
                        act.wait_ge(xz_done, 8 * g + m + 1)
                        if m == 0:
                            act.wait_ge(yT_ready, g)
                        act.activation((x_in if m < CC else gate)[:, m % CC, :], ps_a[:, m % 4, 0:GT],
                                       ACT.Copy if m < CC else ACT.Silu).then_inc(xz_ready, 1)
                    for c in range(CC):
                        act.wait_ge(conv_ready, CC * g + c + 1)
                        act.activation(xc[:, c, :], conv[:, c, :], ACT.Silu).then_inc(xc_ready, 1)
                    act.wait_ge(dbc_done, g + 1)
                    act.wait_ge(dbc_stored, 16 * g)
                    act.activation(dbc[:, :], ps_b[0:ROWS, 0, 0:GT], ACT.Copy).then_inc(dbc_ready, 1)
                    act.wait_ge(delta_ready, g)
                    for c in range(CC):
                        act.wait_ge(delta_done, CC * g + c + 1)
                        act.activation(mag[:, c, :], ps_a[:, c, 0:GT], ACT.Abs, bias=cols[:, 1, c:c + 1]).then_inc(sp_step, 1)
                        act.activation(pos[:, c, :], ps_a[:, c, 0:GT], ACT.Relu, bias=cols[:, 1, c:c + 1]).then_inc(relu_ready, 1)
                    act.wait_ge(sp_step, 5 * g + 4)
                    act.wait_ge(relu_ready, 4 * g + 4)
                    act.activation(mag[:, :, :], mag[:, :, :], ACT.Exp, scale=-1.0).then_inc(sp_step, 1)
                    act.wait_ge(ratio_ready, g + 1)
                    act.activation(square[:, :, :], ratio[:, :, :], ACT.Square).then_inc(square_ready, 1)
                    act.wait_ge(delta_ready, g + 1)
                    for k in range(N):
                        act.wait_ge(scanned, N * g + k + 1)
                        for c in range(CC):
                            ins = act.activation(dA[:, k % 2, c, :, 1:],
                                                 delta[:, c, :].rearrange("p (u t) -> p u t", u=GU)[:, :, 1:], ACT.Exp,
                                                 scale=decay[:, c, k:k + 1])
                        ins.then_inc(dA_ready, 1)

            @block.tensor
            def _(pe):
                pe.wait_ge(w_loaded, 16 * LOADS)
                with pe.Fori(0, G) as g:
                    pe.wait_ge(out_read, GU * g)
                    norm_group_pe(pe, n, g, ps_b, ident)
                    pe.wait_ge(n.xT_ready, 2 * g + 2)
                    for m in range(2 * CC):
                        if m < 4:
                            pe.wait_ge(y_taken, CC * g)
                        else:
                            pe.wait_ge(xz_ready, 8 * g + m - 3)
                        for c in range(DC):
                            mm = pe.matmul(ps_a[:, m % 4, 0:GT], w_in[:, c, m * P:(m + 1) * P], n.xT[:, c, :],
                                           start=(c == 0), stop=(c == DC - 1))
                        mm.then_inc(xz_done, 1)
                    for c in range(CC):
                        pe.wait_ge(xc_ready, CC * g + c + 1)
                        mm = pe.matmul(ps_b[0:ROWS, 0, 0:GT], w_x[:, c, :], xc[:, c, :], start=(c == 0), stop=(c == CC - 1))
                    mm.then_inc(dbc_done, 1)
                    pe.wait_ge(xz_ready, 8 * g + 8)
                    pe.wait_ge(dbc_ready, g + 1)
                    for c in range(CC):
                        pe.matmul(ps_a[:, c, 0:GT], w_dt[:, c * P:(c + 1) * P], dbc[0:RANK, :], start=True,
                                  stop=True).then_inc(delta_done, 1)
                    pe.wait_ge(relu_ready, CC * g + CC)
                    for k in range(N):
                        pe.wait_ge(hc_ready, 8 + N * g + k + 1)
                        for c in range(CC):
                            mm = pe.matmul(ps_a[:, c, 0:GT], ident[:, :], hC[:, k % 2, c, :], start=(k == 0),
                                           stop=(k == N - 1))
                        mm.then_inc(y_acc, 1)
                    pe.wait_ge(yT_ready, g + 1)
                    for u in range(GU):
                        if u >= 2:
                            pe.wait_ge(out_read, GU * g + u - 1)
                        for c in range(CC):
                            mm = pe.matmul(ps_b[0:T, u % 2, 0:D], yT[:, c, u * T:(u + 1) * T], w_out[:, c, :],
                                           start=(c == 0), stop=(c == CC - 1))
                        mm.then_inc(out_done, 1)

            @block.vector
            def _(dve):
                dve.sem_inc(scanned, 2)
                dve.sem_inc(y_acc, 2)
                dve.sem_inc(hc_ready, 8)
                norm_statistics_dve(dve, n, hidden, 1e-5)
                dve.wait_ge(w_loaded, 16 * LOADS)
                dve.wait_ge(decay_exp, 1)
                dve.tensor_scalar(decay[:, :, :], decay[:, :, :], -1.0, None, ALU.mult).then_inc(decay_ready, 1)
                steps = GroupSteps(dve, step, 0, 3 * CC + 2 * GU + 15)
                by_utterance = lambda x: x.rearrange("p (u t) -> p u t", u=GU)
                with dve.Fori(0, G) as g:
                    steps.begin(g)
                    norm_group_dve(dve, n, g, hidden)
                    for c in range(CC):
                        dve.wait_ge(xz_ready, 8 * g + c + 1)
                        if c == 0:
                            dve.wait_ge(xc_ready, CC * g)
                        steps.link(dve.tensor_scalar(conv[:, c, :], x_in[:, c, :], taps[:, c, TAPS - 1:TAPS], cols[:, 0, c:c + 1],
                                                     ALU.mult, ALU.add))
                        for back in range(1, TAPS):
                            to = by_utterance(conv[:, c, :])[:, :, back:]
                            ins = dve.scalar_tensor_tensor(to, by_utterance(x_in[:, c, :])[:, :, 0:T - back],
                                                           taps[:, c, TAPS - 1 - back:TAPS - back], to, ALU.mult, ALU.add)
                            if back < TAPS - 1:
                                steps.link(ins)
                            else:
                                ins.then_inc(conv_ready, 1)
                    dve.wait_ge(sp_step, 5 * g + 5)
                    dve.wait_ge(dbx_ready, N * g)
                    steps.link(dve.tensor_scalar(ratio[:, :, :], mag[:, :, :], 2.0, None, ALU.add))
                    steps.link(dve.reciprocal(ratio[:, :, :], ratio[:, :, :]))
                    dve.tensor_tensor(ratio[:, :, :], mag[:, :, :], ratio[:, :, :], ALU.mult).then_inc(ratio_ready, 1)
                    dve.wait_ge(square_ready, g + 1)
                    steps.link(dve.tensor_scalar(mag[:, :, :], square[:, :, :], ARTANH[-1], None, ALU.mult))
                    flat = lambda x: x[:, :, :].rearrange("p c t -> p (c t)")
                    for coefficient in ARTANH[-2:0:-1]:
                        steps.link(dve.scalar_tensor_tensor(flat(mag), flat(mag), coefficient, flat(square), ALU.add, ALU.mult))
                    dve.scalar_tensor_tensor(flat(mag), flat(mag), ARTANH[0], flat(ratio), ALU.add, ALU.mult).then_inc(sp_ready, 1)
                    for k in range(N):
                        q = k // 4
                        dve.wait_ge(dA_ready, N * g + k + 1)
                        dve.wait_ge(dbx_ready, N * g + k + 1)
                        dve.wait_ge(hc_ready, 7 + N * g + k)
                        dve.tensor_tensor_scan(state[:, k % 2, :, :].rearrange("p c t -> p (c t)"),
                                               dA[:, k % 2, :, :, :].rearrange("p c u t -> p (c u t)"),
                                               dBx[:, k % 2, :, :].rearrange("p c t -> p (c t)"), 0.0, ALU.mult,
                                               ALU.add).then_inc(scanned, 1)
                        dve.wait_ge(scanned, 2 + N * g + k + 1)
                        dve.wait_ge(y_acc, N * g + k + 1)
                        dve.tensor_tensor(hC[:, k % 2, :, :], state[:, k % 2, :, :],
                                          bc[:, q % 2, 1, k % 4, :].unsqueeze(1).broadcast_to([P, CC, GT]),
                                          ALU.mult).then_inc(hc_ready, 1)
                    dve.wait_ge(y_acc, 2 + N * g + N)
                    dve.wait_ge(hc_ready, 8 + N * g + N)
                    for c in range(CC):
                        dve.scalar_tensor_tensor(yT[:, c, :], xc[:, c, :], cols[:, 2, c:c + 1], ps_a[:, c, 0:GT], ALU.mult,
                                                 ALU.add).then_inc(y_taken, 1)
                    dve.wait_ge(y_taken, CC * g + CC)
                    dve.tensor_tensor(yT[:, :, :], yT[:, :, :], gate[:, :, :], ALU.mult).then_inc(yT_ready, 1)
                    for u in range(GU):
                        dve.wait_ge(out_done, GU * g + u + 1)
                        dve.tensor_tensor(res[0:T, u, :], ps_b[0:T, u % 2, 0:D], n.xn[0:T, u, :], ALU.add).then_inc(out_read, 1)
                        dve.wait_ge(out_read, GU * g + u + 1)
                        steps.link(dve.bn_stats(rstat[0:T, u, :], res[0:T, u, :]))
                    mean_e, m2_e, mean_o, m2_o = (rstat[0:T, :, k] for k in (1, 2, 4, 5))
                    mean, apart, both = (ragg[0:T, k, :] for k in range(3))
                    steps.link(dve.tensor_tensor(mean, mean_e, mean_o, ALU.add))
                    steps.link(dve.tensor_tensor(apart, mean_e, mean_o, ALU.subtract))
                    steps.link(dve.tensor_tensor(both, m2_e, m2_o, ALU.add))
                    steps.link(dve.tensor_scalar(mean, mean, 0.5, None, ALU.mult))
                    steps.link(dve.tensor_tensor(apart, apart, apart, ALU.mult))
                    steps.link(dve.tensor_scalar(both, both, 1.0 / D, LN_EPS, ALU.mult, ALU.add))
                    dve.scalar_tensor_tensor(rroot[0:T, 0, :], apart, 0.25, both, ALU.mult, ALU.add).then_inc(spread2, 1)
                    dve.wait_ge(rooted2, g + 1)
                    for u in range(GU):
                        steps.link(dve.tensor_scalar(res[0:T, u, :], res[0:T, u, :], ragg[0:T, 0, u:u + 1], rroot[0:T, 1, u:u + 1],
                                                     ALU.subtract, ALU.mult))
                    steps.link(dve.tensor_tensor(res[0:T, :, :], res[0:T, :, :],
                                                 gamma[0:T, :].unsqueeze(1).broadcast_to([T, GU, D]), ALU.mult))
                    steps.link(dve.tensor_tensor(res[0:T, :, :], res[0:T, :, :],
                                                 beta[0:T, :].unsqueeze(1).broadcast_to([T, GU, D]), ALU.add))
                    steps.link(dve.tensor_tensor(hidden[0:T, bass.ds(GU * g, GU), :], hidden[0:T, bass.ds(GU * g, GU), :],
                                                 res[0:T, :, :], ALU.add))
                    steps.end()



def expert_attention(nc, shared, dram):
    hidden, ident, ident16, minus_half = (shared[k] for k in ("hidden", "ident", "ident16", "minus_half"))
    E, R, GH = 8, 16, 64
    Q, K, V, O = range(4)
    with Scope(nc, "eattn") as s:
        n = Norm(s)
        a = Attention(s, HEADS, False, 1.0 / math.sqrt(HD))
        w = s.sb("w", [P, DC, 4 * D])
        up = s.sb("up", [P, 4, D])
        down = s.sb("down", [P, DC, 4, P])
        strength = s.sb("strength", [P, 4])
        gated = s.sb("gated", [P, 4, B])
        qk_bias = s.sb("qk_bias", [P, 2, DC])
        q_bias = s.sb("q_bias", [P, a.variants, DC])
        v_bias = s.sb("v_bias", [P, D])
        o_bias = s.sb("o_bias", [P, D])
        gw1 = s.sb("gw1", [P, DC, GH])
        gw2 = s.sb("gw2", [GH, E])
        gb1 = s.sb("gb1", [GH, 1])
        gb2 = s.sb("gb2", [P, E])
        pooled = s.sb("pooled", [P, DC, B])
        gate_h = s.sb("gate_h", [GH, B])
        score = s.sb("score", [P, 1, E])
        gate_e = s.sb("gate_e", [P, 1, E])
        chosen = s.sb("chosen", [P, 1, E])
        restart = s.sb("restart", [P, 1, E])
        total = s.sb("total", [P, 3])
        wide = s.sb("wide", [P, E, R])
        work = choice_buffers(s, 1, E)
        ranks = s.sb("ranks", [P, 3, GT])
        ranks_o = s.sb("ranks_o", [P, T])
        summed = s.sb("summed", [P, D])
        (w_loaded, restart_ready, pooled_ready, gates_done, gate_h_ready, gate_in, gate_exp, wide_ready, gated_ready, bias_ready,
         down_done, ranks_in, down_o_done) = (s.sem(k) for k in (
             "w_loaded", "restart_ready", "pooled_ready", "gates_done", "gate_h_ready", "gate_in", "gate_exp",
             "wide_ready", "gated_ready", "bias_ready", "down_done", "ranks_in", "down_o_done"))
        a.ranks_ready = s.sem("ranks_ready")
        LOADS = 4 * 4 + 2 + 2 + 4
        with nc.Block() as block:
            @block.sync
            def _(sync):
                for k, name in enumerate("qkvo"):
                    sync.dma_start(w[:, :, k * D:(k + 1) * D], dram[f"L3_ffn_{name}Wm"].rearrange("(c p) n -> p c n", p=P)
                                   ).then_inc(w_loaded, 16)
                    sync.dma_start(up[:, k, :], dram[f"L3_ffn_{name}U"]).then_inc(w_loaded, 16)
                    sync.dma_start(down[:, :, k, :], dram[f"L3_ffn_{name}V"].rearrange("(c p) n -> p c n", p=P)
                                   ).then_inc(w_loaded, 16)
                    sync.dma_start(strength[:, k:k + 1], dram[f"L3_ffn_{name}S"].rearrange("(e a) -> e a", a=1)
                                   ).then_inc(w_loaded, 16)
                for k, name in enumerate("qk"):
                    sync.dma_start(qk_bias[:, k, :], dram[f"L3_ffn_{name}b_col"]).then_inc(w_loaded, 16)
                load_rows(sync, v_bias[0:T, :], dram["L3_ffn_vb"], w_loaded)
                load_rows(sync, o_bias[0:T, :], dram["L3_ffn_ob"], w_loaded)
                sync.dma_start(gw1[:, :, :], dram["L3_ffn_gw1"].rearrange("(c p) n -> p c n", p=P)).then_inc(w_loaded, 16)
                sync.dma_start(gw2[:, :], dram["L3_ffn_gw2"]).then_inc(w_loaded, 16)
                sync.dma_start(gb1[:, :], dram["L3_ffn_gb1"].rearrange("(e a) -> e a", a=1)).then_inc(w_loaded, 16)
                load_rows(sync, gb2[0:B, :], dram["L3_ffn_gb2"], w_loaded, rows=B)

            @block.gpsimd
            def _(pool):
                pool.memset(restart[:, :, :], 1.0).then_inc(restart_ready, 1)
                pool.wait_ge(restart_ready, 1)
                pool.memset(restart[:, :, 0:1], 0.0).then_inc(restart_ready, 1)
                attention_constants_pool(pool, a)
                norm_root_pool(pool, n, minus_half)

            @block.scalar
            def _(act):
                act.wait_ge(w_loaded, 16 * LOADS)
                with act.Fori(0, G) as g:
                    act.wait_ge(pooled_ready, g)
                    norm_group_act(act, n, g, a.ps_g)
                act.wait_ge(gates_done, 1)
                act.activation(gate_h[:, :], a.ps_s[0:GH, 0, 0:B], ACT.Relu, scale=1.0 / T, bias=gb1[:, 0:1]
                               ).then_inc(gate_h_ready, 1)
                act.wait_ge(gate_in, 1)
                act.activation(gate_e[0:B, 0, :], score[0:B, 0, :], ACT.Exp).then_inc(gate_exp, 1)
                act.wait_ge(gated_ready, 4)
                act.wait_ge(bias_ready, a.variants)
                with act.Fori(0, G) as g:
                    act.wait_ge(a.v_done, GU * g)
                    norm_group_act(act, n, g + G, a.ps_g)
                    for k in range(3):
                        act.wait_ge(down_done, 3 * g + k + 1)
                        for u in range(GU):
                            ins = act.activation(ranks[:, k, u * T:(u + 1) * T], a.ps_g[:, (k + 1) % 2, u * T:(u + 1) * T],
                                                 ACT.Copy, scale=gated[:, k, bass.ds(GU * g + u, 1)])
                        ins.then_inc(ranks_in, 1)
                    queries_keys_act(act, a, g, q_bias, qk_bias[:, 1, :])

                    def ranks_out(u):
                        act.wait_ge(down_o_done, GU * g + u + 1)
                        act.activation(ranks_o[:, :], a.ps_g[:, 1, 0:T], ACT.Copy,
                                       scale=gated[:, O, bass.ds(GU * g + u, 1)]).then_inc(a.ranks_ready, 1)

                    attention_act(act, a, g, extra=ranks_out)

            @block.tensor
            def _(pe):
                pe.wait_ge(w_loaded, 16 * LOADS)
                pe.wait_ge(a.const_ready, attention_constants_ready(a))
                with pe.Fori(0, G) as g:
                    pe.wait_ge(n.xT_ready, 2 * g)
                    norm_group_pe(pe, n, g, a.ps_g, ident)
                pe.wait_ge(n.xT_ready, 2 * G)
                pe.wait_ge(pooled_ready, G)
                for c in range(DC):
                    mm = pe.matmul(a.ps_s[0:GH, 0, 0:B], gw1[:, c, :], pooled[:, c, :], start=(c == 0), stop=(c == DC - 1))
                mm.then_inc(gates_done, 1)
                pe.wait_ge(gate_h_ready, 1)
                pe.matmul(a.ps_t[0:B, 0, 0:E], gate_h[:, :], gw2[:, :], start=True, stop=True).then_inc(gates_done, 1)
                pe.wait_ge(wide_ready, 1)
                pe.transpose(a.ps_t[:, 1, 0:B], wide[0:B, :, :], ident[0:B, 0:B]).then_inc(gates_done, 1)
                pe.wait_ge(gated_ready, 4)
                with pe.Fori(0, G) as g:
                    pe.wait_ge(a.added, GU * g)
                    pe.wait_ge(a.ctxT_ready, GU * g)
                    pe.wait_ge(a.ranks_ready, GU * g)
                    norm_group_pe(pe, n, g + G, a.ps_g, ident)
                    pe.wait_ge(n.xT_ready, 2 * G + 2 * g + 2)
                    for k in range(3):
                        if k == 2:
                            pe.wait_ge(ranks_in, 3 * g + 1)
                        for c in range(DC):
                            mm = pe.matmul(a.ps_g[:, (k + 1) % 2, 0:GT], down[:, c, k, :], n.xT[:, c, :], start=(c == 0),
                                           stop=(c == DC - 1))
                        mm.then_inc(down_done, 1)
                    for k, done in ((Q, a.q_done), (K, a.k_done)):
                        for m in range(DC):
                            if k == Q:
                                pe.wait_ge(ranks_in, 3 * g + 2 + m)
                            else:
                                pe.wait_ge(a.q_ready, 2 * g + m + 1)
                            at = k * D + m * P
                            for c in range(DC):
                                pe.matmul(a.ps_g[:, m, 0:GT], w[:, c, at:at + P], n.xT[:, c, :], start=(c == 0), stop=False)
                            pe.matmul(a.ps_g[:, m, 0:GT], up[:, k, m * P:(m + 1) * P], ranks[:, k, :], start=False,
                                      stop=True).then_inc(done, 1)
                    for u in range(GU):
                        if u < 2:
                            pe.wait_ge(a.k_ready, 2 * g + u + 1)
                        else:
                            pe.wait_ge(a.v_ready, GU * g + u - 1)
                        for c in range(DC):
                            pe.matmul(a.ps_g[0:T, u % 2, 0:D], n.xT[:, c, u * T:(u + 1) * T], w[:, c, V * D:(V + 1) * D],
                                      start=(c == 0), stop=False)
                        pe.matmul(a.ps_g[0:T, u % 2, 0:D], ranks[:, V, u * T:(u + 1) * T], up[:, V, :], start=False,
                                  stop=True).then_inc(a.v_done, 1)

                    def ranks_of_output(u):
                        for c in range(DC):
                            mm = pe.matmul(a.ps_g[:, 1, 0:T], down[:, c, O, :], a.ctxT[:, c, :], start=(c == 0),
                                           stop=(c == DC - 1))
                        mm.then_inc(down_o_done, 1)

                    def add_experts(u):
                        pe.wait_ge(a.ranks_ready, GU * g + u + 1)
                        return pe.matmul(a.ps_g[0:T, 0, 0:D], ranks_o[:, :], up[:, O, :], start=False, stop=True)

                    attention_pe(pe, a, g, ident, ident16, w[:, :, O * D:(O + 1) * D], ranks_of_output, add_experts)

            @block.vector
            def _(dve):
                attention_constants_dve(dve, a, ident)
                norm_statistics_dve(dve, n, hidden, 1e-5)
                with dve.Fori(0, G) as g:
                    norm_group_dve(dve, n, g, hidden)
                    dve.wait_ge(n.xT_ready, 2 * g + 2)
                    dve.tensor_reduce(pooled[:, :, bass.ds(GU * g, GU)], n.xT[:, :, :].rearrange("p c (u t) -> p c u t", u=GU),
                                      AX.X, ALU.add).then_inc(pooled_ready, 1)
                dve.wait_ge(w_loaded, 16 * LOADS)
                dve.wait_ge(a.const_ready, 4)
                dve.wait_ge(a.step, 1)
                dve.wait_ge(restart_ready, 2)
                dve.wait_ge(gates_done, 2)
                steps = Chain(dve, a.step, 1)
                rows = slice(0, B)
                steps.link(dve.tensor_tensor(score[rows, 0, :], a.ps_t[rows, 0, 0:E], gb2[rows, :], ALU.add))
                choose_two_dve(dve, s, steps, score, None, rows, [B, 1, E], restart, work, chosen)
                steps.link(dve.tensor_reduce(total[rows, 0:1], score[rows, 0, :], AX.X, ALU.max))
                dve.tensor_scalar(score[rows, 0, :], score[rows, 0, :], total[rows, 0:1], None, ALU.subtract).then_inc(gate_in, 1)
                dve.wait_ge(gate_exp, 1)
                steps.link(dve.tensor_tensor(gate_e[rows, 0, :], gate_e[rows, 0, :], chosen[rows, 0, :], ALU.mult))
                steps.link(dve.tensor_reduce(total[rows, 1:2], gate_e[rows, 0, :], AX.X, ALU.add))
                steps.link(dve.reciprocal(total[rows, 2:3], total[rows, 1:2]))
                dve.tensor_scalar(wide[rows, :, :], gate_e[rows, 0, :].unsqueeze(2).broadcast_to([B, E, R]), total[rows, 2:3],
                                  None, ALU.mult).then_inc(wide_ready, 1)
                dve.wait_ge(gates_done, 3)
                for k in range(4):
                    dve.tensor_scalar(gated[:, k, :], a.ps_t[:, 1, 0:B], strength[:, k:k + 1], None,
                                      ALU.mult).then_inc(gated_ready, 1)
                for v in range(a.variants):
                    dve.tensor_scalar(q_bias[:, v, :], qk_bias[:, 0, :], a.only[:, v:v + 1], None, ALU.mult).then_inc(bias_ready, 1)
                steps = GroupSteps(dve, a.step, steps.base, 12)
                with dve.Fori(0, G) as g:
                    steps.begin(g)
                    dve.wait_ge(n.turned, GU * G + GU * g)
                    for u in range(GU):
                        b = GU * g + u
                        dve.tensor_scalar(n.xn[0:T, u, :], hidden[0:T, b, :], n.mean[0:T, bass.ds(b, 1)],
                                          n.rstd[0:T, bass.ds(b, 1)], ALU.subtract, ALU.mult).then_inc(n.normed, 1)
                    dve.wait_ge(a.weighed, 4 + a.unit(g, 0, 0))
                    for u in range(GU):
                        dve.wait_ge(a.v_done, GU * g + u + 1)
                        dve.tensor_tensor(a.v[0:T, u, :, 0:HD],
                                          a.ps_g[0:T, u % 2, 0:D].rearrange("p (h e) -> p h e", h=HEADS),
                                          v_bias[0:T, :].rearrange("p (h e) -> p h e", h=HEADS),
                                          ALU.add).then_inc(a.v_ready, 1)

                    def context(u):
                        outputs = a.ps_o[0:T, u % 2, 0:HEADS * (HD + 1)].rearrange("p (h e) -> p h e", h=HEADS)
                        steps.link(dve.reciprocal(a.rden[0:T, 0, :], outputs[:, :, HD]))
                        dve.tensor_tensor(a.ctx[0:T, u % 2, :].rearrange("p (h e) -> p h e", h=HEADS),
                                          outputs[:, :, 0:HD],
                                          a.rden[0:T, 0, :].unsqueeze(2).broadcast_to([T, HEADS, HD]),
                                          ALU.mult).then_inc(a.ctx_ready, 1)

                    def add(u):
                        dve.wait_ge(a.out_done, GU * g + u + 1)
                        steps.link(dve.tensor_tensor(summed[0:T, :], a.ps_g[0:T, 0, 0:D], o_bias[0:T, :], ALU.add))
                        dve.tensor_tensor(hidden[0:T, GU * g + u, :], hidden[0:T, GU * g + u, :], summed[0:T, :],
                                          ALU.add).then_inc(a.added, 1)

                    attention_dve(dve, a, g, steps, context, add)
                    steps.end()


LAYERS = (tokenizer, gated_attention, quantised_linear, layer1_attention, frequency_linear, differential_attention,
          mixture, state_space, expert_attention)



def audio_tower(nc, dram, out):
    with Scope(nc, "top") as top:
        shared = {"hidden": top.sb("hidden", [P, B, D])}
        constants(nc, top, shared)
        for layer in LAYERS:
            layer(nc, shared, dram)
        written = top.sem("written")
        with nc.Block() as block:
            @block.sync
            def _(sync):
                sync.dma_start(out.rearrange("b t d -> t b d"), shared["hidden"][0:T, :, :]).then_inc(written, 16)
                sync.wait_ge(written, 16)



def laid_out(inputs):
    a = {k: np.asarray(v) for k, v in inputs.items()}
    out = {}
    frames = np.zeros((B, (T + 1) * STRIDE, BANDS), a["x"].dtype)
    frames[:, :FRAMES] = a.pop("x")
    out["frames"] = frames.reshape(B, T + 1, STRIDE * BANDS).transpose(2, 0, 1)
    for k, v in a.items():
        out[k.replace("L0_tok", "tok")] = v
    out["tok_W1"] = out["tok_W1"].reshape(2, STRIDE * BANDS, D)
    for k in ("L0_attn_w_qkv", "L0_attn_w_ent", "L0_attn_w_out", "L0_ffn_weight_int8", "L3_ffn_gw1", "L3_ffn_gw2",
              "L3_ffn_qWm", "L3_ffn_kWm", "L3_ffn_vWm", "L3_ffn_oWm"):
        out[k] = out[k].T
    for p in "qkvo":
        U, V, S = (out[f"L3_ffn_{p}{m}"] for m in "UVS")
        out[f"L3_ffn_{p}U"] = U.transpose(0, 2, 1).reshape(-1, D)
        out[f"L3_ffn_{p}V"] = V.reshape(-1, D).T
        out[f"L3_ffn_{p}S"] = S.reshape(-1)
    for k, v in list(out.items()):
        if v.ndim == 1 and v.size % P == 0:
            out[k + "_col"] = v.reshape(-1, P).T
    n = np.arange(D)
    angle = 2.0 * np.pi * (np.outer(n, n) % D) / D
    out["dft"] = np.stack([np.cos(angle), np.sin(angle)]).astype(np.float32)
    out = {k: np.ascontiguousarray(v) for k, v in out.items()}
    out["L0_ffn_weight_int8"] = out["L0_ffn_weight_int8"].view(np.int32)
    return out


def kernel(**inputs):
    import concourse.bacc as bacc
    from concourse.bass_utils import run_bass_kernel_spmd as run

    nc = bacc.Bacc("TRN2", target_bir_lowering=False, num_devices=1)
    arrays, dram = {}, {}
    for name, a in laid_out(inputs).items():
        arrays[f"in_{name}"] = a
        dram[name] = nc.dram_tensor(f"in_{name}", a.shape, mybir.dt.from_np(a.dtype), kind="ExternalInput").ap()
    out = nc.dram_tensor("out", (B, T, D), F32, kind="ExternalOutput").ap()
    audio_tower(nc, dram, out)
    return run(nc, [arrays], core_ids=[0]).results[0]["out"]
```

```python
import math
from contextlib import ExitStack

import numpy as np
import concourse.bass as bass
from concourse import mybir

F32 = mybir.dt.float32
BF16 = mybir.dt.bfloat16
I8 = mybir.dt.int8
ACT = mybir.ActivationFunctionType
ALU = mybir.AluOpType
AX = mybir.AxisListType

P = 128
B = 32
FRAMES, BANDS = 375, 80
STRIDE, WINDOW = 4, 8
T = 93
D = 256
DC = D // P
GU = 4
G = B // GU
GT = GU * T
HEADS, HD = 16, 16
MASKED = -1.0e30
ROUND = 1.5 * 2.0 ** 23


class Chain:

    def __init__(self, eng, sem, base=0):
        self.eng, self.sem, self.base = eng, sem, base

    def link(self, ins):
        self.base = self.base + 1
        ins.then_inc(self.sem, 1)
        self.eng.wait_ge(self.sem, self.base)


class Scope:

    def __init__(self, nc, name):
        self.nc, self.name, self.stack, self.semaphores = nc, name, ExitStack(), []

    def __enter__(self):
        return self

    def __exit__(self, *a):
        self.stack.__exit__(*a)
        if self.semaphores:
            self.nc.clear_and_free_semaphores(self.semaphores)
            self.nc.all_engine_barrier()

    def sb(self, name, shape, dt=F32):
        return self.stack.enter_context(self.nc.sbuf_tensor(f"{self.name}_{name}", shape, dt))

    def ps(self, name, shape, dt=F32):
        return self.stack.enter_context(self.nc.psum_tensor(f"{self.name}_{name}", shape, dt))

    def sem(self, name):
        self.semaphores.append(self.nc.alloc_semaphore(f"{self.name}_{name}"))
        return self.semaphores[-1]



def constants(nc, top, shared):
    shared["ident"] = ident = top.sb("ident", [P, P])
    shared["ident16"] = ident16 = top.sb("ident16", [P, P], BF16)
    shared["minus_half"] = minus_half = top.sb("minus_half", [P, B])
    with Scope(nc, "const") as s:
        filled = s.sem("filled")
        with nc.Block() as block:
            @block.gpsimd
            def _(pool):
                pool.memset(ident[:, :], 0.0).then_inc(filled, 1)
                pool.memset(minus_half[:, :], -0.5).then_inc(filled, 1)
                pool.wait_ge(filled, 2)
                pool.affine_select(out=ident[:, :], in_=ident[:, :], compare_op=ALU.not_equal, fill=1.0, base=0,
                                   pattern=[[-1, P]], channel_multiplier=1).then_inc(filled, 1)

            @block.vector
            def _(dve):
                dve.wait_ge(filled, 3)
                dve.tensor_copy(ident16[:, :], ident[:, :]).then_inc(filled, 1)
                dve.wait_ge(filled, 4)



def tokenizer(nc, shared, dram):
    hidden, ident, minus_half = shared["hidden"], shared["ident"], shared["minus_half"]
    BLOCK = STRIDE * BANDS
    NBLK = T + 1
    rows = [P, P, BLOCK - 2 * P]
    with Scope(nc, "tok") as s:
        frames = s.sb("frames", [P, 3, B, NBLK])
        w1 = s.sb("w1", [P, 2, 3, D])
        w2 = s.sb("w2", [P, DC, D])
        cols = s.sb("cols", [P, 4, DC])
        hid1 = s.sb("hid1", [P, DC, GT])
        hid2 = s.sb("hid2", [P, DC, B * T])
        normal = s.sb("normal", [P, DC, GT])
        stat = s.sb("stat", [P, DC, G, 6])
        agg = s.sb("agg", [P, DC, 2])
        fold = s.sb("fold", [P, 4, DC])
        ps1 = s.ps("ps1", [P, 2, 512])
        ps2 = s.ps("ps2", [P, 2, 512])
        pst = s.ps("pst", [P, 2, 512])
        w_loaded = s.sem("w_loaded")
        cols_loaded = s.sem("cols_loaded")
        frames_loaded = [s.sem(f"frames_loaded{i}") for i in range(4)]
        first_done = s.sem("first_done")
        first_relu = s.sem("first_relu")
        second_done = s.sem("second_done")
        second_relu = s.sem("second_relu")
        step = s.sem("step")
        shifted = s.sem("shifted")
        rooted = s.sem("rooted")
        folded = s.sem("folded")
        normed = s.sem("normed")
        turned = s.sem("turned")
        placed = s.sem("placed")
        with nc.Block() as block:
            @block.sync
            def _(sync):
                for half in range(2):
                    for c in range(3):
                        sync.dma_start(w1[0:rows[c], half, c, :],
                                       dram["tok_W1"][half, c * P:c * P + rows[c], :]).then_inc(w_loaded, 16)
                sync.dma_start(w2[:, :, :], dram["tok_W2"].rearrange("(c p) n -> p c n", p=P)).then_inc(w_loaded, 16)
                for n, name in enumerate(("tok_b1", "tok_b2", "tok_gamma", "tok_beta")):
                    sync.dma_start(cols[:, n, :], dram[name + "_col"]).then_inc(cols_loaded, 16)

            @block.scalar
            def _(act):
                for part in range(4):
                    for c in range(3):
                        act.dma_start(frames[0:rows[c], c, 8 * part:8 * part + 8, :],
                                      dram["frames"][c * P:c * P + rows[c], 8 * part:8 * part + 8, :]
                                      ).then_inc(frames_loaded[part], 16)
                act.wait_ge(cols_loaded, 64)
                with act.Fori(0, G) as g:
                    for c in range(DC):
                        act.wait_ge(first_done, 2 * g + c + 1)
                        act.activation(hid1[:, c, :], ps1[:, c, 0:GT], ACT.Relu,
                                       bias=cols[:, 0, c:c + 1]).then_inc(first_relu, 1)
                    for c in range(DC):
                        act.wait_ge(second_done, 2 * g + c + 1)
                        act.activation(hid2[:, c, bass.ds(g * GT, GT)], ps2[:, c, 0:GT], ACT.Relu,
                                       bias=cols[:, 1, c:c + 1]).then_inc(second_relu, 1)
                act.wait_ge(folded, 1)
                with act.Fori(0, G) as g:
                    act.wait_ge(turned, 4 * g)
                    for c in range(DC):
                        act.activation(normal[:, c, :], hid2[:, c, bass.ds(g * GT, GT)], ACT.Identity,
                                       bias=fold[:, 3, c:c + 1], scale=fold[:, 2, c:c + 1]).then_inc(normed, 1)

            @block.tensor
            def _(pe):
                pe.wait_ge(w_loaded, 7 * 16)
                for part in range(4):
                    pe.wait_ge(frames_loaded[part], 48)
                with pe.Fori(0, G) as g:
                    for m in range(DC):
                        pe.wait_ge(first_relu, 2 * g)
                        for n in range(6):
                            half, c = n // 3, n % 3
                            mm = pe.matmul(ps1[:, m, 0:GT], w1[0:rows[c], half, c, m * P:(m + 1) * P],
                                           frames[0:rows[c], c, bass.ds(g * GU, GU), half:half + T],
                                           start=(n == 0), stop=(n == 5))
                        mm.then_inc(first_done, 1)
                    pe.wait_ge(first_relu, 2 * g + 2)
                    pe.wait_ge(second_relu, 2 * g)
                    for m in range(DC):
                        for c in range(DC):
                            mm = pe.matmul(ps2[:, m, 0:GT], w2[:, c, m * P:(m + 1) * P], hid1[:, c, :],
                                           start=(c == 0), stop=(c == DC - 1))
                        mm.then_inc(second_done, 1)
                with pe.Fori(0, G) as g:
                    pe.wait_ge(normed, 2 * g + 2)
                    for u in range(GU):
                        if u >= 2:
                            pe.wait_ge(placed, 4 * g + u - 1)
                        else:
                            pe.wait_ge(placed, 4 * g)
                        for c in range(DC):
                            mm = pe.transpose(pst[0:T, u % 2, c * P:(c + 1) * P], normal[:, c, u * T:(u + 1) * T],
                                              ident[:, :])
                        mm.then_inc(turned, 1)

            @block.vector
            def _(dve):
                with dve.Fori(0, G) as g:
                    for c in range(DC):
                        dve.wait_ge(second_relu, 2 * g + c + 1)
                        dve.bn_stats(stat[:, c, g, :], hid2[:, c, bass.ds(g * GT, GT)]).then_inc(step, 1)
                dve.wait_ge(step, 2 * G)
                steps = Chain(dve, step, 2 * G)
                for c in range(DC):
                    steps.link(dve.bn_aggr(agg[:, c, :], stat[:, c, :, :]))
                dve.tensor_scalar(fold[:, 0, :], agg[:, :, 1], 1e-5, None, ALU.add).then_inc(shifted, 1)
                dve.wait_ge(rooted, 1)
                dve.wait_ge(cols_loaded, 64)
                steps.link(dve.tensor_tensor(fold[:, 2, :], fold[:, 1, :], cols[:, 2, :], ALU.mult))
                steps.link(dve.tensor_tensor(fold[:, 0, :], agg[:, :, 0], fold[:, 2, :], ALU.mult))
                dve.tensor_tensor(fold[:, 3, :], cols[:, 3, :], fold[:, 0, :], ALU.subtract).then_inc(folded, 1)
                with dve.Fori(0, G) as g:
                    for u in range(GU):
                        dve.wait_ge(turned, 4 * g + u + 1)
                        dve.tensor_copy(hidden[0:T, 4 * g + u, :], pst[0:T, u % 2, 0:D]).then_inc(placed, 1)

            @block.gpsimd
            def _(pool):
                pool.wait_ge(shifted, 1)
                pool.tensor_tensor(fold[:, 1, :], fold[:, 0, :], minus_half[:, 0:DC], ALU.pow).then_inc(rooted, 1)



class Norm:

    def __init__(self, s, prefix=""):
        self.stat = s.sb(prefix + "stat", [P, B, 6])
        self.tmp = s.sb(prefix + "stat_tmp", [P, 4, B])
        self.mean = s.sb(prefix + "mean", [P, B])
        self.rstd = s.sb(prefix + "rstd", [P, B])
        self.xn = s.sb(prefix + "xn", [P, GU, D])
        self.xT = s.sb(prefix + "xT", [P, DC, GT])
        self.measured = s.sem(prefix + "measured")
        self.step = s.sem(prefix + "norm_step")
        self.spread = s.sem(prefix + "spread")
        self.rooted = s.sem(prefix + "rooted")
        self.normed = s.sem(prefix + "normed")
        self.turned = s.sem(prefix + "turned")
        self.xT_ready = s.sem(prefix + "xT_ready")


def norm_statistics_dve(dve, n, source, eps):
    with dve.Fori(0, B) as b:
        dve.bn_stats(n.stat[0:T, b, :], source[0:T, b, :]).then_inc(n.measured, 1)
    dve.wait_ge(n.measured, B)
    mean_e, m2_e, mean_o, m2_o = (n.stat[0:T, :, k] for k in (1, 2, 4, 5))
    t = [n.tmp[0:T, k, :] for k in range(4)]
    steps = Chain(dve, n.step)
    dve.tensor_tensor(t[0], mean_e, mean_o, ALU.add).then_inc(n.step, 1)
    dve.tensor_tensor(t[1], mean_e, mean_o, ALU.subtract).then_inc(n.step, 1)
    dve.tensor_tensor(t[2], m2_e, m2_o, ALU.add).then_inc(n.step, 1)
    steps.base = 3
    dve.wait_ge(n.step, 3)
    dve.tensor_scalar(n.mean[0:T, :], t[0], 0.5, None, ALU.mult).then_inc(n.step, 1)
    dve.tensor_tensor(t[3], t[1], t[1], ALU.mult).then_inc(n.step, 1)
    dve.tensor_scalar(t[2], t[2], 1.0 / D, eps, ALU.mult, ALU.add).then_inc(n.step, 1)
    dve.wait_ge(n.step, 6)
    dve.scalar_tensor_tensor(t[0], t[3], 0.25, t[2], ALU.mult, ALU.add).then_inc(n.spread, 1)
    dve.wait_ge(n.rooted, 1)


def norm_root_pool(pool, n, minus_half):
    pool.wait_ge(n.spread, 1)
    pool.tensor_tensor(n.rstd[0:T, :], n.tmp[0:T, 0, :], minus_half[0:T, :], ALU.pow).then_inc(n.rooted, 1)


def norm_group_dve(dve, n, g, source):
    dve.wait_ge(n.turned, GU * g)
    for u in range(GU):
        b = GU * g + u
        dve.tensor_scalar(n.xn[0:T, u, :], source[0:T, b, :], n.mean[0:T, bass.ds(b, 1)], n.rstd[0:T, bass.ds(b, 1)],
                          ALU.subtract, ALU.mult).then_inc(n.normed, 1)


def norm_group_pe(pe, n, g, banks, ident):
    for u in range(GU):
        pe.wait_ge(n.normed, GU * g + u + 1)
        for c in range(DC):
            mm = pe.transpose(banks[:, c, u * T:(u + 1) * T], n.xn[0:T, u, c * P:(c + 1) * P], ident[0:T, 0:T])
        mm.then_inc(n.turned, 1)


def norm_group_act(act, n, g, banks, scale=None, shift=None):
    act.wait_ge(n.turned, GU * g + GU)
    for c in range(DC):
        act.activation(n.xT[:, c, :], banks[:, c, 0:GT], ACT.Identity,
                       bias=0.0 if shift is None else shift[:, c:c + 1],
                       scale=1.0 if scale is None else scale[:, c:c + 1]).then_inc(n.xT_ready, 1)



class Attention:

    def __init__(self, s, maps, causal, exp_scale):
        self.maps, self.causal, self.exp_scale = maps, causal, exp_scale
        self.width = D // maps
        self.variants = P // self.width
        self.units = maps // 4
        self.banks_o = maps // HEADS
        self.turn_at = 1 if self.units == 4 else 4
        self.q_all = s.sb("q_all", [P, DC, B * T])
        self.k_all = s.sb("k_all", [P, DC, B * T])
        self.v = s.sb("v", [P, B, HEADS, HD + 1])
        self.q = s.sb("q", [P, 2, DC, self.variants, T])
        self.k = s.sb("k", [P, 2, DC, T])
        self.only = s.sb("only", [P, self.variants])
        self.sel = s.sb("sel", [P, maps, T], BF16)
        self.negmax = s.sb("negmax", [P, maps])
        self.split_width = 2 * maps if maps == HEADS else 2 * maps + 2
        self.split = s.sb("split", [P, self.split_width], BF16)
        self.maxT = s.sb("maxT", [P, T], BF16)
        self.probs = s.sb("probs", [P, 4, GT])
        self.rden = s.sb("rden", [P, self.banks_o, HEADS])
        self.ctx = s.sb("ctx", [P, 2, D])
        self.ctxT = s.sb("ctxT", [P, DC, T])
        if causal:
            self.mask_q = s.sb("mask_q", [P, 4, T], BF16)
            self.mask_k = s.sb("mask_k", [P, 4, T], BF16)
        self.ps_s = s.ps("scores", [P, 2, 512])
        self.ps_t = s.ps("scoresT", [P, 2, 512])
        self.ps_o = s.ps("outputs", [P, 2, 512])
        self.ps_g = s.ps("general", [P, 2, 512])
        self.const_ready = s.sem("att_const")
        self.q_done = s.sem("q_done")
        self.k_done = s.sem("k_done")
        self.v_done = s.sem("v_done")
        self.q_ready = s.sem("q_ready")
        self.k_ready = s.sem("k_ready")
        self.v_ready = s.sem("v_ready")
        self.v_gated = None
        self.ranks_ready = None
        self.cut_ready = s.sem("cut_ready")
        self.scored = s.sem("scored")
        self.maxed = s.sem("maxed")
        self.split_ready = s.sem("split_ready")
        self.max_turned = s.sem("max_turned")
        self.maxT_ready = s.sem("maxT_ready")
        self.scoredT = s.sem("scoredT")
        self.probs_ready = s.sem("probs_ready")
        self.weighed = s.sem("weighed")
        self.outputs_read = s.sem("outputs_read")
        self.ctx_ready = s.sem("ctx_ready")
        self.ctx_turned = s.sem("ctx_turned")
        self.ctxT_ready = s.sem("ctxT_ready")
        self.out_done = s.sem("out_done")
        self.added = s.sem("added")
        self.biased = s.sem("biased")
        self.half_split = s.sem("half_split")
        self.step = s.sem("att_step")

    def chunk(self, w):
        return 4 * w // self.variants, 4 * w % self.variants


def over_utterances(eng, body):
    body(0, 0, True, False)
    with eng.Fori(0, B // 2 - 1) as i:
        for j in range(2):
            body(2 * i + j + 1, 1 - j, False, False)
    body(B - 1, 1, False, True)


def attention_constants_pool(pool, a):
    pool.memset(a.sel[:, :, :], 0.0).then_inc(a.const_ready, 1)
    pool.memset(a.v[:, :, :, HD:HD + 1], 1.0).then_inc(a.const_ready, 1)
    pool.memset(a.maxT[:, :], 0.0).then_inc(a.const_ready, 1)
    pool.memset(a.split[:, :], 0.0).then_inc(a.const_ready, 1)
    pool.wait_ge(a.const_ready, 4)
    for part in range(2):
        pool.affine_select(out=a.sel[:, :, :], in_=a.sel[:, :, :], compare_op=ALU.not_equal, fill=1.0,
                           base=-part * a.maps, pattern=[[-1, a.maps], [0, T]],
                           channel_multiplier=1).then_inc(a.const_ready, 1)
        pool.wait_ge(a.const_ready, 5 + part)
    if a.causal:
        for m in (a.mask_q, a.mask_k):
            pool.memset(m[:, :, :], 0.0).then_inc(a.const_ready, 1)
        pool.wait_ge(a.const_ready, 8)
        for m, sign in ((a.mask_q, -1), (a.mask_k, 1)):
            pool.affine_select(out=m[:, :, :], in_=m[:, :, :], compare_op=ALU.is_ge, fill=MASKED, base=0,
                               pattern=[[0, 4], [sign, T]], channel_multiplier=-sign).then_inc(a.const_ready, 1)


def attention_constants_dve(dve, a, ident):
    rows = ident[:, :].rearrange("p (v e) -> p v e", v=a.variants)
    dve.tensor_reduce(a.only[:, :], rows, AX.X, ALU.add).then_inc(a.step, 1)
    dve.sem_inc(a.maxed, 2)
    dve.sem_inc(a.probs_ready, 2)
    dve.sem_inc(a.weighed, 4)
    dve.sem_inc(a.scoredT, 2 * a.units)
    dve.sem_inc(a.outputs_read, 3 - a.banks_o)


def attention_constants_ready(a):
    return 10 if a.causal else 6


def attention_pool(pool, a, root=None):
    pool.wait_ge(a.step, 1)
    pool.wait_ge(a.q_ready, DC * G)
    pool.wait_ge(a.k_ready, DC * G)

    def cut(b, buf, c):
        pool.wait_ge(a.scoredT, a.units * b + (c + 1) * a.units // DC)
        pool.tensor_tensor(a.q[:, buf, c, :, :],
                           a.q_all[:, c, bass.ds(b * T, T)].unsqueeze(1).broadcast_to([P, a.variants, T]),
                           a.only[:, :].unsqueeze(2).broadcast_to([P, a.variants, T]), ALU.mult)
        pool.tensor_copy(a.k[:, buf, c, :], a.k_all[:, c, bass.ds(b * T, T)]).then_inc(a.cut_ready, 1)

    def step(b, buf):
        cut(b + 1, 1 - buf, 1)
        if root is not None:
            root(b - 1)
        cut(b + 2, buf, 0)

    cut(0, 0, 0)
    cut(0, 0, 1)
    cut(1, 1, 0)
    cut(1, 1, 1)
    cut(2, 0, 0)
    with pool.Fori(0, B // 2 - 2) as i:
        for j in range(2):
            step(2 * i + j + 1, 1 - j)
    step(B - 3, 1)
    cut(B - 1, 1, 1)
    if root is not None:
        for b in (B - 3, B - 2, B - 1):
            root(b)


def attention_pe(pe, a, ident, ident16, w_out, before_out=None, extra_out=None):

    def scores(b, buf, w):
        if w % (a.units // DC) == 0:
            pe.wait_ge(a.cut_ready, DC * b + (w * DC // a.units + 1))
        pe.wait_ge(a.maxed, b * a.units + (w + 1))
        bank = a.ps_s[0:T, w % 2, :]
        if a.causal:
            pe.matmul(bank[:, 0:GT], ident16[:, 0:T], a.mask_q[:, :, :], start=True, stop=False,
                      skip_group_check=True)
        c, v = a.chunk(w)
        for j in range(4):
            mm = pe.matmul(bank[:, j * T:(j + 1) * T], a.q[:, buf, c, v + j, :], a.k[:, buf, c, :],
                           start=not a.causal, stop=True, skip_group_check=True)
        mm.then_inc(a.scored, 1)

    def turn_max(b, first):
        pe.wait_ge(a.split_ready, b + 1)
        if not first:
            pe.wait_ge(a.added, b - 1)
        pe.transpose(a.ps_g[0:a.split_width, 0, :].bitcast(BF16)[:, 0:T], a.split[0:T, :],
                     ident16[0:T, 0:T]).then_inc(a.max_turned, 1)

    def scores_t(b, buf, w):
        pe.wait_ge(a.probs_ready, b * a.units + (w + 1))
        bank = a.ps_t[0:T, w % 2, :]
        if a.causal:
            pe.matmul(bank[:, 0:GT], ident16[:, 0:T], a.mask_k[:, :, :], start=True, stop=False,
                      skip_group_check=True)
        c, v = a.chunk(w)
        pe.matmul(bank[:, 0:GT], a.k[:, buf, c, :], a.q[:, buf, c, v:v + 4, :], start=not a.causal, stop=False,
                  skip_group_check=True)
        if w == 0:
            pe.wait_ge(a.maxT_ready, b + 1)
        for j in range(4):
            mm = pe.matmul(bank[:, j * T:(j + 1) * T], a.sel[:, 4 * w + j, :], a.maxT[:, :], start=False, stop=True,
                           skip_group_check=True)
        mm.then_inc(a.scoredT, 1)

    def weigh(b, buf, w):
        if w == 0:
            pe.wait_ge(a.outputs_read, b + 1)
        pe.wait_ge(a.probs_ready, b * a.units + (w + 3))
        for j in range(4):
            m = 4 * w + j
            if a.banks_o == 1:
                h, bank = m, buf
            else:
                h, bank = m // 2, m % 2
            mm = pe.matmul(a.ps_o[0:T, bank, h * (HD + 1):(h + 1) * (HD + 1)], a.probs[0:T, w % 4, j * T:(j + 1) * T],
                           a.v[0:T, b, h, :], start=True, stop=True, skip_group_check=True)
        mm.then_inc(a.weighed, 1)

    def turn_ctx(b, buf, first):
        pe.wait_ge(a.ctx_ready, b + 1)
        if not first:
            pe.wait_ge(a.ctxT_ready, b)
            if a.ranks_ready is not None:
                pe.wait_ge(a.ranks_ready, b)
        for c in range(DC):
            mm = pe.transpose(a.ps_g[:, 1, c * T:(c + 1) * T], a.ctx[0:T, buf, c * P:(c + 1) * P], ident[0:T, 0:T])
        mm.then_inc(a.ctx_turned, 1)

    def project(b, first, last):
        pe.wait_ge(a.ctxT_ready, b + 1)
        if not first:
            pe.wait_ge(a.added, b)
        if not last:
            pe.wait_ge(a.maxT_ready, b + 2)
        if before_out is not None:
            before_out(b)
        for c in range(DC):
            mm = pe.matmul(a.ps_g[0:T, 0, 0:D], a.ctxT[:, c, :], w_out[:, c, :], start=(c == 0),
                           stop=(c == DC - 1 and extra_out is None))
        if extra_out is not None:
            mm = extra_out(b)
        mm.then_inc(a.out_done, 1)

    def utterance(b, buf, first, last, second=False):
        for w in range(a.units):
            if not last:
                scores(b + 1, 1 - buf, w)
            scores_t(b, buf, w)
            if w:
                weigh(b, buf, w - 1)
            if not first:
                if w == a.turn_at:
                    turn_ctx(b - 1, 1 - buf, second)
                if w == a.units - 2:
                    project(b - 1, second, False)
        weigh(b, buf, a.units - 1)
        if not last:
            turn_max(b + 1, False)

    pe.wait_ge(a.v_ready if a.v_gated is None else a.v_gated, B)
    for w in range(a.units):
        scores(0, 0, w)
    turn_max(0, True)
    over_utterances(pe, utterance)
    turn_ctx(B - 1, 1, False)
    project(B - 1, False, True)


def attention_act(act, a, ctx_scale=None, extra=None):

    def ctx_t(b):
        act.wait_ge(a.ctx_turned, b + 1)
        act.wait_ge(a.out_done, b)
        if ctx_scale is None:
            act.activation(a.ctxT[:, :, :], a.ps_g[:, 1, 0:DC * T], ACT.Copy).then_inc(a.ctxT_ready, 1)
        else:
            act.activation(a.ctxT[:, :, :], a.ps_g[:, 1, 0:DC * T], ACT.Copy,
                           scale=ctx_scale).then_inc(a.ctxT_ready, 1)

    def utterance(b, buf, first, last):
        for w in range(a.units):
            n = b * a.units + w
            act.wait_ge(a.scoredT, n + (2 * a.units + 1))
            act.wait_ge(a.weighed, n + 1)
            act.activation(a.probs[0:T, w % 4, :], a.ps_t[0:T, w % 2, 0:GT], ACT.Exp,
                           scale=a.exp_scale).then_inc(a.probs_ready, 1)
            if w == a.turn_at and not first:
                ctx_t(b - 1)
                if extra is not None:
                    extra(b - 1)

    over_utterances(act, utterance)
    ctx_t(B - 1)
    if extra is not None:
        extra(B - 1)


def attention_dve(dve, a, steps, context, add, finish=None):

    def maximum(b, w):
        dve.wait_ge(a.scored, b * a.units + (w + 1))
        dve.tensor_reduce(a.negmax[0:T, 4 * w:4 * w + 4],
                          a.ps_s[0:T, w % 2, 0:GT].rearrange("p (j t) -> p j t", j=4), AX.X, ALU.max,
                          negate=True).then_inc(a.maxed, 1)

    def split(b):
        dve.wait_ge(a.maxed, 2 + (b + 1) * a.units)
        dve.tensor_copy(a.split[0:T, 0:a.maps], a.negmax[0:T, :]).then_inc(a.half_split, 1)
        dve.wait_ge(a.half_split, b + 1)
        dve.tensor_tensor(a.split[0:T, a.maps:2 * a.maps], a.negmax[0:T, :], a.split[0:T, 0:a.maps],
                          ALU.subtract).then_inc(a.split_ready, 1)
        dve.wait_ge(a.split_ready, b + 1)

    def max_t(b):
        dve.wait_ge(a.max_turned, b + 1)
        dve.wait_ge(a.scoredT, a.units * (b + 2))
        dve.tensor_copy(a.maxT[0:2 * a.maps, :], a.ps_g[0:2 * a.maps, 0, :].bitcast(BF16)[:, 0:T]).then_inc(a.maxT_ready, 1)

    def utterance(b, buf, first, last):
        if last:
            if finish is not None:
                finish(b - 1, 1 - buf)
        else:
            for w in range(a.units):
                maximum(b + 1, w)
                if w == 1 and not first and finish is not None:
                    finish(b - 1, 1 - buf)
            split(b + 1)
        if not first:
            add(b - 1)
        if not last:
            max_t(b + 1)
        dve.wait_ge(a.weighed, 4 + a.units * (b + 1))
        steps.begin(b)
        context(b, buf)
        steps.end()

    for w in range(a.units):
        maximum(0, w)
    split(0)
    max_t(0)
    over_utterances(dve, utterance)
    if finish is not None:
        finish(B - 1, 1)
    add(B - 1)


class GroupSteps:

    def __init__(self, eng, sem, base, per):
        self.eng, self.sem, self.base, self.per = eng, sem, base, per

    def begin(self, g):
        self.g, self.n = g, 0
        return self

    def link(self, ins):
        self.n += 1
        ins.then_inc(self.sem, 1)
        self.eng.wait_ge(self.sem, self.g * self.per + (self.base + self.n))

    def end(self):
        assert self.n == self.per, (self.n, self.per)


def load_rows(eng, tile, vector, sem, rows=T):
    eng.dma_start(tile, vector.partition_broadcast(rows)).then_inc(sem, 16)


def project_group_pe(pe, a, n, g, w_qkv, v_cols):
    pe.wait_ge(n.xT_ready, 2 * g + 2)
    for what, (bank, done, read) in enumerate(((a.ps_s, a.q_done, a.q_ready), (a.ps_t, a.k_done, a.k_ready))):
        for m in range(DC):
            pe.wait_ge(read, DC * g)
            for c in range(DC):
                mm = pe.matmul(bank[:, m, 0:GT], w_qkv[:, c, what * D + m * P:what * D + (m + 1) * P],
                               n.xT[:, c, :], start=(c == 0), stop=(c == DC - 1))
            mm.then_inc(done, 1)
    for u in range(GU):
        values_free_pe(pe, a, g, u)
        for c in range(DC):
            mm = pe.matmul(a.ps_g[0:T, u % 2, 0:v_cols], n.xT[:, c, u * T:(u + 1) * T],
                           w_qkv[:, c, 2 * D:2 * D + v_cols], start=(c == 0), stop=(c == DC - 1))
        mm.then_inc(a.v_done, 1)


def values_free_pe(pe, a, g, u):
    if u < 2:
        pe.wait_ge(a.v_ready, GU * g)
    else:
        pe.wait_ge(a.v_ready, GU * g + (u - 1))


def queries_keys_act(act, a, g, q_bias, k_bias):
    for kept, bank, done, ready, bias in ((a.q_all, a.ps_s, a.q_done, a.q_ready, q_bias),
                                          (a.k_all, a.ps_t, a.k_done, a.k_ready, k_bias)):
        for m in range(DC):
            act.wait_ge(done, DC * g + m + 1)
            act.activation(kept[:, m, bass.ds(g * GT, GT)], bank[:, m, 0:GT], ACT.Identity,
                           bias=0.0 if bias is None else bias[:, m:m + 1]).then_inc(ready, 1)



def gated_attention(nc, shared, dram):
    hidden, ident, ident16, minus_half = (shared[k] for k in ("hidden", "ident", "ident16", "minus_half"))
    TEMPERATURE, OUT_SCALE, EPS, EPS2 = 0.1, 0.1, 1e-5, 1e-6
    with Scope(nc, "gattn") as s:
        n = Norm(s)
        a = Attention(s, HEADS, True, 1.0 / (math.sqrt(HD) * TEMPERATURE))
        spread2 = s.sb("spread2", [P, 3, B])
        w_qkv = s.sb("w_qkv", [P, DC, 3 * D + 1])
        w_out = s.sb("w_out", [P, DC, D])
        ln = s.sb("ln", [P, 2, DC])
        qk_bias = s.sb("qk_bias", [P, 2, DC])
        v_bias = s.sb("v_bias", [P, D])
        o_bias = s.sb("o_bias", [P, D])
        b_ent = s.sb("b_ent", [P, 1])
        gate = s.sb("gate", [P, 3, GU])
        summed = s.sb("summed", [P, D])
        w_loaded, spread2_ready, rooted2, gate_in, gate_exp = (
            s.sem(k) for k in ("w_loaded", "spread2_ready", "rooted2", "gate_in", "gate_exp"))
        a.v_gated = s.sem("v_gated")
        LOADS = 9
        with nc.Block() as block:
            @block.sync
            def _(sync):
                sync.dma_start(w_qkv[:, :, 0:3 * D], dram["L0_attn_w_qkv"].rearrange("(c p) n -> p c n", p=P)
                               ).then_inc(w_loaded, 16)
                for c in range(DC):
                    sync.dma_start(w_qkv[:, c, 3 * D:], dram["L0_attn_w_ent"][c * P:(c + 1) * P, :]).then_inc(w_loaded, 16)
                sync.dma_start(w_out[:, :, :], dram["L0_attn_w_out"].rearrange("(c p) n -> p c n", p=P)
                               ).then_inc(w_loaded, 16)
                sync.dma_start(ln[:, 0, :], dram["L0_attn_ln_g_col"]).then_inc(w_loaded, 16)
                sync.dma_start(ln[:, 1, :], dram["L0_attn_ln_b_col"]).then_inc(w_loaded, 16)
                sync.dma_start(qk_bias[:, :, :], dram["L0_attn_b_qkv_col"][:, 0:4].rearrange("p (a c) -> p a c", a=2)
                               ).then_inc(w_loaded, 16)
                load_rows(sync, v_bias[0:T, :], dram["L0_attn_b_qkv"][2 * D:3 * D], w_loaded)
                load_rows(sync, o_bias[0:T, :], dram["L0_attn_b_out"], w_loaded)
                load_rows(sync, b_ent[0:T, :], dram["L0_attn_b_ent"], w_loaded)

            @block.gpsimd
            def _(pool):
                attention_constants_pool(pool, a)
                norm_root_pool(pool, n, minus_half)
                pool.wait_ge(spread2_ready, 1)
                pool.tensor_tensor(spread2[0:T, 2, :], spread2[0:T, 1, :], minus_half[0:T, :], ALU.pow).then_inc(rooted2, 1)
                attention_pool(pool, a)

            @block.scalar
            def _(act):
                act.wait_ge(w_loaded, 16 * (LOADS + 1))
                act.wait_ge(a.step, 1)
                with act.Fori(0, G) as g:
                    act.wait_ge(a.v_done, GU * g)
                    norm_group_act(act, n, g, a.ps_o, scale=ln[:, 0, :], shift=ln[:, 1, :])
                    queries_keys_act(act, a, g, qk_bias[:, 0, :], qk_bias[:, 1, :])
                    act.wait_ge(gate_in, g + 1)
                    act.activation(gate[0:T, 1, :], gate[0:T, 0, :], ACT.Exp, scale=-1.0).then_inc(gate_exp, 1)
                attention_act(act, a)

            @block.tensor
            def _(pe):
                pe.wait_ge(w_loaded, 16 * (LOADS + 1))
                pe.wait_ge(a.const_ready, attention_constants_ready(a))
                with pe.Fori(0, G) as g:
                    pe.wait_ge(n.xT_ready, 2 * g)
                    norm_group_pe(pe, n, g, a.ps_o, ident)
                    project_group_pe(pe, a, n, g, w_qkv, D + 1)
                attention_pe(pe, a, ident, ident16, w_out)

            @block.vector
            def _(dve):
                attention_constants_dve(dve, a, ident)
                norm_statistics_dve(dve, n, hidden, EPS)
                steps = Chain(dve, n.step, 6)
                var, scaled_var = spread2[0:T, 0, :], spread2[0:T, 1, :]
                steps.link(dve.tensor_tensor(var, n.stat[0:T, :, 2], n.stat[0:T, :, 5], ALU.add))
                steps.link(dve.tensor_scalar(var, var, 1.0 / D, None, ALU.mult))
                steps.link(dve.scalar_tensor_tensor(var, n.tmp[0:T, 3, :], 0.25, var, ALU.mult, ALU.add))
                steps.link(dve.tensor_tensor(var, var, n.rstd[0:T, :], ALU.mult))
                steps.link(dve.tensor_tensor(var, var, n.rstd[0:T, :], ALU.mult))
                dve.tensor_scalar(scaled_var, var, 1.0, EPS2, ALU.mult, ALU.add).then_inc(spread2_ready, 1)
                dve.wait_ge(rooted2, 1)
                steps.link(dve.tensor_tensor(n.rstd[0:T, :], n.rstd[0:T, :], spread2[0:T, 2, :], ALU.mult))
                dve.wait_ge(w_loaded, 16 * (LOADS + 1))
                dve.wait_ge(a.const_ready, 4)
                dve.wait_ge(a.step, 1)
                steps = GroupSteps(dve, a.step, 1, 7)
                with dve.Fori(0, G) as g:
                    steps.begin(g)
                    norm_group_dve(dve, n, g, hidden)
                    for u in range(GU):
                        dve.wait_ge(a.v_done, GU * g + u + 1)
                        steps.link(dve.tensor_tensor(gate[0:T, 0, u:u + 1], a.ps_g[0:T, u % 2, D:D + 1], b_ent[0:T, :],
                                                     ALU.add))
                        dve.tensor_tensor(a.v[0:T, GU * g + u, :, 0:HD],
                                          a.ps_g[0:T, u % 2, 0:D].rearrange("p (h e) -> p h e", h=HEADS),
                                          v_bias[0:T, :].rearrange("p (h e) -> p h e", h=HEADS),
                                          ALU.add).then_inc(a.v_ready, 1)
                    dve.sem_inc(gate_in, 1)
                    dve.wait_ge(gate_exp, g + 1)
                    steps.link(dve.tensor_scalar(gate[0:T, 1, :], gate[0:T, 1, :], 1.0, None, ALU.add))
                    steps.link(dve.reciprocal(gate[0:T, 2, :], gate[0:T, 1, :]))
                    steps.link(dve.tensor_scalar(gate[0:T, 2, :], gate[0:T, 2, :], 0.1, 2.0, ALU.max, ALU.min))
                    dve.wait_ge(a.v_ready, GU * g + GU)
                    for u in range(GU):
                        dve.tensor_scalar(a.v[0:T, GU * g + u, :, 0:HD], a.v[0:T, GU * g + u, :, 0:HD], gate[0:T, 2, u:u + 1],
                                          None, ALU.mult).then_inc(a.v_gated, 1)
                    steps.end()
                steps = GroupSteps(dve, a.step, 1 + 7 * G, 2)

                def context(b, buf):
                    outputs = a.ps_o[0:T, buf, 0:HEADS * (HD + 1)].rearrange("p (h e) -> p h e", h=HEADS)
                    steps.link(dve.reciprocal(a.rden[0:T, 0, :], outputs[:, :, HD]))
                    steps.link(dve.tensor_tensor(a.ctx[0:T, buf, :].rearrange("p (h e) -> p h e", h=HEADS),
                                                 outputs[:, :, 0:HD],
                                                 a.rden[0:T, 0, :].unsqueeze(2).broadcast_to([T, HEADS, HD]), ALU.mult))
                    dve.sem_inc(a.ctx_ready, 1)
                    dve.sem_inc(a.outputs_read, 1)

                def add(b):
                    dve.wait_ge(a.out_done, b + 1)
                    dve.tensor_tensor(summed[0:T, :], a.ps_g[0:T, 0, 0:D], o_bias[0:T, :], ALU.add).then_inc(a.biased, 1)
                    dve.wait_ge(a.biased, b + 1)
                    dve.scalar_tensor_tensor(hidden[0:T, b, :], summed[0:T, :], OUT_SCALE, hidden[0:T, b, :], ALU.mult,
                                             ALU.add).then_inc(a.added, 1)

                attention_dve(dve, a, steps, context, add)





def quantised_linear(nc, shared, dram):
    hidden, ident, ident16, minus_half = (shared[k] for k in ("hidden", "ident", "ident16", "minus_half"))
    TE = T + 1
    with Scope(nc, "quant") as s:
        n = Norm(s)
        x1 = s.sb("x1", [P, B, D])
        w_int = s.sb("w_int", [P, DC, D // 4], mybir.dt.int32)
        w = s.sb("w", [P, DC, D], BF16)
        w_scale = s.sb("w_scale", [P, D])
        bias = s.sb("bias", [P, D])
        largest = s.sb("largest", [P, B])
        most = s.sb("most", [P, 2])
        x_scale = s.sb("x_scale", [P, 2])
        xs = s.sb("xs", [P, 2, D])
        xq = s.sb("xq", [P, 2, D], BF16)
        xqT = s.sb("xqT", [P, 2, DC * TE], BF16)
        scaled = s.sb("scaled", [P, 2, D])
        ps_t = s.ps("turned", [P, 2, 512])
        ps_y = s.ps("product", [P, 2, 512])
        w_loaded, w_ready, x1_ready, found, most_ready, step, rounded, xq_turned, xqT_ready, multiplied, added = (
            s.sem(k) for k in ("w_loaded", "w_ready", "x1_ready", "found", "most_ready", "step", "rounded", "xq_turned",
                               "xqT_ready", "multiplied", "added"))
        with nc.Block() as block:
            @block.sync
            def _(sync):
                sync.dma_start(w_int[:, :, :], dram["L0_ffn_weight_int8"].rearrange("(c p) n -> p c n", p=P)
                               ).then_inc(w_loaded, 16)
                load_rows(sync, w_scale[0:T, :], dram["L0_ffn_weight_scale"].rearrange("n a -> (n a)"), w_loaded)
                load_rows(sync, bias[0:T, :], dram["L0_ffn_bias"], w_loaded)

            @block.gpsimd
            def _(pool):
                pool.memset(most[:, :], 0.0).then_inc(most_ready, 1)
                norm_root_pool(pool, n, minus_half)
                pool.wait_ge(found, 1)
                pool.partition_all_reduce(most[:, 1:2], most[:, 0:1], P, bass.bass_isa.ReduceOp.max).then_inc(most_ready, 1)

            @block.scalar
            def _(act):
                with act.Fori(0, B // 2) as i:
                    for j in range(2):
                        act.wait_ge(xq_turned, 2 * i + j + 1)
                        act.wait_ge(multiplied, 2 * i)
                        act.activation(xqT[:, j, :], ps_t[:, j, :].bitcast(BF16)[:, 0:DC * TE],
                                       ACT.Copy).then_inc(xqT_ready, 1)

            @block.tensor
            def _(pe):
                pe.wait_ge(w_ready, 1)
                with pe.Fori(0, B // 2) as i:
                    for j in range(2):
                        pe.wait_ge(rounded, 2 * i + j + 1)
                        pe.wait_ge(xqT_ready, 2 * i)
                        for c in range(DC):
                            mm = pe.transpose(ps_t[:, j, :].bitcast(BF16)[:, c * TE:c * TE + T],
                                              xq[0:T, j, c * P:(c + 1) * P], ident16[0:T, 0:T])
                        mm.then_inc(xq_turned, 1)
                    for j in range(2):
                        pe.wait_ge(xqT_ready, 2 * i + j + 1)
                        pe.wait_ge(added, 2 * i)
                        for c in range(DC):
                            mm = pe.matmul(ps_y[0:T, j, 0:D], xqT[:, j, c * TE:c * TE + T], w[:, c, :],
                                           start=(c == 0), stop=(c == DC - 1))
                        mm.then_inc(multiplied, 1)

            @block.vector
            def _(dve):
                norm_statistics_dve(dve, n, hidden, 1e-5)
                with dve.Fori(0, B) as b:
                    dve.tensor_scalar(x1[0:T, b, :], hidden[0:T, b, :], n.mean[0:T, bass.ds(b, 1)],
                                      n.rstd[0:T, bass.ds(b, 1)], ALU.subtract, ALU.mult).then_inc(x1_ready, 1)
                    dve.wait_ge(x1_ready, b + 1)
                    dve.tensor_reduce(largest[0:T, bass.ds(b, 1)], x1[0:T, b, :], AX.X, ALU.max,
                                      apply_absolute_value=True).then_inc(step, 1)
                dve.wait_ge(w_loaded, 48)
                for c in range(DC):
                    ins = dve.tensor_copy(w[:, c, :], w_int[:, c, :].bitcast(I8))
                ins.then_inc(w_ready, 1)
                dve.wait_ge(step, B)
                dve.wait_ge(most_ready, 1)
                dve.tensor_reduce(most[0:T, 0:1], largest[0:T, :], AX.X, ALU.max).then_inc(found, 1)
                dve.wait_ge(most_ready, 2)
                steps = Chain(dve, step, B)
                steps.link(dve.tensor_scalar(x_scale[:, 0:1], most[:, 1:2], 1.0 / 127.0, 1e-5, ALU.mult, ALU.max))
                steps.link(dve.reciprocal(x_scale[:, 1:2], x_scale[:, 0:1]))
                steps = GroupSteps(dve, step, B + 2, 8)
                with dve.Fori(0, B // 2) as i:
                    steps.begin(i)
                    dve.wait_ge(xq_turned, 2 * i)
                    for j in range(2):
                        x = xs[0:T, j, :]
                        steps.link(dve.tensor_scalar(x, x1[0:T, 2 * i + j, :], x_scale[0:T, 1:2], -128.0, ALU.mult, ALU.max))
                        steps.link(dve.tensor_scalar(x, x, 127.0, ROUND, ALU.min, ALU.add))
                        dve.tensor_scalar(xq[0:T, j, :], x, ROUND, None, ALU.subtract).then_inc(rounded, 1)
                    for j in range(2):
                        y = scaled[0:T, j, :]
                        dve.wait_ge(multiplied, 2 * i + j + 1)
                        steps.link(dve.scalar_tensor_tensor(y, ps_y[0:T, j, 0:D], x_scale[0:T, 0:1], w_scale[0:T, :],
                                                            ALU.mult, ALU.mult))
                        steps.link(dve.tensor_tensor(y, y, bias[0:T, :], ALU.add))
                        dve.tensor_tensor(hidden[0:T, 2 * i + j, :], hidden[0:T, 2 * i + j, :], y,
                                          ALU.add).then_inc(added, 1)
                    steps.end()



def frequency_linear(nc, shared, dram):
    hidden, ident, minus_half = (shared[k] for k in ("hidden", "ident", "minus_half"))
    with Scope(nc, "freq") as s:
        n = Norm(s)
        dft = s.sb("dft", [P, 2, DC, D])
        minus_sin = s.sb("minus_sin", [P, DC, D])
        back = s.sb("back", [P, 2, DC, D])
        w_freq = s.sb("w_freq", [P, 2, DC, D])
        folded = s.sb("folded", [P, 2, DC, D])
        m = s.sb("m", [P, DC, D])
        bias = s.sb("bias", [P, D])
        summed = s.sb("summed", [P, 2, D])
        ps_t = s.ps("turned", [P, 2, 512])
        ps_y = s.ps("product", [P, 2, 512])
        w_loaded, prepared, fold_done, fold_ready, y_done, step, added = (
            s.sem(k) for k in ("w_loaded", "prepared", "fold_done", "fold_ready", "y_done", "step", "added"))
        with nc.Block() as block:
            @block.sync
            def _(sync):
                for k in range(2):
                    sync.dma_start(dft[:, k, :, :], dram["dft"][k].rearrange("(c p) n -> p c n", p=P)).then_inc(w_loaded, 16)
                for k, name in enumerate(("L1_ffn_w_freq_real", "L1_ffn_w_freq_imag")):
                    sync.dma_start(w_freq[:, k, :, :], dram[name].rearrange("(c p) n -> p c n", p=P)).then_inc(w_loaded, 16)
                load_rows(sync, bias[0:T, :], dram["L1_ffn_bias"], w_loaded)

            @block.gpsimd
            def _(pool):
                norm_root_pool(pool, n, minus_half)

            @block.scalar
            def _(act):
                act.wait_ge(w_loaded, 80)
                act.activation(minus_sin[:, :, :], dft[:, 1, :, :], ACT.Copy, scale=-1.0).then_inc(prepared, 1)
                act.activation(back[:, 0, :, :], dft[:, 0, :, :], ACT.Copy, scale=1.0 / D).then_inc(prepared, 1)
                act.activation(back[:, 1, :, :], dft[:, 1, :, :], ACT.Copy, scale=-1.0 / D).then_inc(prepared, 1)
                for k in range(4):
                    act.wait_ge(fold_done, k + 1)
                    act.activation(folded[:, k // 2, k % 2, :], ps_y[:, k % 2, 0:D], ACT.Copy).then_inc(fold_ready, 1)
                for k in range(2):
                    act.wait_ge(fold_done, 5 + k)
                    act.activation(m[:, k, :], ps_y[:, k, 0:D], ACT.Copy).then_inc(fold_ready, 1)
                with act.Fori(0, G) as g:
                    act.wait_ge(y_done, GU * g)
                    norm_group_act(act, n, g, ps_t)

            @block.tensor
            def _(pe):
                pe.wait_ge(w_loaded, 80)
                pe.wait_ge(prepared, 3)
                for k, terms in enumerate((((0, dft[:, 0]), (1, dft[:, 1])), ((1, dft[:, 0]), (0, minus_sin)))):
                    for row in range(DC):
                        if k:
                            pe.wait_ge(fold_ready, row + 1)
                        for t, (part, right) in enumerate(terms):
                            for c in range(DC):
                                mm = pe.matmul(ps_y[:, row, 0:D], w_freq[:, part, c, row * P:(row + 1) * P], right[:, c, :],
                                               start=(t == 0 and c == 0), stop=(t == 1 and c == DC - 1))
                        mm.then_inc(fold_done, 1)
                pe.wait_ge(fold_ready, 4)
                for row in range(DC):
                    for t in range(2):
                        for c in range(DC):
                            mm = pe.matmul(ps_y[:, row, 0:D], folded[:, t, c, row * P:(row + 1) * P], back[:, t, c, :],
                                           start=(t == 0 and c == 0), stop=(t == 1 and c == DC - 1))
                    mm.then_inc(fold_done, 1)
                pe.wait_ge(fold_ready, 6)
                with pe.Fori(0, G) as g:
                    pe.wait_ge(n.xT_ready, 2 * g)
                    norm_group_pe(pe, n, g, ps_t, ident)
                    pe.wait_ge(n.xT_ready, 2 * g + 2)
                    for u in range(GU):
                        if u < 2:
                            pe.wait_ge(added, GU * g)
                        else:
                            pe.wait_ge(added, GU * g + u - 1)
                        for c in range(DC):
                            mm = pe.matmul(ps_y[0:T, u % 2, 0:D], n.xT[:, c, u * T:(u + 1) * T], m[:, c, :],
                                           start=(c == 0), stop=(c == DC - 1))
                        mm.then_inc(y_done, 1)

            @block.vector
            def _(dve):
                norm_statistics_dve(dve, n, hidden, 1e-5)
                dve.wait_ge(w_loaded, 80)
                steps = GroupSteps(dve, step, 0, GU)
                with dve.Fori(0, G) as g:
                    steps.begin(g)
                    norm_group_dve(dve, n, g, hidden)
                    for u in range(GU):
                        dve.wait_ge(y_done, GU * g + u + 1)
                        steps.link(dve.tensor_tensor(summed[0:T, u % 2, :], ps_y[0:T, u % 2, 0:D], bias[0:T, :], ALU.add))
                        dve.tensor_tensor(hidden[0:T, GU * g + u, :], hidden[0:T, GU * g + u, :], summed[0:T, u % 2, :],
                                          ALU.add).then_inc(added, 1)
                    steps.end()



def reshaped_projection(nc, shared, dram):
    hidden, ident, minus_half = (shared[k] for k in ("hidden", "ident", "minus_half"))
    with Scope(nc, "rproj") as s:
        n = Norm(s)
        w_qkv = s.sb("w_qkv", [P, DC, 3 * D])
        bias = s.sb("bias", [P, 3 * D])
        rows = s.sb("rows", [P, 2, 3, D])
        ps_t = s.ps("xturned", [P, 2, 512])
        ps_y = s.ps("product", [P, 2, 2, 512])
        w_loaded, y_done, y_copied = (s.sem(k) for k in ("w_loaded", "y_done", "y_copied"))
        stored = [s.sem(f"stored{j}") for j in range(2)]
        qkv = shared["qkv"]
        with nc.Block() as block:
            @block.sync
            def _(sync):
                sync.dma_start(w_qkv[:, :, :], dram["L1_attn_Wqkv"].rearrange("(c p) n -> p c n", p=P)).then_inc(w_loaded, 16)
                load_rows(sync, bias[0:T, :], dram["L1_attn_bqkv"], w_loaded)
                with sync.Fori(0, B // 2) as i:
                    for j in range(2):
                        sync.wait_ge(y_copied, 4 * i + 2 * j + 2)
                        sync.dma_start(qkv[bass.ds(2 * i + j, 1), :, :, :].rearrange("b a t d -> t (b a) d"),
                                       rows[0:T, j, :, :]).then_inc(stored[j], 16)
                for j in range(2):
                    sync.wait_ge(stored[j], 16 * (B // 2))

            @block.gpsimd
            def _(pool):
                norm_root_pool(pool, n, minus_half)

            @block.scalar
            def _(act):
                with act.Fori(0, G) as g:
                    act.wait_ge(y_done, GU * g)
                    norm_group_act(act, n, g, ps_t)

            @block.tensor
            def _(pe):
                pe.wait_ge(w_loaded, 32)
                with pe.Fori(0, G) as g:
                    pe.wait_ge(n.xT_ready, 2 * g)
                    norm_group_pe(pe, n, g, ps_t, ident)
                    pe.wait_ge(n.xT_ready, 2 * g + 2)
                    for u in range(GU):
                        if u < 2:
                            pe.wait_ge(y_copied, 2 * GU * g)
                        else:
                            pe.wait_ge(y_copied, 2 * (GU * g + u - 1))
                        for bank, (at, size) in enumerate(((0, 2 * D), (2 * D, D))):
                            for c in range(DC):
                                mm = pe.matmul(ps_y[0:T, u % 2, bank, 0:size], n.xT[:, c, u * T:(u + 1) * T],
                                               w_qkv[:, c, at:at + size], start=(c == 0), stop=(c == DC - 1))
                        mm.then_inc(y_done, 1)

            @block.vector
            def _(dve):
                norm_statistics_dve(dve, n, hidden, 1e-5)
                dve.wait_ge(w_loaded, 32)
                with dve.Fori(0, G) as g:
                    norm_group_dve(dve, n, g, hidden)
                    for u in range(GU):
                        dve.wait_ge(y_done, GU * g + u + 1)
                        if u < 2:
                            dve.wait_ge(stored[u], 32 * g)
                        else:
                            dve.wait_ge(stored[u % 2], 32 * g + 16)
                        dve.tensor_tensor(rows[0:T, u % 2, 0:2, :].rearrange("p a d -> p (a d)"), ps_y[0:T, u % 2, 0, 0:2 * D],
                                          bias[0:T, 0:2 * D], ALU.add).then_inc(y_copied, 1)
                        dve.tensor_tensor(rows[0:T, u % 2, 2, :], ps_y[0:T, u % 2, 1, 0:D], bias[0:T, 2 * D:],
                                          ALU.add).then_inc(y_copied, 1)


def reshaped_attention(nc, shared, dram):
    hidden, ident, ident16 = (shared[k] for k in ("hidden", "ident", "ident16"))
    with Scope(nc, "rattn") as s:
        a = Attention(s, HEADS, True, 1.0 / math.sqrt(HD))
        w_out = s.sb("w_out", [P, DC, D])
        o_bias = s.sb("o_bias", [P, D])
        heads = s.sb("heads", [P, 2, GU, 3, D])
        summed = s.sb("summed", [P, D])
        w_loaded = s.sem("w_loaded")
        heads_loaded = [s.sem(f"heads_loaded{j}") for j in range(2)]
        LOADS = 2
        source = shared["qkv"].rearrange("b a t d -> b a (t d)").rearrange("b a (h t e) -> b t a h e", h=HEADS, e=HD)
        with nc.Block() as block:
            @block.sync
            def _(sync):
                sync.dma_start(w_out[:, :, :], dram["L1_attn_Wproj"].rearrange("(c p) n -> p c n", p=P)).then_inc(w_loaded, 16)
                load_rows(sync, o_bias[0:T, :], dram["L1_attn_bproj"], w_loaded)
                with sync.Fori(0, G // 2) as i:
                    for j in range(2):
                        sync.wait_ge(a.v_ready, 2 * GU * i)
                        for u in range(GU):
                            for part in range(3):
                                sync.dma_start(heads[0:T, j, u, part, :].rearrange("p (h e) -> p h e", h=HEADS),
                                               source[bass.ds(2 * GU * i + GU * j + u, 1), :, part, :, :].rearrange(
                                                   "b t h e -> (b t) h e")).then_inc(heads_loaded[j], 16)

            @block.gpsimd
            def _(pool):
                attention_constants_pool(pool, a)
                attention_pool(pool, a)

            @block.scalar
            def _(act):
                with act.Fori(0, G) as g:
                    queries_keys_act(act, a, g, None, None)
                attention_act(act, a)

            @block.tensor
            def _(pe):
                pe.wait_ge(w_loaded, 16 * LOADS)
                pe.wait_ge(a.const_ready, attention_constants_ready(a))
                with pe.Fori(0, G // 2) as i:
                    for j in range(2):
                        g = 2 * i + j
                        pe.wait_ge(heads_loaded[j], 16 * 3 * GU * (i + 1))
                        for what, (bank, done, read) in enumerate(((a.ps_s, a.q_done, a.q_ready), (a.ps_t, a.k_done, a.k_ready))):
                            for m in range(DC):
                                pe.wait_ge(read, DC * g)
                                for u in range(GU):
                                    mm = pe.transpose(bank[:, m, u * T:(u + 1) * T],
                                                      heads[0:T, j, u, what, m * P:(m + 1) * P], ident[0:T, 0:T])
                                mm.then_inc(done, 1)
                attention_pe(pe, a, ident, ident16, w_out)

            @block.vector
            def _(dve):
                attention_constants_dve(dve, a, ident)
                dve.wait_ge(w_loaded, 16 * LOADS)
                dve.wait_ge(a.const_ready, 4)
                dve.wait_ge(a.step, 1)
                with dve.Fori(0, G // 2) as i:
                    for j in range(2):
                        g = 2 * i + j
                        dve.wait_ge(heads_loaded[j], 16 * 3 * GU * (i + 1))
                        dve.wait_ge(a.k_done, 2 * g + 2)
                        for u in range(GU):
                            dve.tensor_copy(a.v[0:T, GU * g + u, :, 0:HD],
                                            heads[0:T, j, u, 2, :].rearrange("p (h e) -> p h e", h=HEADS)).then_inc(a.v_ready, 1)
                steps = GroupSteps(dve, a.step, 1, 2)

                def context(b, buf):
                    outputs = a.ps_o[0:T, buf, 0:HEADS * (HD + 1)].rearrange("p (h e) -> p h e", h=HEADS)
                    steps.link(dve.reciprocal(a.rden[0:T, 0, :], outputs[:, :, HD]))
                    steps.link(dve.tensor_tensor(a.ctx[0:T, buf, :].rearrange("p (h e) -> p h e", h=HEADS),
                                                 outputs[:, :, 0:HD],
                                                 a.rden[0:T, 0, :].unsqueeze(2).broadcast_to([T, HEADS, HD]), ALU.mult))
                    dve.sem_inc(a.ctx_ready, 1)
                    dve.sem_inc(a.outputs_read, 1)

                def add(b):
                    dve.wait_ge(a.out_done, b + 1)
                    dve.tensor_tensor(summed[0:T, :], a.ps_g[0:T, 0, 0:D], o_bias[0:T, :], ALU.add).then_inc(a.biased, 1)
                    dve.wait_ge(a.biased, b + 1)
                    dve.tensor_tensor(hidden[0:T, b, :], hidden[0:T, b, :], summed[0:T, :], ALU.add).then_inc(a.added, 1)

                attention_dve(dve, a, steps, context, add)



def differential_attention(nc, shared, dram):
    hidden, ident, ident16, minus_half = (shared[k] for k in ("hidden", "ident", "ident16", "minus_half"))
    LAMBDA_INIT, EPS = 0.8 - 0.6 * math.exp(0.0), 1e-5
    MAPS = 2 * HEADS
    with Scope(nc, "dattn") as s:
        n = Norm(s)
        a = Attention(s, MAPS, True, 1.0 / (D // MAPS))
        w_qkv = s.sb("w_qkv", [P, DC, 3 * D])
        w_out = s.sb("w_out", [P, DC, D])
        lam = s.sb("lam", [P, 4, 8])
        lam_s = s.sb("lam_s", [P, 6])
        gamma = s.sb("gamma", [P, 2])
        diff = s.sb("diff", [P, 2, D])
        square = s.sb("square", [P, 3, HEADS])
        w_loaded, lam_summed, lam_exp, gamma_ready, ms_ready, rms_ready = (
            s.sem(k) for k in ("w_loaded", "lam_summed", "lam_exp", "gamma_ready", "ms_ready", "rms_ready"))
        LOADS = 6 + P // HD
        with nc.Block() as block:
            @block.sync
            def _(sync):
                sync.dma_start(w_qkv[:, :, :], dram["L2_attn_w_attn"].rearrange("(c p) n -> p c n", p=P)).then_inc(w_loaded, 16)
                sync.dma_start(w_out[:, :, :], dram["L2_attn_w_proj"].rearrange("(c p) n -> p c n", p=P)).then_inc(w_loaded, 16)
                for k, name in enumerate(("q1", "k1", "q2", "k2")):
                    load_rows(sync, lam[0:T, k, :], dram[f"L2_attn_lambda_{name}"], w_loaded)
                for k in range(P // HD):
                    sync.dma_start(gamma[k * HD:(k + 1) * HD, 0:1], dram["L2_attn_gamma"].rearrange("(e a) -> e a", a=1)
                                   ).then_inc(w_loaded, 16)

            @block.gpsimd
            def _(pool):
                attention_constants_pool(pool, a)
                norm_root_pool(pool, n, minus_half)

                def root(b):
                    pool.wait_ge(ms_ready, b + 1)
                    pool.tensor_tensor(square[0:T, 2, :], square[0:T, 1, :], minus_half[0:T, 0:HEADS],
                                       ALU.pow).then_inc(rms_ready, 1)

                attention_pool(pool, a, root)

            @block.scalar
            def _(act):
                act.wait_ge(w_loaded, 16 * LOADS)
                act.activation(gamma[:, 1:2], gamma[:, 0:1], ACT.Copy, scale=1.0 - LAMBDA_INIT).then_inc(gamma_ready, 1)
                act.wait_ge(lam_summed, 2)
                act.activation(lam_s[0:T, 2:4], lam_s[0:T, 0:2], ACT.Exp).then_inc(lam_exp, 1)
                act.wait_ge(gamma_ready, 1)
                act.wait_ge(a.step, 1)
                with act.Fori(0, G) as g:
                    act.wait_ge(a.v_done, GU * g)
                    norm_group_act(act, n, g, a.ps_o)
                    queries_keys_act(act, a, g, None, None)
                attention_act(act, a, ctx_scale=gamma[:, 1:2])

            @block.tensor
            def _(pe):
                pe.wait_ge(w_loaded, 16 * LOADS)
                pe.wait_ge(a.const_ready, attention_constants_ready(a))
                with pe.Fori(0, G) as g:
                    pe.wait_ge(n.xT_ready, 2 * g)
                    norm_group_pe(pe, n, g, a.ps_o, ident)
                    project_group_pe(pe, a, n, g, w_qkv, D)
                attention_pe(pe, a, ident, ident16, w_out)

            @block.vector
            def _(dve):
                attention_constants_dve(dve, a, ident)
                norm_statistics_dve(dve, n, hidden, 1e-5)
                dve.wait_ge(w_loaded, 16 * LOADS)
                dve.wait_ge(a.const_ready, 4)
                dve.wait_ge(a.step, 1)
                steps = Chain(dve, a.step, 1)
                for k in range(2):
                    steps.link(dve.tensor_tensor(lam[0:T, 2 * k, :], lam[0:T, 2 * k, :], lam[0:T, 2 * k + 1, :], ALU.mult))
                    dve.tensor_reduce(lam_s[0:T, k:k + 1], lam[0:T, 2 * k, :], AX.X, ALU.add).then_inc(lam_summed, 1)
                dve.wait_ge(lam_exp, 1)
                steps.link(dve.tensor_tensor(lam_s[0:T, 4:5], lam_s[0:T, 3:4], lam_s[0:T, 2:3], ALU.subtract))
                steps.link(dve.tensor_scalar(lam_s[0:T, 5:6], lam_s[0:T, 4:5], LAMBDA_INIT, None, ALU.subtract))
                minus_lambda = lam_s[0:T, 5:6]
                with dve.Fori(0, G) as g:
                    norm_group_dve(dve, n, g, hidden)
                    for u in range(GU):
                        dve.wait_ge(a.v_done, GU * g + u + 1)
                        dve.tensor_copy(a.v[0:T, GU * g + u, :, 0:HD],
                                        a.ps_g[0:T, u % 2, 0:D].rearrange("p (h e) -> p h e", h=HEADS)).then_inc(a.v_ready, 1)
                steps = GroupSteps(dve, a.step, 5, 6)
                d0, d1 = (diff[0:T, k, :].rearrange("p (h e) -> p h e", h=HEADS) for k in range(2))
                wide = lambda x: x.unsqueeze(2).broadcast_to([T, HEADS, HD])

                def context(b, buf):
                    first, second = (a.ps_o[0:T, k, 0:HEADS * (HD + 1)].rearrange("p (h e) -> p h e", h=HEADS)
                                     for k in range(2))
                    dve.reciprocal(a.rden[0:T, 0, :], first[:, :, HD])
                    steps.link(dve.reciprocal(a.rden[0:T, 1, :], second[:, :, HD]))
                    steps.link(dve.tensor_scalar(a.rden[0:T, 1, :], a.rden[0:T, 1, :], minus_lambda, None, ALU.mult))
                    dve.tensor_tensor(d0, first[:, :, 0:HD], wide(a.rden[0:T, 0, :]), ALU.mult)
                    dve.tensor_tensor(d1, second[:, :, 0:HD], wide(a.rden[0:T, 1, :]), ALU.mult).then_inc(a.outputs_read, 1)
                    dve.wait_ge(a.outputs_read, b + 2)
                    steps.link(dve.tensor_tensor(d0, d0, d1, ALU.add))
                    steps.link(dve.tensor_tensor(d1, d0, d0, ALU.mult))
                    steps.link(dve.tensor_reduce(square[0:T, 0, :], d1, AX.X, ALU.add))
                    steps.link(dve.tensor_scalar(square[0:T, 1, :], square[0:T, 0, :], 1.0 / HD, EPS, ALU.mult, ALU.add))
                    dve.sem_inc(ms_ready, 1)

                def finish(b, buf):
                    dve.wait_ge(rms_ready, b + 1)
                    dve.tensor_tensor(a.ctx[0:T, buf, :].rearrange("p (h e) -> p h e", h=HEADS), d0,
                                      wide(square[0:T, 2, :]), ALU.mult).then_inc(a.ctx_ready, 1)

                def add(b):
                    dve.wait_ge(a.out_done, b + 1)
                    dve.tensor_tensor(hidden[0:T, b, :], a.ps_g[0:T, 0, 0:D], hidden[0:T, b, :], ALU.add).then_inc(a.added, 1)

                attention_dve(dve, a, steps, context, add, finish)


def layer1_attention(nc, shared, dram):
    shared["qkv"] = nc.dram_tensor("qkv_rows", (B, 3, T, D), F32, kind="Internal").ap()
    reshaped_projection(nc, shared, dram)
    reshaped_attention(nc, shared, dram)



def choose_two_dve(dve, s, steps, score, score2d, rows, wide_shape, restart, work, chosen):
    top, hit, rank, first = work["top"], work["hit"], work["rank"], work["first"]
    flat = lambda x: x[rows, :, :].rearrange("p b e -> p (b e)")
    left = score
    for k in range(2):
        steps.link(dve.tensor_reduce(top[rows, :], left[rows, :, :], AX.X, ALU.max))
        steps.link(dve.tensor_tensor(hit[rows, :, :], left[rows, :, :],
                                     top[rows, :].unsqueeze(2).broadcast_to(wide_shape), ALU.is_equal))
        steps.link(dve.tensor_tensor_scan(flat(rank), flat(restart), flat(hit), 0.0, ALU.mult, ALU.add))
        steps.link(dve.scalar_tensor_tensor(first[k][rows, :, :], rank[rows, :, :], 1.0, hit[rows, :, :],
                                            ALU.is_equal, ALU.mult))
        if k == 0:
            steps.link(dve.scalar_tensor_tensor(work["left"][rows, :, :], first[0][rows, :, :], MASKED,
                                                left[rows, :, :], ALU.mult, ALU.add))
            left = work["left"]
    steps.link(dve.tensor_tensor(chosen[rows, :, :], first[0][rows, :, :], first[1][rows, :, :], ALU.add))


def choice_buffers(s, sets, experts):
    work = {k: s.sb(f"choice_{k}", [P, sets, experts]) for k in ("hit", "rank", "left", "first0", "first1")}
    work["first"] = [work["first0"], work["first1"]]
    work["top"] = s.sb("choice_top", [P, sets])
    return work



def split_products(pe, out, w, x, start, stop):
    (w_high, w_low), (x_high, x_low) = w, x
    pe.matmul(out, w_high, x_high, start=start, stop=False)
    pe.matmul(out, w_high, x_low, start=False, stop=False)
    return pe.matmul(out, w_low, x_high, start=False, stop=stop)


def mixture(nc, shared, dram):
    hidden, ident, minus_half = (shared[k] for k in ("hidden", "ident", "minus_half"))
    E, F = 8, 1024
    FC = F // P
    PAIRS = FC // 2
    with Scope(nc, "moe") as s:
        n = Norm(s)
        x_part = [s.sb(f"x_part{k}", [P, DC, B * T], BF16) for k in range(2)]
        w_router = s.sb("w_router", [P, DC, E])
        w1_in = s.sb("w1_in", [P, DC, F])
        w2_in = s.sb("w2_in", [P, FC, D])
        w1 = [s.sb(f"w1_part{k}", [P, 2, DC, F], BF16) for k in range(2)]
        w2 = [s.sb(f"w2_part{k}", [P, 2, FC, D], BF16) for k in range(2)]
        gelu = s.sb("gelu", [P, 2, 2, GT])
        act1 = [s.sb(f"act1_part{k}", [P, FC, GT], BF16) for k in range(2)]
        token_weight = s.sb("token_weight", [P, 2, GT])
        weighted = s.sb("weighted", [P, DC, GT])
        total_out = s.sb("total_out", [P, DC, B * T])
        logits = s.sb("logits", [P, B, E])
        prob = s.sb("prob", [P, B, E])
        chosen = s.sb("chosen", [P, B, E])
        weight = s.sb("weight", [P, B, E])
        weightT = s.sb("weightT", [P, 2, T])
        restart = s.sb("restart", [P, B, E])
        one = s.sb("one", [P, 1])
        total = s.sb("total", [P, 2, B])
        work = choice_buffers(s, B, E)
        ps_h = s.ps("hidden", [P, 4, 512])
        ps_y = s.ps("product", [P, 4, 512])
        names = ("router_loaded restart_ready x_high_ready x_low_ready routed logits_ready step prob_in prob_exp weight_ready "
                 "weight_turned weightT_ready weight_stored w_loaded w_split expert_ready h_done high_ready low_ready y_done y_read "
                 "summed_up expert_used outT_ready out_turned out_added").split()
        sem = {k: s.sem(k) for k in names}
        (router_loaded, restart_ready, x_high_ready, x_low_ready, routed, logits_ready, step, prob_in, prob_exp, weight_ready,
         weight_turned, weightT_ready, weight_stored, w_loaded, w_split, expert_ready, h_done, high_ready, low_ready, y_done, y_read,
         summed_up, expert_used, outT_ready, out_turned, out_added) = (sem[k] for k in names)
        token_weight_loaded = [s.sem(f"token_weight_loaded{j}") for j in range(2)]
        scratch = nc.dram_tensor("token_weights", (B, E, T), F32, kind="Internal").ap()
        with nc.Block() as block:
            @block.sync
            def _(sync):
                sync.dma_start(w_router[:, :, :], dram["L2_ffn_Wr"].rearrange("(c p) n -> p c n", p=P)).then_inc(router_loaded, 16)
                sync.wait_ge(weightT_ready, 1)
                for k in range(2):
                    sync.dma_start(scratch[k * B // 2:(k + 1) * B // 2, :, :].rearrange("b e t -> (b e) t"),
                                   weightT[:, k, :]).then_inc(weight_stored, 16)
                sync.wait_ge(weight_stored, 32)
                with sync.Fori(0, E) as e:
                    with sync.Fori(0, G // 2) as i:
                        for j in range(2):
                            sync.wait_ge(y_read, e * G + 2 * i + j + 1)
                            sync.dma_start(token_weight[:, j, :].rearrange("p (u t) -> p u t", u=GU),
                                           scratch[bass.ds(2 * GU * i + GU * j, GU), bass.ds(e, 1), :].rearrange(
                                               "b e t -> (b e) t").partition_broadcast(P)).then_inc(token_weight_loaded[j], 16)

            @block.gpsimd
            def _(pool):
                pool.memset(restart[:, :, :], 1.0).then_inc(restart_ready, 1)
                pool.wait_ge(restart_ready, 1)
                pool.memset(restart[:, :, 0:1], 0.0).then_inc(restart_ready, 1)
                norm_root_pool(pool, n, minus_half)
                pool.memset(one[:, :], 1.0).then_inc(restart_ready, 1)
                pool.wait_ge(restart_ready, 3)
                pool.memset(total_out[:, :, :], 0.0).then_inc(summed_up, 1)
                with pool.Fori(0, E // 2) as i:
                    for j in range(2):
                        e = 2 * i + j
                        pool.dma_start(w1_in[:, :, :], dram["L2_ffn_W1"][bass.ds(e, 1), :, :].rearrange(
                            "e (c p) n -> p (e c) n", p=P)).then_inc(w_loaded, 16)
                        pool.dma_start(w2_in[:, :, :], dram["L2_ffn_W2"][bass.ds(e, 1), :, :].rearrange(
                            "e (c p) n -> p (e c) n", p=P)).then_inc(w_loaded, 16)
                        pool.wait_ge(w_loaded, 32 * (e + 1))
                        pool.wait_ge(expert_used, e + 1)
                        for source, parts in ((w1_in, w1), (w2_in, w2)):
                            pool.tensor_tensor(parts[0][:, j, :, :], source[:, :, :],
                                               one[:, :].unsqueeze(2).broadcast_to(source.shape), ALU.mult).then_inc(w_split, 1)
                        pool.wait_ge(w_split, 2 * e + 2)
                        for source, parts in ((w1_in, w1), (w2_in, w2)):
                            pool.tensor_tensor(parts[1][:, j, :, :], source[:, :, :], parts[0][:, j, :, :],
                                               ALU.subtract).then_inc(expert_ready, 1)
                        pool.wait_ge(expert_ready, 2 * e + 2)

            @block.scalar
            def _(act):
                with act.Fori(0, G) as g:
                    act.wait_ge(routed, GU * g)
                    act.wait_ge(x_low_ready, g)
                    norm_group_act(act, n, g, ps_h)
                    act.activation(x_part[0][:, :, bass.ds(g * GT, GT)], ps_h[:, 0:DC, 0:GT], ACT.Copy).then_inc(x_high_ready, 1)
                act.wait_ge(prob_in, 1)
                act.activation(prob[0:T, :, :], logits[0:T, :, :], ACT.Exp).then_inc(prob_exp, 1)
                act.wait_ge(weight_turned, 1)
                act.activation(weightT[:, :, :], ps_y[:, 0:2, 0:T], ACT.Copy).then_inc(weightT_ready, 1)
                with act.Fori(0, E * G) as r:
                    act.wait_ge(y_done, r)
                    for k in range(PAIRS):
                        act.wait_ge(h_done, PAIRS * r + k + 1)
                        act.wait_ge(low_ready, PAIRS * r + k + 1)
                        act.activation(gelu[:, k % 2, :, :], ps_h[:, 2 * (k % 2):2 * (k % 2) + 2, 0:GT], ACT.Gelu)
                        act.activation(act1[0][:, 2 * k:2 * k + 2, :], ps_h[:, 2 * (k % 2):2 * (k % 2) + 2, 0:GT],
                                       ACT.Gelu).then_inc(high_ready, 1)
                act.wait_ge(summed_up, E * G + 1)
                with act.Fori(0, G) as g:
                    act.wait_ge(out_turned, g)
                    act.activation(n.xT[:, :, :], total_out[:, :, bass.ds(g * GT, GT)], ACT.Copy).then_inc(outT_ready, 1)

            @block.tensor
            def _(pe):
                pe.wait_ge(router_loaded, 16)
                with pe.Fori(0, G) as g:
                    pe.wait_ge(x_high_ready, g)
                    norm_group_pe(pe, n, g, ps_h, ident)
                    pe.wait_ge(n.xT_ready, 2 * g + 2)
                    pe.wait_ge(logits_ready, g)
                    for u in range(GU):
                        for c in range(DC):
                            mm = pe.matmul(ps_y[0:T, 0, u * E:(u + 1) * E], n.xT[:, c, u * T:(u + 1) * T], w_router[:, c, :],
                                           start=(c == 0), stop=(c == DC - 1))
                        mm.then_inc(routed, 1)
                pe.wait_ge(weight_ready, 1)
                for k in range(2):
                    mm = pe.transpose(ps_y[:, k, 0:T], weight[0:T, k * B // 2:(k + 1) * B // 2, :].rearrange("p b e -> p (b e)"),
                                      ident[0:T, 0:T])
                mm.then_inc(weight_turned, 1)
                pe.wait_ge(weightT_ready, 1)
                pe.wait_ge(x_low_ready, G)
                with pe.Fori(0, E // 2) as i:
                    for j in range(2):
                        with pe.Fori(0, G // 2) as h:
                            for odd in range(2):
                                g = 2 * h + odd
                                r = (2 * i + j) * G + g
                                pe.wait_ge(expert_ready, 2 * (2 * i + j) + 2)
                                for k in range(PAIRS):
                                    pe.wait_ge(high_ready, PAIRS * r + k + 1)
                                    for f in (2 * k, 2 * k + 1):
                                        for c in range(DC):
                                            mm = split_products(pe, ps_h[:, f % 4, 0:GT],
                                                                [w[:, j, c, f * P:(f + 1) * P] for w in w1],
                                                                [part[:, c, bass.ds(g * GT, GT)] for part in x_part],
                                                                c == 0, c == DC - 1)
                                    mm.then_inc(h_done, 1)
                                pe.wait_ge(y_read, r + 1)
                                for f in range(FC):
                                    if f % 2 == 0:
                                        pe.wait_ge(low_ready, PAIRS * r + f // 2 + 3)
                                    for m in range(DC):
                                        mm = split_products(pe, ps_y[:, 2 * odd + m, 0:GT],
                                                            [w[:, j, f, m * P:(m + 1) * P] for w in w2],
                                                            [part[:, f, :] for part in act1], f == 0, f == FC - 1)
                                mm.then_inc(y_done, 1)
                with pe.Fori(0, G) as g:
                    pe.wait_ge(outT_ready, g + 1)
                    pe.wait_ge(out_added, g)
                    for u in range(GU):
                        for c in range(DC):
                            mm = pe.transpose(ps_h[0:T, u, c * P:(c + 1) * P], n.xT[:, c, u * T:(u + 1) * T], ident[:, :])
                    mm.then_inc(out_turned, 1)

            @block.vector
            def _(dve):
                dve.sem_inc(expert_used, 2)
                dve.sem_inc(high_ready, 2)
                dve.sem_inc(low_ready, 2)
                dve.sem_inc(y_read, 2)
                norm_statistics_dve(dve, n, hidden, 1e-5)
                with dve.Fori(0, G) as g:
                    norm_group_dve(dve, n, g, hidden)
                    dve.wait_ge(x_high_ready, g + 1)
                    dve.tensor_tensor(x_part[1][:, :, bass.ds(g * GT, GT)], n.xT[:, :, :], x_part[0][:, :, bass.ds(g * GT, GT)],
                                      ALU.subtract).then_inc(x_low_ready, 1)
                    dve.wait_ge(routed, GU * g + GU)
                    dve.tensor_copy(logits[0:T, bass.ds(GU * g, GU), :],
                                    ps_y[0:T, 0, 0:GU * E].rearrange("p (u e) -> p u e", e=E)).then_inc(logits_ready, 1)
                dve.wait_ge(logits_ready, G)
                dve.wait_ge(restart_ready, 2)
                rows, wide = slice(0, T), [T, B, E]
                steps = Chain(dve, step)
                steps.link(dve.tensor_reduce(total[rows, 0, :], logits[rows, :, :], AX.X, ALU.max))
                dve.tensor_tensor(logits[rows, :, :], logits[rows, :, :], total[rows, 0, :].unsqueeze(2).broadcast_to(wide),
                                  ALU.subtract).then_inc(prob_in, 1)
                dve.wait_ge(prob_exp, 1)
                steps.link(dve.tensor_reduce(total[rows, 0, :], prob[rows, :, :], AX.X, ALU.add))
                steps.link(dve.reciprocal(total[rows, 1, :], total[rows, 0, :]))
                steps.link(dve.tensor_tensor(prob[rows, :, :], prob[rows, :, :],
                                             total[rows, 1, :].unsqueeze(2).broadcast_to(wide), ALU.mult))
                choose_two_dve(dve, s, steps, prob, None, rows, wide, restart, work, chosen)
                dve.tensor_tensor(weight[rows, :, :], prob[rows, :, :], chosen[rows, :, :], ALU.mult).then_inc(weight_ready, 1)
                dve.wait_ge(summed_up, 1)
                with dve.Fori(0, E) as e:
                    with dve.Fori(0, G // 2) as h:
                        for odd in range(2):
                            r = e * G + 2 * h + odd
                            for k in range(PAIRS):
                                dve.wait_ge(high_ready, PAIRS * r + k + 3)
                                dve.tensor_tensor(act1[1][:, 2 * k:2 * k + 2, :], gelu[:, k % 2, :, :], act1[0][:, 2 * k:2 * k + 2, :],
                                                  ALU.subtract).then_inc(low_ready, 1)
                            dve.wait_ge(token_weight_loaded[odd], 16 * (e * (G // 2) + h + 1))
                            dve.wait_ge(y_done, r + 1)
                            dve.wait_ge(summed_up, r + 1)
                            dve.tensor_tensor(weighted[:, :, :], ps_y[:, 2 * odd:2 * odd + 2, 0:GT],
                                              token_weight[:, odd, :].unsqueeze(1).broadcast_to([P, DC, GT]),
                                              ALU.mult).then_inc(y_read, 1)
                            dve.wait_ge(y_read, r + 3)
                            at = bass.ds((2 * h + odd) * GT, GT)
                            dve.tensor_tensor(total_out[:, :, at], total_out[:, :, at], weighted[:, :, :],
                                              ALU.add).then_inc(summed_up, 1)
                    dve.wait_ge(summed_up, (e + 1) * G + 1)
                    dve.sem_inc(expert_used, 1)
                with dve.Fori(0, G) as g:
                    dve.wait_ge(out_turned, g + 1)
                    dve.tensor_tensor(hidden[0:T, bass.ds(GU * g, GU), :], hidden[0:T, bass.ds(GU * g, GU), :],
                                      ps_h[0:T, :, 0:D], ALU.add).then_inc(out_added, 1)



def state_space(nc, shared, dram):
    hidden, ident, minus_half = (shared[k] for k in ("hidden", "ident", "minus_half"))
    CH, N, TAPS, RANK = 512, 16, 4, 16
    CC = CH // P
    ROWS = RANK + 2 * N
    LN_EPS = 1e-5
    nodes = (np.cos(np.pi * (np.arange(64) + 0.5) / 64) + 1) / 18
    fit = np.polynomial.Chebyshev.fit(nodes, 2 * np.arctanh(np.sqrt(nodes)) / np.sqrt(nodes), 4, domain=[0, 1 / 9])
    ARTANH = [float(x) for x in fit.convert(kind=np.polynomial.Polynomial).coef]
    with Scope(nc, "ssm") as s:
        n = Norm(s)
        w_in = s.sb("w_in", [P, DC, 2 * CH])
        w_x = s.sb("w_x", [P, CC, ROWS])
        w_dt = s.sb("w_dt", [RANK, CH])
        w_out = s.sb("w_out", [P, CC, D])
        taps = s.sb("taps", [P, CC, TAPS])
        cols = s.sb("cols", [P, 3, CC])
        decay = s.sb("decay", [P, CC, N])
        gamma = s.sb("gamma", [P, D])
        beta = s.sb("beta", [P, D])
        x_in = s.sb("x_in", [P, CC, GT])
        conv = s.sb("conv", [P, CC, GT])
        xc = s.sb("xc", [P, CC, GT])
        gate = s.sb("gate", [P, CC, GT])
        dbc = s.sb("dbc", [ROWS, GT])
        pos = s.sb("pos", [P, CC, GT])
        mag = s.sb("mag", [P, CC, GT])
        delta = s.sb("delta", [P, CC, GT])
        du = s.sb("du", [P, CC, GT])
        ratio, square = du, conv
        bc = s.sb("bc", [P, 2, 2, 4, GT])
        dA = s.sb("dA", [P, 2, CC, GU, T])
        dBx = s.sb("dBx", [P, 2, CC, GT])
        state = s.sb("state", [P, 2, CC, GT])
        hC = s.sb("hC", [P, 2, CC, GT])
        yT = s.sb("yT", [P, CC, GT])
        res = s.sb("res", [P, GU, D])
        rstat = s.sb("rstat", [P, GU, 6])
        ragg = s.sb("ragg", [P, 3, GU])
        rroot = s.sb("rroot", [P, 2, GU])
        ps_a = s.ps("wide", [P, 4, 512])
        ps_b = s.ps("small", [P, 2, 512])
        names = ("w_loaded dA_zeroed decay_exp decay_ready xz_done xz_ready conv_ready xc_ready dbc_done dbc_ready dbc_stored "
                 "delta_done relu_ready sp_ready sp_step ratio_ready square_ready delta_ready du_ready dA_ready dbx_ready scanned hc_ready y_acc "
                 "y_taken yT_ready out_done out_read step spread2 rooted2").split()
        sem = {k: s.sem(k) for k in names}
        (w_loaded, dA_zeroed, decay_exp, decay_ready, xz_done, xz_ready, conv_ready, xc_ready, dbc_done, dbc_ready,
         dbc_stored, delta_done, relu_ready, sp_ready, sp_step, ratio_ready, square_ready, delta_ready, du_ready, dA_ready, dbx_ready, scanned,
         hc_ready, y_acc, y_taken, yT_ready, out_done, out_read, step, spread2, rooted2) = (sem[k] for k in names)
        bc_loaded = [s.sem(f"bc_loaded{j}") for j in range(2)]
        scratch = nc.dram_tensor("dbc_rows", (G, ROWS, GT), F32, kind="Internal").ap()
        LOADS = 11
        with nc.Block() as block:
            @block.sync
            def _(sync):
                for tile, name in ((w_in, "L3_attn_W_in"), (w_x, "L3_attn_W_x"), (w_out, "L3_attn_W_out"),
                                   (taps, "L3_attn_conv_w"), (decay, "L3_attn_A_log")):
                    sync.dma_start(tile[:, :, :], dram[name].rearrange("(c p) n -> p c n", p=P)).then_inc(w_loaded, 16)
                sync.dma_start(w_dt[:, :], dram["L3_attn_W_dt"]).then_inc(w_loaded, 16)
                for k, name in enumerate(("conv_b", "b_dt", "D")):
                    sync.dma_start(cols[:, k, :], dram[f"L3_attn_{name}_col"]).then_inc(w_loaded, 16)
                load_rows(sync, gamma[0:T, :], dram["L3_attn_gamma"], w_loaded)
                load_rows(sync, beta[0:T, :], dram["L3_attn_beta"], w_loaded)
                with sync.Fori(0, G) as g:
                    sync.wait_ge(dbc_ready, g + 1)
                    sync.dma_start(scratch[bass.ds(g, 1), :, :].rearrange("g r t -> (g r) t"), dbc[:, :]).then_inc(dbc_stored, 16)
                    sync.wait_ge(dbc_stored, 16 * (g + 1))
                    for q in range(N // 4):
                        sync.wait_ge(hc_ready, N * g + 4 * q + 4)
                        for k in range(2):
                            r = RANK + k * N + 4 * q
                            sync.dma_start(bc[:, q % 2, k, :, :].rearrange("p r t -> p (r t)"),
                                           scratch[bass.ds(g, 1), r:r + 4, :].rearrange("g r t -> (g r t)").partition_broadcast(P)
                                           ).then_inc(bc_loaded[q % 2], 16)

            @block.gpsimd
            def _(pool):
                pool.memset(dA[:, :, :, :, :], 0.0).then_inc(dA_zeroed, 1)
                norm_root_pool(pool, n, minus_half)
                with pool.Fori(0, G) as g:
                    pool.wait_ge(sp_ready, g + 1)
                    pool.tensor_tensor(delta[:, :, :], pos[:, :, :], mag[:, :, :], ALU.add).then_inc(delta_ready, 1)
                    pool.wait_ge(delta_ready, g + 1)
                    pool.tensor_tensor(du[:, :, :], delta[:, :, :], xc[:, :, :], ALU.mult).then_inc(du_ready, 1)
                    pool.wait_ge(du_ready, g + 1)
                    for k in range(N):
                        q = k // 4
                        pool.wait_ge(bc_loaded[q % 2], 64 * g + 32 * (q // 2 + 1))
                        pool.wait_ge(scanned, N * g + k + 1)
                        pool.tensor_tensor(dBx[:, k % 2, :, :], du[:, :, :],
                                           bc[:, q % 2, 0, k % 4, :].unsqueeze(1).broadcast_to([P, CC, GT]),
                                           ALU.mult).then_inc(dbx_ready, 1)
                    pool.wait_ge(spread2, g + 1)
                    pool.tensor_tensor(rroot[0:T, 1, :], rroot[0:T, 0, :], minus_half[0:T, 0:GU], ALU.pow).then_inc(rooted2, 1)

            @block.scalar
            def _(act):
                act.wait_ge(w_loaded, 16 * LOADS)
                act.activation(decay[:, :, :], decay[:, :, :], ACT.Exp).then_inc(decay_exp, 1)
                act.wait_ge(decay_ready, 1)
                act.wait_ge(dA_zeroed, 1)
                with act.Fori(0, G) as g:
                    act.wait_ge(xz_done, 8 * g)
                    norm_group_act(act, n, g, ps_b)
                    for m in range(2 * CC):
                        act.wait_ge(xz_done, 8 * g + m + 1)
                        if m == 0:
                            act.wait_ge(yT_ready, g)
                        act.activation((x_in if m < CC else gate)[:, m % CC, :], ps_a[:, m % 4, 0:GT],
                                       ACT.Copy if m < CC else ACT.Silu).then_inc(xz_ready, 1)
                    for c in range(CC):
                        act.wait_ge(conv_ready, CC * g + c + 1)
                        act.activation(xc[:, c, :], conv[:, c, :], ACT.Silu).then_inc(xc_ready, 1)
                    act.wait_ge(dbc_done, g + 1)
                    act.wait_ge(dbc_stored, 16 * g)
                    act.activation(dbc[:, :], ps_b[0:ROWS, 0, 0:GT], ACT.Copy).then_inc(dbc_ready, 1)
                    act.wait_ge(delta_ready, g)
                    for c in range(CC):
                        act.wait_ge(delta_done, CC * g + c + 1)
                        act.activation(mag[:, c, :], ps_a[:, c, 0:GT], ACT.Abs, bias=cols[:, 1, c:c + 1]).then_inc(sp_step, 1)
                        act.activation(pos[:, c, :], ps_a[:, c, 0:GT], ACT.Relu, bias=cols[:, 1, c:c + 1]).then_inc(relu_ready, 1)
                    act.wait_ge(sp_step, 5 * g + 4)
                    act.wait_ge(relu_ready, 4 * g + 4)
                    act.activation(mag[:, :, :], mag[:, :, :], ACT.Exp, scale=-1.0).then_inc(sp_step, 1)
                    act.wait_ge(ratio_ready, g + 1)
                    act.activation(square[:, :, :], ratio[:, :, :], ACT.Square).then_inc(square_ready, 1)
                    act.wait_ge(delta_ready, g + 1)
                    for k in range(N):
                        act.wait_ge(scanned, N * g + k + 1)
                        for c in range(CC):
                            ins = act.activation(dA[:, k % 2, c, :, 1:],
                                                 delta[:, c, :].rearrange("p (u t) -> p u t", u=GU)[:, :, 1:], ACT.Exp,
                                                 scale=decay[:, c, k:k + 1])
                        ins.then_inc(dA_ready, 1)

            @block.tensor
            def _(pe):
                pe.wait_ge(w_loaded, 16 * LOADS)
                with pe.Fori(0, G) as g:
                    pe.wait_ge(out_read, GU * g)
                    norm_group_pe(pe, n, g, ps_b, ident)
                    pe.wait_ge(n.xT_ready, 2 * g + 2)
                    for m in range(2 * CC):
                        if m < 4:
                            pe.wait_ge(y_taken, CC * g)
                        else:
                            pe.wait_ge(xz_ready, 8 * g + m - 3)
                        for c in range(DC):
                            mm = pe.matmul(ps_a[:, m % 4, 0:GT], w_in[:, c, m * P:(m + 1) * P], n.xT[:, c, :],
                                           start=(c == 0), stop=(c == DC - 1))
                        mm.then_inc(xz_done, 1)
                    for c in range(CC):
                        pe.wait_ge(xc_ready, CC * g + c + 1)
                        mm = pe.matmul(ps_b[0:ROWS, 0, 0:GT], w_x[:, c, :], xc[:, c, :], start=(c == 0), stop=(c == CC - 1))
                    mm.then_inc(dbc_done, 1)
                    pe.wait_ge(xz_ready, 8 * g + 8)
                    pe.wait_ge(dbc_ready, g + 1)
                    for c in range(CC):
                        pe.matmul(ps_a[:, c, 0:GT], w_dt[:, c * P:(c + 1) * P], dbc[0:RANK, :], start=True,
                                  stop=True).then_inc(delta_done, 1)
                    pe.wait_ge(relu_ready, CC * g + CC)
                    for k in range(N):
                        pe.wait_ge(hc_ready, 8 + N * g + k + 1)
                        for c in range(CC):
                            mm = pe.matmul(ps_a[:, c, 0:GT], ident[:, :], hC[:, k % 2, c, :], start=(k == 0),
                                           stop=(k == N - 1))
                        mm.then_inc(y_acc, 1)
                    pe.wait_ge(yT_ready, g + 1)
                    for u in range(GU):
                        if u >= 2:
                            pe.wait_ge(out_read, GU * g + u - 1)
                        for c in range(CC):
                            mm = pe.matmul(ps_b[0:T, u % 2, 0:D], yT[:, c, u * T:(u + 1) * T], w_out[:, c, :],
                                           start=(c == 0), stop=(c == CC - 1))
                        mm.then_inc(out_done, 1)

            @block.vector
            def _(dve):
                dve.sem_inc(scanned, 2)
                dve.sem_inc(y_acc, 2)
                dve.sem_inc(hc_ready, 8)
                norm_statistics_dve(dve, n, hidden, 1e-5)
                dve.wait_ge(w_loaded, 16 * LOADS)
                dve.wait_ge(decay_exp, 1)
                dve.tensor_scalar(decay[:, :, :], decay[:, :, :], -1.0, None, ALU.mult).then_inc(decay_ready, 1)
                steps = GroupSteps(dve, step, 0, 3 * CC + 2 * GU + 15)
                by_utterance = lambda x: x.rearrange("p (u t) -> p u t", u=GU)
                with dve.Fori(0, G) as g:
                    steps.begin(g)
                    norm_group_dve(dve, n, g, hidden)
                    for c in range(CC):
                        dve.wait_ge(xz_ready, 8 * g + c + 1)
                        if c == 0:
                            dve.wait_ge(xc_ready, CC * g)
                        steps.link(dve.tensor_scalar(conv[:, c, :], x_in[:, c, :], taps[:, c, TAPS - 1:TAPS], cols[:, 0, c:c + 1],
                                                     ALU.mult, ALU.add))
                        for back in range(1, TAPS):
                            to = by_utterance(conv[:, c, :])[:, :, back:]
                            ins = dve.scalar_tensor_tensor(to, by_utterance(x_in[:, c, :])[:, :, 0:T - back],
                                                           taps[:, c, TAPS - 1 - back:TAPS - back], to, ALU.mult, ALU.add)
                            if back < TAPS - 1:
                                steps.link(ins)
                            else:
                                ins.then_inc(conv_ready, 1)
                    dve.wait_ge(sp_step, 5 * g + 5)
                    dve.wait_ge(dbx_ready, N * g)
                    steps.link(dve.tensor_scalar(ratio[:, :, :], mag[:, :, :], 2.0, None, ALU.add))
                    steps.link(dve.reciprocal(ratio[:, :, :], ratio[:, :, :]))
                    dve.tensor_tensor(ratio[:, :, :], mag[:, :, :], ratio[:, :, :], ALU.mult).then_inc(ratio_ready, 1)
                    dve.wait_ge(square_ready, g + 1)
                    steps.link(dve.tensor_scalar(mag[:, :, :], square[:, :, :], ARTANH[-1], None, ALU.mult))
                    flat = lambda x: x[:, :, :].rearrange("p c t -> p (c t)")
                    for coefficient in ARTANH[-2:0:-1]:
                        steps.link(dve.scalar_tensor_tensor(flat(mag), flat(mag), coefficient, flat(square), ALU.add, ALU.mult))
                    dve.scalar_tensor_tensor(flat(mag), flat(mag), ARTANH[0], flat(ratio), ALU.add, ALU.mult).then_inc(sp_ready, 1)
                    for k in range(N):
                        q = k // 4
                        dve.wait_ge(dA_ready, N * g + k + 1)
                        dve.wait_ge(dbx_ready, N * g + k + 1)
                        dve.wait_ge(hc_ready, 7 + N * g + k)
                        dve.tensor_tensor_scan(state[:, k % 2, :, :].rearrange("p c t -> p (c t)"),
                                               dA[:, k % 2, :, :, :].rearrange("p c u t -> p (c u t)"),
                                               dBx[:, k % 2, :, :].rearrange("p c t -> p (c t)"), 0.0, ALU.mult,
                                               ALU.add).then_inc(scanned, 1)
                        dve.wait_ge(scanned, 2 + N * g + k + 1)
                        dve.wait_ge(y_acc, N * g + k + 1)
                        dve.tensor_tensor(hC[:, k % 2, :, :], state[:, k % 2, :, :],
                                          bc[:, q % 2, 1, k % 4, :].unsqueeze(1).broadcast_to([P, CC, GT]),
                                          ALU.mult).then_inc(hc_ready, 1)
                    dve.wait_ge(y_acc, 2 + N * g + N)
                    dve.wait_ge(hc_ready, 8 + N * g + N)
                    for c in range(CC):
                        dve.scalar_tensor_tensor(yT[:, c, :], xc[:, c, :], cols[:, 2, c:c + 1], ps_a[:, c, 0:GT], ALU.mult,
                                                 ALU.add).then_inc(y_taken, 1)
                    dve.wait_ge(y_taken, CC * g + CC)
                    dve.tensor_tensor(yT[:, :, :], yT[:, :, :], gate[:, :, :], ALU.mult).then_inc(yT_ready, 1)
                    for u in range(GU):
                        dve.wait_ge(out_done, GU * g + u + 1)
                        dve.tensor_tensor(res[0:T, u, :], ps_b[0:T, u % 2, 0:D], n.xn[0:T, u, :], ALU.add).then_inc(out_read, 1)
                        dve.wait_ge(out_read, GU * g + u + 1)
                        steps.link(dve.bn_stats(rstat[0:T, u, :], res[0:T, u, :]))
                    mean_e, m2_e, mean_o, m2_o = (rstat[0:T, :, k] for k in (1, 2, 4, 5))
                    mean, apart, both = (ragg[0:T, k, :] for k in range(3))
                    steps.link(dve.tensor_tensor(mean, mean_e, mean_o, ALU.add))
                    steps.link(dve.tensor_tensor(apart, mean_e, mean_o, ALU.subtract))
                    steps.link(dve.tensor_tensor(both, m2_e, m2_o, ALU.add))
                    steps.link(dve.tensor_scalar(mean, mean, 0.5, None, ALU.mult))
                    steps.link(dve.tensor_tensor(apart, apart, apart, ALU.mult))
                    steps.link(dve.tensor_scalar(both, both, 1.0 / D, LN_EPS, ALU.mult, ALU.add))
                    dve.scalar_tensor_tensor(rroot[0:T, 0, :], apart, 0.25, both, ALU.mult, ALU.add).then_inc(spread2, 1)
                    dve.wait_ge(rooted2, g + 1)
                    for u in range(GU):
                        steps.link(dve.tensor_scalar(res[0:T, u, :], res[0:T, u, :], ragg[0:T, 0, u:u + 1], rroot[0:T, 1, u:u + 1],
                                                     ALU.subtract, ALU.mult))
                    steps.link(dve.tensor_tensor(res[0:T, :, :], res[0:T, :, :],
                                                 gamma[0:T, :].unsqueeze(1).broadcast_to([T, GU, D]), ALU.mult))
                    steps.link(dve.tensor_tensor(res[0:T, :, :], res[0:T, :, :],
                                                 beta[0:T, :].unsqueeze(1).broadcast_to([T, GU, D]), ALU.add))
                    steps.link(dve.tensor_tensor(hidden[0:T, bass.ds(GU * g, GU), :], hidden[0:T, bass.ds(GU * g, GU), :],
                                                 res[0:T, :, :], ALU.add))
                    steps.end()



def expert_attention(nc, shared, dram):
    hidden, ident, ident16, minus_half = (shared[k] for k in ("hidden", "ident", "ident16", "minus_half"))
    E, R, GH = 8, 16, 64
    Q, K, V, O = range(4)
    with Scope(nc, "eattn") as s:
        n = Norm(s)
        a = Attention(s, HEADS, False, 1.0 / math.sqrt(HD))
        w = s.sb("w", [P, DC, 4 * D])
        up = s.sb("up", [P, 4, D])
        down = s.sb("down", [P, DC, 4, P])
        strength = s.sb("strength", [P, 4])
        gated = s.sb("gated", [P, 4, B])
        qk_bias = s.sb("qk_bias", [P, 2, DC])
        v_bias = s.sb("v_bias", [P, D])
        o_bias = s.sb("o_bias", [P, D])
        gw1 = s.sb("gw1", [P, DC, GH])
        gw2 = s.sb("gw2", [GH, E])
        gb1 = s.sb("gb1", [GH, 1])
        gb2 = s.sb("gb2", [P, E])
        pooled = s.sb("pooled", [P, DC, B])
        gate_h = s.sb("gate_h", [GH, B])
        score = s.sb("score", [P, 1, E])
        gate_e = s.sb("gate_e", [P, 1, E])
        chosen = s.sb("chosen", [P, 1, E])
        restart = s.sb("restart", [P, 1, E])
        total = s.sb("total", [P, 3])
        wide = s.sb("wide", [P, E, R])
        work = choice_buffers(s, 1, E)
        ranks = s.sb("ranks", [P, 3, GT])
        ranks_o = s.sb("ranks_o", [P, T])
        summed = s.sb("summed", [P, D])
        (w_loaded, restart_ready, pooled_ready, gates_done, gate_h_ready, gate_in, gate_exp, wide_ready, gated_ready,
         down_done, ranks_in, down_o_done) = (s.sem(k) for k in (
             "w_loaded", "restart_ready", "pooled_ready", "gates_done", "gate_h_ready", "gate_in", "gate_exp",
             "wide_ready", "gated_ready", "down_done", "ranks_in", "down_o_done"))
        a.ranks_ready = s.sem("ranks_ready")
        LOADS = 4 * 4 + 2 + 2 + 4
        with nc.Block() as block:
            @block.sync
            def _(sync):
                for k, name in enumerate("qkvo"):
                    sync.dma_start(w[:, :, k * D:(k + 1) * D], dram[f"L3_ffn_{name}Wm"].rearrange("(c p) n -> p c n", p=P)
                                   ).then_inc(w_loaded, 16)
                    sync.dma_start(up[:, k, :], dram[f"L3_ffn_{name}U"]).then_inc(w_loaded, 16)
                    sync.dma_start(down[:, :, k, :], dram[f"L3_ffn_{name}V"].rearrange("(c p) n -> p c n", p=P)
                                   ).then_inc(w_loaded, 16)
                    sync.dma_start(strength[:, k:k + 1], dram[f"L3_ffn_{name}S"].rearrange("(e a) -> e a", a=1)
                                   ).then_inc(w_loaded, 16)
                for k, name in enumerate("qk"):
                    sync.dma_start(qk_bias[:, k, :], dram[f"L3_ffn_{name}b_col"]).then_inc(w_loaded, 16)
                load_rows(sync, v_bias[0:T, :], dram["L3_ffn_vb"], w_loaded)
                load_rows(sync, o_bias[0:T, :], dram["L3_ffn_ob"], w_loaded)
                sync.dma_start(gw1[:, :, :], dram["L3_ffn_gw1"].rearrange("(c p) n -> p c n", p=P)).then_inc(w_loaded, 16)
                sync.dma_start(gw2[:, :], dram["L3_ffn_gw2"]).then_inc(w_loaded, 16)
                sync.dma_start(gb1[:, :], dram["L3_ffn_gb1"].rearrange("(e a) -> e a", a=1)).then_inc(w_loaded, 16)
                load_rows(sync, gb2[0:B, :], dram["L3_ffn_gb2"], w_loaded, rows=B)

            @block.gpsimd
            def _(pool):
                pool.memset(restart[:, :, :], 1.0).then_inc(restart_ready, 1)
                pool.wait_ge(restart_ready, 1)
                pool.memset(restart[:, :, 0:1], 0.0).then_inc(restart_ready, 1)
                attention_constants_pool(pool, a)
                norm_root_pool(pool, n, minus_half)
                attention_pool(pool, a)

            @block.scalar
            def _(act):
                act.wait_ge(w_loaded, 16 * LOADS)
                with act.Fori(0, G) as g:
                    act.wait_ge(pooled_ready, g)
                    norm_group_act(act, n, g, a.ps_g)
                act.wait_ge(gates_done, 1)
                act.activation(gate_h[:, :], a.ps_s[0:GH, 0, 0:B], ACT.Relu, scale=1.0 / T, bias=gb1[:, 0:1]
                               ).then_inc(gate_h_ready, 1)
                act.wait_ge(gate_in, 1)
                act.activation(gate_e[0:B, 0, :], score[0:B, 0, :], ACT.Exp).then_inc(gate_exp, 1)
                act.wait_ge(gated_ready, 4)
                with act.Fori(0, G) as g:
                    act.wait_ge(a.v_done, GU * g)
                    norm_group_act(act, n, g + G, a.ps_o)
                    for k in range(3):
                        act.wait_ge(down_done, 3 * g + k + 1)
                        for u in range(GU):
                            ins = act.activation(ranks[:, k, u * T:(u + 1) * T], a.ps_g[:, (k + 1) % 2, u * T:(u + 1) * T],
                                                 ACT.Copy, scale=gated[:, k, bass.ds(GU * g + u, 1)])
                        ins.then_inc(ranks_in, 1)
                    queries_keys_act(act, a, g, qk_bias[:, 0, :], qk_bias[:, 1, :])

                def ranks_out(b):
                    act.wait_ge(down_o_done, b + 1)
                    act.activation(ranks_o[:, :], a.ps_g[:, 1, 0:T], ACT.Copy,
                                   scale=gated[:, O, bass.ds(b, 1)]).then_inc(a.ranks_ready, 1)

                attention_act(act, a, extra=ranks_out)

            @block.tensor
            def _(pe):
                pe.wait_ge(w_loaded, 16 * LOADS)
                pe.wait_ge(a.const_ready, attention_constants_ready(a))
                with pe.Fori(0, G) as g:
                    pe.wait_ge(n.xT_ready, 2 * g)
                    norm_group_pe(pe, n, g, a.ps_g, ident)
                pe.wait_ge(n.xT_ready, 2 * G)
                pe.wait_ge(pooled_ready, G)
                for c in range(DC):
                    mm = pe.matmul(a.ps_s[0:GH, 0, 0:B], gw1[:, c, :], pooled[:, c, :], start=(c == 0), stop=(c == DC - 1))
                mm.then_inc(gates_done, 1)
                pe.wait_ge(gate_h_ready, 1)
                pe.matmul(a.ps_t[0:B, 0, 0:E], gate_h[:, :], gw2[:, :], start=True, stop=True).then_inc(gates_done, 1)
                pe.wait_ge(wide_ready, 1)
                pe.transpose(a.ps_t[:, 1, 0:B], wide[0:B, :, :], ident[0:B, 0:B]).then_inc(gates_done, 1)
                pe.wait_ge(gated_ready, 4)
                with pe.Fori(0, G) as g:
                    pe.wait_ge(n.xT_ready, 2 * G + 2 * g)
                    norm_group_pe(pe, n, g + G, a.ps_o, ident)
                    pe.wait_ge(n.xT_ready, 2 * G + 2 * g + 2)
                    for k in range(3):
                        if k < 2:
                            pe.wait_ge(a.v_ready, GU * g)
                        else:
                            pe.wait_ge(ranks_in, 3 * g + 1)
                        for c in range(DC):
                            mm = pe.matmul(a.ps_g[:, (k + 1) % 2, 0:GT], down[:, c, k, :], n.xT[:, c, :], start=(c == 0),
                                           stop=(c == DC - 1))
                        mm.then_inc(down_done, 1)
                    for k, bank, done, read in ((Q, a.ps_s, a.q_done, a.q_ready), (K, a.ps_t, a.k_done, a.k_ready)):
                        pe.wait_ge(read, DC * g)
                        for m in range(DC):
                            at = k * D + m * P
                            for c in range(DC):
                                pe.matmul(bank[:, m, 0:GT], w[:, c, at:at + P], n.xT[:, c, :], start=(c == 0), stop=False)
                            pe.wait_ge(ranks_in, 3 * g + 1 + k)
                            pe.matmul(bank[:, m, 0:GT], up[:, k, m * P:(m + 1) * P], ranks[:, k, :], start=False,
                                      stop=True).then_inc(done, 1)
                    pe.wait_ge(ranks_in, 3 * g + 3)
                    for u in range(GU):
                        values_free_pe(pe, a, g, u)
                        for c in range(DC):
                            pe.matmul(a.ps_g[0:T, u % 2, 0:D], n.xT[:, c, u * T:(u + 1) * T], w[:, c, V * D:(V + 1) * D],
                                      start=(c == 0), stop=False)
                        pe.matmul(a.ps_g[0:T, u % 2, 0:D], ranks[:, V, u * T:(u + 1) * T], up[:, V, :], start=False,
                                  stop=True).then_inc(a.v_done, 1)

                def ranks_of_output(b):
                    for c in range(DC):
                        mm = pe.matmul(a.ps_g[:, 1, 0:T], down[:, c, O, :], a.ctxT[:, c, :], start=(c == 0),
                                       stop=(c == DC - 1))
                    mm.then_inc(down_o_done, 1)

                def add_experts(b):
                    pe.wait_ge(a.ranks_ready, b + 1)
                    return pe.matmul(a.ps_g[0:T, 0, 0:D], ranks_o[:, :], up[:, O, :], start=False, stop=True)

                attention_pe(pe, a, ident, ident16, w[:, :, O * D:(O + 1) * D], ranks_of_output, add_experts)

            @block.vector
            def _(dve):
                attention_constants_dve(dve, a, ident)
                norm_statistics_dve(dve, n, hidden, 1e-5)
                with dve.Fori(0, G) as g:
                    norm_group_dve(dve, n, g, hidden)
                    dve.wait_ge(n.xT_ready, 2 * g + 2)
                    dve.tensor_reduce(pooled[:, :, bass.ds(GU * g, GU)], n.xT[:, :, :].rearrange("p c (u t) -> p c u t", u=GU),
                                      AX.X, ALU.add).then_inc(pooled_ready, 1)
                dve.wait_ge(w_loaded, 16 * LOADS)
                dve.wait_ge(a.const_ready, 4)
                dve.wait_ge(a.step, 1)
                dve.wait_ge(restart_ready, 2)
                dve.wait_ge(gates_done, 2)
                steps = Chain(dve, a.step, 1)
                rows = slice(0, B)
                steps.link(dve.tensor_tensor(score[rows, 0, :], a.ps_t[rows, 0, 0:E], gb2[rows, :], ALU.add))
                choose_two_dve(dve, s, steps, score, None, rows, [B, 1, E], restart, work, chosen)
                steps.link(dve.tensor_reduce(total[rows, 0:1], score[rows, 0, :], AX.X, ALU.max))
                dve.tensor_scalar(score[rows, 0, :], score[rows, 0, :], total[rows, 0:1], None, ALU.subtract).then_inc(gate_in, 1)
                dve.wait_ge(gate_exp, 1)
                steps.link(dve.tensor_tensor(gate_e[rows, 0, :], gate_e[rows, 0, :], chosen[rows, 0, :], ALU.mult))
                steps.link(dve.tensor_reduce(total[rows, 1:2], gate_e[rows, 0, :], AX.X, ALU.add))
                steps.link(dve.reciprocal(total[rows, 2:3], total[rows, 1:2]))
                dve.tensor_scalar(wide[rows, :, :], gate_e[rows, 0, :].unsqueeze(2).broadcast_to([B, E, R]), total[rows, 2:3],
                                  None, ALU.mult).then_inc(wide_ready, 1)
                dve.wait_ge(gates_done, 3)
                for k in range(4):
                    dve.tensor_scalar(gated[:, k, :], a.ps_t[:, 1, 0:B], strength[:, k:k + 1], None,
                                      ALU.mult).then_inc(gated_ready, 1)
                base = steps.base
                with dve.Fori(0, G) as g:
                    dve.wait_ge(n.turned, GU * G + GU * g)
                    for u in range(GU):
                        b = GU * g + u
                        dve.tensor_scalar(n.xn[0:T, u, :], hidden[0:T, b, :], n.mean[0:T, bass.ds(b, 1)],
                                          n.rstd[0:T, bass.ds(b, 1)], ALU.subtract, ALU.mult).then_inc(n.normed, 1)
                    for u in range(GU):
                        dve.wait_ge(a.v_done, GU * g + u + 1)
                        dve.tensor_tensor(a.v[0:T, GU * g + u, :, 0:HD],
                                          a.ps_g[0:T, u % 2, 0:D].rearrange("p (h e) -> p h e", h=HEADS),
                                          v_bias[0:T, :].rearrange("p (h e) -> p h e", h=HEADS),
                                          ALU.add).then_inc(a.v_ready, 1)
                steps = GroupSteps(dve, a.step, base, 2)

                def context(b, buf):
                    outputs = a.ps_o[0:T, buf, 0:HEADS * (HD + 1)].rearrange("p (h e) -> p h e", h=HEADS)
                    steps.link(dve.reciprocal(a.rden[0:T, 0, :], outputs[:, :, HD]))
                    steps.link(dve.tensor_tensor(a.ctx[0:T, buf, :].rearrange("p (h e) -> p h e", h=HEADS),
                                                 outputs[:, :, 0:HD],
                                                 a.rden[0:T, 0, :].unsqueeze(2).broadcast_to([T, HEADS, HD]), ALU.mult))
                    dve.sem_inc(a.ctx_ready, 1)
                    dve.sem_inc(a.outputs_read, 1)

                def add(b):
                    dve.wait_ge(a.out_done, b + 1)
                    dve.tensor_tensor(summed[0:T, :], a.ps_g[0:T, 0, 0:D], o_bias[0:T, :], ALU.add).then_inc(a.biased, 1)
                    dve.wait_ge(a.biased, b + 1)
                    dve.tensor_tensor(hidden[0:T, b, :], hidden[0:T, b, :], summed[0:T, :], ALU.add).then_inc(a.added, 1)

                attention_dve(dve, a, steps, context, add)


LAYERS = (tokenizer, gated_attention, quantised_linear, layer1_attention, frequency_linear, differential_attention,
          mixture, state_space, expert_attention)



def audio_tower(nc, dram, out):
    with Scope(nc, "top") as top:
        shared = {"hidden": top.sb("hidden", [P, B, D])}
        constants(nc, top, shared)
        for layer in LAYERS:
            layer(nc, shared, dram)
        written = top.sem("written")
        with nc.Block() as block:
            @block.sync
            def _(sync):
                sync.dma_start(out.rearrange("b t d -> t b d"), shared["hidden"][0:T, :, :]).then_inc(written, 16)
                sync.wait_ge(written, 16)



def laid_out(inputs):
    a = {k: np.asarray(v) for k, v in inputs.items()}
    out = {}
    frames = np.zeros((B, (T + 1) * STRIDE, BANDS), a["x"].dtype)
    frames[:, :FRAMES] = a.pop("x")
    out["frames"] = frames.reshape(B, T + 1, STRIDE * BANDS).transpose(2, 0, 1)
    for k, v in a.items():
        out[k.replace("L0_tok", "tok")] = v
    out["tok_W1"] = out["tok_W1"].reshape(2, STRIDE * BANDS, D)
    for k in ("L0_attn_w_qkv", "L0_attn_w_ent", "L0_attn_w_out", "L0_ffn_weight_int8", "L3_ffn_gw1", "L3_ffn_gw2",
              "L3_ffn_qWm", "L3_ffn_kWm", "L3_ffn_vWm", "L3_ffn_oWm"):
        out[k] = out[k].T
    for p in "qkvo":
        U, V, S = (out[f"L3_ffn_{p}{m}"] for m in "UVS")
        out[f"L3_ffn_{p}U"] = U.transpose(0, 2, 1).reshape(-1, D)
        out[f"L3_ffn_{p}V"] = V.reshape(-1, D).T
        out[f"L3_ffn_{p}S"] = S.reshape(-1)
    for k, v in list(out.items()):
        if v.ndim == 1 and v.size % P == 0:
            out[k + "_col"] = v.reshape(-1, P).T
    n = np.arange(D)
    angle = 2.0 * np.pi * (np.outer(n, n) % D) / D
    out["dft"] = np.stack([np.cos(angle), np.sin(angle)]).astype(np.float32)
    out = {k: np.ascontiguousarray(v) for k, v in out.items()}
    out["L0_ffn_weight_int8"] = out["L0_ffn_weight_int8"].view(np.int32)
    return out


def kernel(**inputs):
    import concourse.bacc as bacc
    from concourse.bass_utils import run_bass_kernel_spmd as run

    nc = bacc.Bacc("TRN2", target_bir_lowering=False, num_devices=1)
    arrays, dram = {}, {}
    for name, a in laid_out(inputs).items():
        arrays[f"in_{name}"] = a
        dram[name] = nc.dram_tensor(f"in_{name}", a.shape, mybir.dt.from_np(a.dtype), kind="ExternalInput").ap()
    out = nc.dram_tensor("out", (B, T, D), F32, kind="ExternalOutput").ap()
    audio_tower(nc, dram, out)
    return run(nc, [arrays], core_ids=[0]).results[0]["out"]
```

```python
import math
from contextlib import ExitStack

import numpy as np
import concourse.bass as bass
from concourse import mybir

F32 = mybir.dt.float32
BF16 = mybir.dt.bfloat16
I8 = mybir.dt.int8
ACT = mybir.ActivationFunctionType
ALU = mybir.AluOpType
AX = mybir.AxisListType

P = 128
B = 32
FRAMES, BANDS = 375, 80
STRIDE, WINDOW = 4, 8
T = 93
D = 256
DC = D // P
GU = 4
G = B // GU
GT = GU * T
HEADS, HD = 16, 16
MASKED = -1.0e30
ROUND = 1.5 * 2.0 ** 23


class Chain:

    def __init__(self, eng, sem, base=0):
        self.eng, self.sem, self.base = eng, sem, base

    def link(self, ins):
        self.base = self.base + 1
        ins.then_inc(self.sem, 1)
        self.eng.wait_ge(self.sem, self.base)


class Scope:

    def __init__(self, nc, name):
        self.nc, self.name, self.stack, self.semaphores = nc, name, ExitStack(), []

    def __enter__(self):
        return self

    def __exit__(self, *a):
        self.stack.__exit__(*a)
        if self.semaphores:
            self.nc.clear_and_free_semaphores(self.semaphores)
            self.nc.all_engine_barrier()

    def sb(self, name, shape, dt=F32):
        return self.stack.enter_context(self.nc.sbuf_tensor(f"{self.name}_{name}", shape, dt))

    def ps(self, name, shape, dt=F32):
        return self.stack.enter_context(self.nc.psum_tensor(f"{self.name}_{name}", shape, dt))

    def sem(self, name):
        self.semaphores.append(self.nc.alloc_semaphore(f"{self.name}_{name}"))
        return self.semaphores[-1]



def constants(nc, top, shared):
    shared["ident"] = ident = top.sb("ident", [P, P])
    shared["ident16"] = ident16 = top.sb("ident16", [P, P], BF16)
    shared["minus_half"] = minus_half = top.sb("minus_half", [P, B])
    shared["stat"] = top.sb("stat", [P, B, 6])
    with Scope(nc, "const") as s:
        filled = s.sem("filled")
        with nc.Block() as block:
            @block.gpsimd
            def _(pool):
                pool.memset(ident[:, :], 0.0).then_inc(filled, 1)
                pool.memset(minus_half[:, :], -0.5).then_inc(filled, 1)
                pool.wait_ge(filled, 2)
                pool.affine_select(out=ident[:, :], in_=ident[:, :], compare_op=ALU.not_equal, fill=1.0, base=0,
                                   pattern=[[-1, P]], channel_multiplier=1).then_inc(filled, 1)

            @block.vector
            def _(dve):
                dve.wait_ge(filled, 3)
                dve.tensor_copy(ident16[:, :], ident[:, :]).then_inc(filled, 1)
                dve.wait_ge(filled, 4)



def tokenizer(nc, shared, dram):
    hidden, ident, minus_half = shared["hidden"], shared["ident"], shared["minus_half"]
    BLOCK = STRIDE * BANDS
    NBLK = T + 1
    rows = [P, P, BLOCK - 2 * P]
    with Scope(nc, "tok") as s:
        frames = s.sb("frames", [P, 3, B, NBLK])
        w1 = s.sb("w1", [P, 2, 3, D])
        w2 = s.sb("w2", [P, DC, D])
        cols = s.sb("cols", [P, 4, DC])
        hid1 = s.sb("hid1", [P, DC, GT])
        hid2 = s.sb("hid2", [P, DC, B * T])
        normal = s.sb("normal", [P, DC, GT])
        stat = s.sb("stat", [P, DC, G, 6])
        agg = s.sb("agg", [P, DC, 2])
        fold = s.sb("fold", [P, 4, DC])
        ps1 = s.ps("ps1", [P, 2, 512])
        ps2 = s.ps("ps2", [P, 2, 512])
        pst = s.ps("pst", [P, 2, 512])
        w_loaded = s.sem("w_loaded")
        cols_loaded = s.sem("cols_loaded")
        frames_loaded = [s.sem(f"frames_loaded{i}") for i in range(4)]
        first_done = s.sem("first_done")
        first_relu = s.sem("first_relu")
        second_done = s.sem("second_done")
        second_relu = s.sem("second_relu")
        step = s.sem("step")
        shifted = s.sem("shifted")
        rooted = s.sem("rooted")
        folded = s.sem("folded")
        normed = s.sem("normed")
        turned = s.sem("turned")
        placed = s.sem("placed")
        with nc.Block() as block:
            @block.sync
            def _(sync):
                for half in range(2):
                    for c in range(3):
                        sync.dma_start(w1[0:rows[c], half, c, :],
                                       dram["tok_W1"][half, c * P:c * P + rows[c], :]).then_inc(w_loaded, 16)
                sync.dma_start(w2[:, :, :], dram["tok_W2"].rearrange("(c p) n -> p c n", p=P)).then_inc(w_loaded, 16)
                for n, name in enumerate(("tok_b1", "tok_b2", "tok_gamma", "tok_beta")):
                    sync.dma_start(cols[:, n, :], dram[name + "_col"]).then_inc(cols_loaded, 16)

            @block.scalar
            def _(act):
                for part in range(4):
                    for c in range(3):
                        act.dma_start(frames[0:rows[c], c, 8 * part:8 * part + 8, :],
                                      dram["frames"][c * P:c * P + rows[c], 8 * part:8 * part + 8, :]
                                      ).then_inc(frames_loaded[part], 16)
                act.wait_ge(cols_loaded, 64)
                with act.Fori(0, G) as g:
                    for c in range(DC):
                        act.wait_ge(first_done, 2 * g + c + 1)
                        act.activation(hid1[:, c, :], ps1[:, c, 0:GT], ACT.Relu,
                                       bias=cols[:, 0, c:c + 1]).then_inc(first_relu, 1)
                    for c in range(DC):
                        act.wait_ge(second_done, 2 * g + c + 1)
                        act.activation(hid2[:, c, bass.ds(g * GT, GT)], ps2[:, c, 0:GT], ACT.Relu,
                                       bias=cols[:, 1, c:c + 1]).then_inc(second_relu, 1)
                act.wait_ge(folded, 1)
                with act.Fori(0, G) as g:
                    act.wait_ge(turned, 4 * g)
                    for c in range(DC):
                        act.activation(normal[:, c, :], hid2[:, c, bass.ds(g * GT, GT)], ACT.Identity,
                                       bias=fold[:, 3, c:c + 1], scale=fold[:, 2, c:c + 1]).then_inc(normed, 1)

            @block.tensor
            def _(pe):
                pe.wait_ge(w_loaded, 7 * 16)

                def layers(g):
                    for m in range(DC):
                        pe.wait_ge(first_relu, 2 * g)
                        for n in range(6):
                            half, c = n // 3, n % 3
                            mm = pe.matmul(ps1[:, m, 0:GT], w1[0:rows[c], half, c, m * P:(m + 1) * P],
                                           frames[0:rows[c], c, bass.ds(g * GU, GU), half:half + T],
                                           start=(n == 0), stop=(n == 5))
                        mm.then_inc(first_done, 1)
                    pe.wait_ge(first_relu, 2 * g + 2)
                    pe.wait_ge(second_relu, 2 * g)
                    for m in range(DC):
                        for c in range(DC):
                            mm = pe.matmul(ps2[:, m, 0:GT], w2[:, c, m * P:(m + 1) * P], hid1[:, c, :],
                                           start=(c == 0), stop=(c == DC - 1))
                        mm.then_inc(second_done, 1)
                for part in range(4):
                    pe.wait_ge(frames_loaded[part], 48)
                    with pe.Fori(0, G // 4) as i:
                        layers(G // 4 * part + i)
                with pe.Fori(0, G) as g:
                    pe.wait_ge(normed, 2 * g + 2)
                    for u in range(GU):
                        if u >= 2:
                            pe.wait_ge(placed, 4 * g + u - 1)
                        else:
                            pe.wait_ge(placed, 4 * g)
                        for c in range(DC):
                            mm = pe.transpose(pst[0:T, u % 2, c * P:(c + 1) * P], normal[:, c, u * T:(u + 1) * T],
                                              ident[:, :])
                        mm.then_inc(turned, 1)

            @block.vector
            def _(dve):
                with dve.Fori(0, G) as g:
                    for c in range(DC):
                        dve.wait_ge(second_relu, 2 * g + c + 1)
                        dve.bn_stats(stat[:, c, g, :], hid2[:, c, bass.ds(g * GT, GT)]).then_inc(step, 1)
                dve.wait_ge(step, 2 * G)
                steps = Chain(dve, step, 2 * G)
                for c in range(DC):
                    steps.link(dve.bn_aggr(agg[:, c, :], stat[:, c, :, :]))
                dve.tensor_scalar(fold[:, 0, :], agg[:, :, 1], 1e-5, None, ALU.add).then_inc(shifted, 1)
                dve.wait_ge(rooted, 1)
                dve.wait_ge(cols_loaded, 64)
                steps.link(dve.tensor_tensor(fold[:, 2, :], fold[:, 1, :], cols[:, 2, :], ALU.mult))
                steps.link(dve.tensor_tensor(fold[:, 0, :], agg[:, :, 0], fold[:, 2, :], ALU.mult))
                dve.tensor_tensor(fold[:, 3, :], cols[:, 3, :], fold[:, 0, :], ALU.subtract).then_inc(folded, 1)
                with dve.Fori(0, G) as g:
                    for u in range(GU):
                        dve.wait_ge(turned, 4 * g + u + 1)
                        dve.tensor_copy(hidden[0:T, 4 * g + u, :], pst[0:T, u % 2, 0:D]).then_inc(placed, 1)
                        measure_dve(dve, shared, 4 * g + u, placed, 4 * g + u + 1)

            @block.gpsimd
            def _(pool):
                pool.wait_ge(shifted, 1)
                pool.tensor_tensor(fold[:, 1, :], fold[:, 0, :], minus_half[:, 0:DC], ALU.pow).then_inc(rooted, 1)



class Norm:

    def __init__(self, s, stat=None, prefix=""):
        self.known = stat is not None
        self.stat = stat if self.known else s.sb(prefix + "stat", [P, B, 6])
        self.tmp = s.sb(prefix + "stat_tmp", [P, 4, B])
        self.mean = s.sb(prefix + "mean", [P, B])
        self.rstd = s.sb(prefix + "rstd", [P, B])
        self.xn = s.sb(prefix + "xn", [P, GU, D])
        self.xT = s.sb(prefix + "xT", [P, DC, GT])
        self.measured = s.sem(prefix + "measured")
        self.step = s.sem(prefix + "norm_step")
        self.spread = s.sem(prefix + "spread")
        self.rooted = s.sem(prefix + "rooted")
        self.normed = s.sem(prefix + "normed")
        self.turned = s.sem(prefix + "turned")
        self.xT_ready = s.sem(prefix + "xT_ready")


def norm_statistics_dve(dve, n, source, eps, first_only=False):
    if not n.known:
        with dve.Fori(0, G) as g:
            for u in range(GU):
                dve.bn_stats(n.stat[0:T, GU * g + u, :], source[0:T, GU * g + u, :]).then_inc(n.measured, 1)
        dve.wait_ge(n.measured, B)
    mean_e, m2_e, mean_o, m2_o = (n.stat[0:T, :, k] for k in (1, 2, 4, 5))
    t = [n.tmp[0:T, k, :] for k in range(4)]
    steps = Chain(dve, n.step)
    dve.tensor_tensor(t[0], mean_e, mean_o, ALU.add).then_inc(n.step, 1)
    dve.tensor_tensor(t[1], mean_e, mean_o, ALU.subtract).then_inc(n.step, 1)
    dve.tensor_tensor(t[2], m2_e, m2_o, ALU.add).then_inc(n.step, 1)
    steps.base = 3
    dve.wait_ge(n.step, 3)
    dve.tensor_scalar(n.mean[0:T, :], t[0], 0.5, None, ALU.mult).then_inc(n.step, 1)
    dve.tensor_tensor(t[3], t[1], t[1], ALU.mult).then_inc(n.step, 1)
    dve.tensor_scalar(t[2], t[2], 1.0 / D, eps, ALU.mult, ALU.add).then_inc(n.step, 1)
    dve.wait_ge(n.step, 6)
    dve.scalar_tensor_tensor(t[0], t[3], 0.25, t[2], ALU.mult, ALU.add).then_inc(n.spread, 1)
    dve.wait_ge(n.rooted, 1 if first_only else 2)


def measure_dve(dve, shared, b, added, count):
    dve.wait_ge(added, count)
    dve.bn_stats(shared["stat"][0:T, b, :], shared["hidden"][0:T, b, :])


def norm_root_pool(pool, n, minus_half):
    pool.wait_ge(n.spread, 1)
    for part in (slice(0, GU), slice(GU, B)):
        pool.tensor_tensor(n.rstd[0:T, part], n.tmp[0:T, 0, part], minus_half[0:T, part], ALU.pow).then_inc(n.rooted, 1)


def norm_group_dve(dve, n, g, source, rounds=0):
    if not isinstance(g, int) or g:
        dve.wait_ge(n.rooted, 2)
        dve.wait_ge(n.turned, GU * g + rounds * B)
    elif rounds:
        dve.wait_ge(n.turned, rounds * B)
    for u in range(GU):
        b = GU * g + u
        dve.tensor_scalar(n.xn[0:T, u, :], source[0:T, b, :], n.mean[0:T, bass.ds(b, 1)], n.rstd[0:T, bass.ds(b, 1)],
                          ALU.subtract, ALU.mult).then_inc(n.normed, 1)


def over_groups(eng, body):
    with eng.Fori(0, G - 1) as g:
        body(g, False)
    body(G - 1, True)


def norm_group_pe(pe, n, g, banks, ident):
    for u in range(GU):
        pe.wait_ge(n.normed, GU * g + u + 1)
        for c in range(DC):
            mm = pe.transpose(banks[:, c, u * T:(u + 1) * T], n.xn[0:T, u, c * P:(c + 1) * P], ident[0:T, 0:T])
        mm.then_inc(n.turned, 1)


def norm_group_act(act, n, g, banks, scale=None, shift=None):
    act.wait_ge(n.turned, GU * g + GU)
    for c in range(DC):
        act.activation(n.xT[:, c, :], banks[:, c, 0:GT], ACT.Identity,
                       bias=0.0 if shift is None else shift[:, c:c + 1],
                       scale=1.0 if scale is None else scale[:, c:c + 1]).then_inc(n.xT_ready, 1)



class Attention:

    def __init__(self, s, maps, causal, exp_scale):
        self.maps, self.causal, self.exp_scale = maps, causal, exp_scale
        self.width = D // maps
        self.variants = P // self.width
        self.units = maps // 4
        self.banks_o = maps // HEADS
        self.turn_at = 1 if self.units == 4 else 4
        self.q_all = s.sb("q_all", [P, DC, B * T])
        self.k_all = s.sb("k_all", [P, DC, B * T])
        self.v = s.sb("v", [P, B, HEADS, HD + 1])
        self.q = s.sb("q", [P, 2, DC, self.variants, T])
        self.k = s.sb("k", [P, 2, DC, T])
        self.only = s.sb("only", [P, self.variants])
        self.sel = s.sb("sel", [P, maps, T], BF16)
        self.negmax = s.sb("negmax", [P, maps])
        self.split_width = 2 * maps if maps == HEADS else 2 * maps + 2
        self.split = s.sb("split", [P, self.split_width], BF16)
        self.merged = causal and 2 * maps + T <= P
        self.maxT = s.sb("maxT", [P, T], BF16)
        self.probs = s.sb("probs", [P, 4, GT])
        self.rden = s.sb("rden", [P, self.banks_o, HEADS])
        self.ctx = s.sb("ctx", [P, 2, D])
        self.ctxT = s.sb("ctxT", [P, DC, T])
        if causal:
            self.mask_q = s.sb("mask_q", [P, 4, T], BF16)
            if not self.merged:
                self.mask_k = s.sb("mask_k", [P, 4, T], BF16)
        self.ps_s = s.ps("scores", [P, 2, 512])
        self.ps_t = s.ps("scoresT", [P, 2, 512])
        self.ps_o = s.ps("outputs", [P, 2, 512])
        self.ps_g = s.ps("general", [P, 2, 512])
        self.const_ready = s.sem("att_const")
        self.q_done = s.sem("q_done")
        self.k_done = s.sem("k_done")
        self.v_done = s.sem("v_done")
        self.q_ready = s.sem("q_ready")
        self.k_ready = s.sem("k_ready")
        self.v_ready = s.sem("v_ready")
        self.v_gated = None
        self.ranks_ready = None
        self.cut_ready = s.sem("cut_ready")
        self.scored = s.sem("scored")
        self.maxed = s.sem("maxed")
        self.split_ready = s.sem("split_ready")
        self.max_turned = s.sem("max_turned")
        self.maxT_ready = s.sem("maxT_ready")
        self.scoredT = s.sem("scoredT")
        self.probs_ready = s.sem("probs_ready")
        self.weighed = s.sem("weighed")
        self.outputs_read = s.sem("outputs_read")
        self.ctx_ready = s.sem("ctx_ready")
        self.ctx_turned = s.sem("ctx_turned")
        self.ctxT_ready = s.sem("ctxT_ready")
        self.out_done = s.sem("out_done")
        self.added = s.sem("added")
        self.biased = s.sem("biased")
        self.half_split = s.sem("half_split")
        self.step = s.sem("att_step")

    def chunk(self, w):
        return 4 * w // self.variants, 4 * w % self.variants


def over_utterances(eng, body):
    body(0, 0, True, False)
    with eng.Fori(0, B // 2 - 1) as i:
        for j in range(2):
            body(2 * i + j + 1, 1 - j, False, False)
    body(B - 1, 1, False, True)


def attention_constants_pool(pool, a):
    pool.memset(a.sel[:, :, :], 0.0).then_inc(a.const_ready, 1)
    pool.memset(a.v[:, :, :, HD:HD + 1], 1.0).then_inc(a.const_ready, 1)
    pool.memset(a.maxT[:, :], 0.0).then_inc(a.const_ready, 1)
    pool.memset(a.split[:, :], 0.0).then_inc(a.const_ready, 1)
    pool.wait_ge(a.const_ready, 4)
    for part in range(2):
        pool.affine_select(out=a.sel[:, :, :], in_=a.sel[:, :, :], compare_op=ALU.not_equal, fill=1.0,
                           base=-part * a.maps, pattern=[[-1, a.maps], [0, T]],
                           channel_multiplier=1).then_inc(a.const_ready, 1)
        pool.wait_ge(a.const_ready, 5 + part)
    if a.causal:
        masks = [(a.mask_q[:, :, :], -1, 0, [0, 4])]
        if a.merged:
            masks.append((a.maxT[:, :], 1, 2 * a.maps, None))
        else:
            masks.append((a.mask_k[:, :, :], 1, 0, [0, 4]))
        for m, _, first, _ in masks:
            if not first:
                pool.memset(m, 0.0).then_inc(a.const_ready, 1)
        pool.wait_ge(a.const_ready, 7 if a.merged else 8)
        for m, sign, first, maps in masks:
            pool.affine_select(out=m, in_=m, compare_op=ALU.is_ge, fill=MASKED, base=sign * first,
                               pattern=([maps] if maps else []) + [[sign, T]], channel_multiplier=-sign
                               ).then_inc(a.const_ready, 1)
        if a.merged:
            pool.affine_select(out=a.sel[:, :, :], in_=a.sel[:, :, :], compare_op=ALU.not_equal, fill=1.0,
                               base=-2 * a.maps, pattern=[[0, a.maps], [-1, T]],
                               channel_multiplier=1).then_inc(a.const_ready, 1)


def attention_constants_dve(dve, a, ident):
    rows = ident[:, :].rearrange("p (v e) -> p v e", v=a.variants)
    dve.tensor_reduce(a.only[:, :], rows, AX.X, ALU.add).then_inc(a.step, 1)
    dve.sem_inc(a.maxed, 2)
    dve.sem_inc(a.probs_ready, 2)
    dve.sem_inc(a.weighed, 4)
    dve.sem_inc(a.scoredT, 2 * a.units)
    dve.sem_inc(a.outputs_read, 3 - a.banks_o)


def attention_constants_ready(a):
    return 10 if a.causal else 6


def attention_pool(pool, a, root=None):
    pool.wait_ge(a.step, 1)
    pool.wait_ge(a.q_ready, DC * G)
    pool.wait_ge(a.k_ready, DC * G)

    def cut(b, buf, c):
        pool.wait_ge(a.scoredT, a.units * b + (c + 1) * a.units // DC)
        pool.tensor_tensor(a.q[:, buf, c, :, :],
                           a.q_all[:, c, bass.ds(b * T, T)].unsqueeze(1).broadcast_to([P, a.variants, T]),
                           a.only[:, :].unsqueeze(2).broadcast_to([P, a.variants, T]), ALU.mult)
        pool.tensor_copy(a.k[:, buf, c, :], a.k_all[:, c, bass.ds(b * T, T)]).then_inc(a.cut_ready, 1)

    def step(b, buf):
        cut(b + 1, 1 - buf, 1)
        if root is not None:
            root(b - 1)
        cut(b + 2, buf, 0)

    cut(0, 0, 0)
    cut(0, 0, 1)
    cut(1, 1, 0)
    cut(1, 1, 1)
    cut(2, 0, 0)
    with pool.Fori(0, B // 2 - 2) as i:
        for j in range(2):
            step(2 * i + j + 1, 1 - j)
    step(B - 3, 1)
    cut(B - 1, 1, 1)
    if root is not None:
        for b in (B - 3, B - 2, B - 1):
            root(b)


def attention_pe(pe, a, ident, ident16, w_out, before_out=None, extra_out=None):

    def scores(b, buf, w):
        if w % (a.units // DC) == 0:
            pe.wait_ge(a.cut_ready, DC * b + (w * DC // a.units + 1))
        pe.wait_ge(a.maxed, b * a.units + (w + 1))
        bank = a.ps_s[0:T, w % 2, :]
        if a.causal:
            pe.matmul(bank[:, 0:GT], ident16[:, 0:T], a.mask_q[:, :, :], start=True, stop=False,
                      skip_group_check=True)
        c, v = a.chunk(w)
        for j in range(4):
            mm = pe.matmul(bank[:, j * T:(j + 1) * T], a.q[:, buf, c, v + j, :], a.k[:, buf, c, :],
                           start=not a.causal, stop=True, skip_group_check=True)
        mm.then_inc(a.scored, 1)

    def turn_max(b, first):
        pe.wait_ge(a.split_ready, b + 1)
        if not first:
            pe.wait_ge(a.added, b - 1)
        pe.transpose(a.ps_g[0:a.split_width, 0, :].bitcast(BF16)[:, 0:T], a.split[0:T, :],
                     ident16[0:T, 0:T]).then_inc(a.max_turned, 1)

    def scores_t(b, buf, w):
        pe.wait_ge(a.probs_ready, b * a.units + (w + 1))
        bank = a.ps_t[0:T, w % 2, :]
        masked = a.causal and not a.merged
        if masked:
            pe.matmul(bank[:, 0:GT], ident16[:, 0:T], a.mask_k[:, :, :], start=True, stop=False,
                      skip_group_check=True)
        c, v = a.chunk(w)
        pe.matmul(bank[:, 0:GT], a.k[:, buf, c, :], a.q[:, buf, c, v:v + 4, :], start=not masked, stop=False,
                  skip_group_check=True)
        if w == 0:
            pe.wait_ge(a.maxT_ready, b + 1)
        for j in range(4):
            mm = pe.matmul(bank[:, j * T:(j + 1) * T], a.sel[:, 4 * w + j, :], a.maxT[:, :], start=False, stop=True,
                           skip_group_check=True)
        mm.then_inc(a.scoredT, 1)

    def weigh(b, buf, w):
        if w == 0:
            pe.wait_ge(a.outputs_read, b + 1)
        pe.wait_ge(a.probs_ready, b * a.units + (w + 3))
        for j in range(4):
            m = 4 * w + j
            if a.banks_o == 1:
                h, bank = m, buf
            else:
                h, bank = m // 2, m % 2
            mm = pe.matmul(a.ps_o[0:T, bank, h * (HD + 1):(h + 1) * (HD + 1)], a.probs[0:T, w % 4, j * T:(j + 1) * T],
                           a.v[0:T, b, h, :], start=True, stop=True, skip_group_check=True)
        mm.then_inc(a.weighed, 1)

    def turn_ctx(b, buf, first):
        pe.wait_ge(a.ctx_ready, b + 1)
        if not first:
            pe.wait_ge(a.ctxT_ready, b)
            if a.ranks_ready is not None:
                pe.wait_ge(a.ranks_ready, b)
        for c in range(DC):
            mm = pe.transpose(a.ps_g[:, 1, c * T:(c + 1) * T], a.ctx[0:T, buf, c * P:(c + 1) * P], ident[0:T, 0:T])
        mm.then_inc(a.ctx_turned, 1)

    def project(b, first, last):
        pe.wait_ge(a.ctxT_ready, b + 1)
        if not first:
            pe.wait_ge(a.added, b)
        if not last:
            pe.wait_ge(a.maxT_ready, b + 2)
        if before_out is not None:
            before_out(b)
        for c in range(DC):
            mm = pe.matmul(a.ps_g[0:T, 0, 0:D], a.ctxT[:, c, :], w_out[:, c, :], start=(c == 0),
                           stop=(c == DC - 1 and extra_out is None))
        if extra_out is not None:
            mm = extra_out(b)
        mm.then_inc(a.out_done, 1)

    def utterance(b, buf, first, last, second=False):
        for w in range(a.units):
            if not last:
                scores(b + 1, 1 - buf, w)
            scores_t(b, buf, w)
            if w:
                weigh(b, buf, w - 1)
            if not first:
                if w == a.turn_at:
                    turn_ctx(b - 1, 1 - buf, second)
                if w == a.units - 2:
                    project(b - 1, second, False)
        weigh(b, buf, a.units - 1)
        if not last:
            turn_max(b + 1, False)

    pe.wait_ge(a.v_ready if a.v_gated is None else a.v_gated, B)
    for w in range(a.units):
        scores(0, 0, w)
    turn_max(0, True)
    over_utterances(pe, utterance)
    turn_ctx(B - 1, 1, False)
    project(B - 1, False, True)


def attention_act(act, a, ctx_scale=None, extra=None):

    def ctx_t(b):
        act.wait_ge(a.ctx_turned, b + 1)
        act.wait_ge(a.out_done, b)
        if ctx_scale is None:
            act.activation(a.ctxT[:, :, :], a.ps_g[:, 1, 0:DC * T], ACT.Copy).then_inc(a.ctxT_ready, 1)
        else:
            act.activation(a.ctxT[:, :, :], a.ps_g[:, 1, 0:DC * T], ACT.Copy,
                           scale=ctx_scale).then_inc(a.ctxT_ready, 1)

    def utterance(b, buf, first, last):
        for w in range(a.units):
            n = b * a.units + w
            act.wait_ge(a.scoredT, n + (2 * a.units + 1))
            act.wait_ge(a.weighed, n + 1)
            act.activation(a.probs[0:T, w % 4, :], a.ps_t[0:T, w % 2, 0:GT], ACT.Exp,
                           scale=a.exp_scale).then_inc(a.probs_ready, 1)
            if w == a.turn_at and not first:
                ctx_t(b - 1)
                if extra is not None:
                    extra(b - 1)

    over_utterances(act, utterance)
    ctx_t(B - 1)
    if extra is not None:
        extra(B - 1)


def attention_dve(dve, a, steps, context, add, finish=None, shared=None):

    def maximum(b, w):
        dve.wait_ge(a.scored, b * a.units + (w + 1))
        dve.tensor_reduce(a.negmax[0:T, 4 * w:4 * w + 4],
                          a.ps_s[0:T, w % 2, 0:GT].rearrange("p (j t) -> p j t", j=4), AX.X, ALU.max,
                          negate=True).then_inc(a.maxed, 1)

    def split(b):
        dve.wait_ge(a.maxed, 2 + (b + 1) * a.units)
        dve.tensor_copy(a.split[0:T, 0:a.maps], a.negmax[0:T, :]).then_inc(a.half_split, 1)
        dve.wait_ge(a.half_split, b + 1)
        dve.tensor_tensor(a.split[0:T, a.maps:2 * a.maps], a.negmax[0:T, :], a.split[0:T, 0:a.maps],
                          ALU.subtract).then_inc(a.split_ready, 1)
        dve.wait_ge(a.split_ready, b + 1)

    def max_t(b):
        dve.wait_ge(a.max_turned, b + 1)
        dve.wait_ge(a.scoredT, a.units * (b + 2))
        dve.tensor_copy(a.maxT[0:2 * a.maps, :], a.ps_g[0:2 * a.maps, 0, :].bitcast(BF16)[:, 0:T]).then_inc(a.maxT_ready, 1)

    def utterance(b, buf, first, last):
        if last:
            if finish is not None:
                finish(b - 1, 1 - buf)
        else:
            for w in range(a.units):
                maximum(b + 1, w)
                if w == 1 and not first and finish is not None:
                    finish(b - 1, 1 - buf)
            split(b + 1)
        if not first:
            add(b - 1)
        if not last:
            max_t(b + 1)
        if not first and shared is not None:
            measure_dve(dve, shared, b - 1, a.added, b)
        dve.wait_ge(a.weighed, 4 + a.units * (b + 1))
        steps.begin(b)
        context(b, buf)
        steps.end()

    for w in range(a.units):
        maximum(0, w)
    split(0)
    max_t(0)
    over_utterances(dve, utterance)
    if finish is not None:
        finish(B - 1, 1)
    add(B - 1)
    if shared is not None:
        measure_dve(dve, shared, B - 1, a.added, B)


class GroupSteps:

    def __init__(self, eng, sem, base, per):
        self.eng, self.sem, self.base, self.per = eng, sem, base, per

    def begin(self, g):
        self.g, self.n = g, 0
        return self

    def link(self, ins):
        self.n += 1
        ins.then_inc(self.sem, 1)
        self.eng.wait_ge(self.sem, self.g * self.per + (self.base + self.n))

    def end(self):
        assert self.n == self.per, (self.n, self.per)


def load_rows(eng, tile, vector, sem, rows=T):
    eng.dma_start(tile, vector.partition_broadcast(rows)).then_inc(sem, 16)


def project_group_pe(pe, a, n, g, last, w_qkv, v_cols, ident):
    pe.wait_ge(n.xT_ready, 2 * g + 2)
    for what, (bank, done, read) in enumerate(((a.ps_s, a.q_done, a.q_ready), (a.ps_t, a.k_done, a.k_ready))):
        for m in range(DC):
            pe.wait_ge(read, DC * g)
            for c in range(DC):
                mm = pe.matmul(bank[:, m, 0:GT], w_qkv[:, c, what * D + m * P:what * D + (m + 1) * P],
                               n.xT[:, c, :], start=(c == 0), stop=(c == DC - 1))
            mm.then_inc(done, 1)
    if not last:
        norm_group_pe(pe, n, g + 1, a.ps_o, ident)
    for u in range(GU):
        values_free_pe(pe, a, g, u)
        for c in range(DC):
            mm = pe.matmul(a.ps_g[0:T, u % 2, 0:v_cols], n.xT[:, c, u * T:(u + 1) * T],
                           w_qkv[:, c, 2 * D:2 * D + v_cols], start=(c == 0), stop=(c == DC - 1))
        mm.then_inc(a.v_done, 1)


def values_free_pe(pe, a, g, u):
    if u < 2:
        pe.wait_ge(a.v_ready, GU * g)
    else:
        pe.wait_ge(a.v_ready, GU * g + (u - 1))


def queries_keys_act(act, a, g, q_bias, k_bias):
    for kept, bank, done, ready, bias in ((a.q_all, a.ps_s, a.q_done, a.q_ready, q_bias),
                                          (a.k_all, a.ps_t, a.k_done, a.k_ready, k_bias)):
        for m in range(DC):
            act.wait_ge(done, DC * g + m + 1)
            act.activation(kept[:, m, bass.ds(g * GT, GT)], bank[:, m, 0:GT], ACT.Identity,
                           bias=0.0 if bias is None else bias[:, m:m + 1]).then_inc(ready, 1)



def gated_attention(nc, shared, dram):
    hidden, ident, ident16, minus_half = (shared[k] for k in ("hidden", "ident", "ident16", "minus_half"))
    TEMPERATURE, OUT_SCALE, EPS, EPS2 = 0.1, 0.1, 1e-5, 1e-6
    with Scope(nc, "gattn") as s:
        n = Norm(s, shared["stat"])
        a = Attention(s, HEADS, True, 1.0 / (math.sqrt(HD) * TEMPERATURE))
        spread2 = s.sb("spread2", [P, 3, B])
        w_qkv = s.sb("w_qkv", [P, DC, 3 * D + 1])
        w_out = s.sb("w_out", [P, DC, D])
        ln = s.sb("ln", [P, 2, DC])
        qk_bias = s.sb("qk_bias", [P, 2, DC])
        v_bias = s.sb("v_bias", [P, D])
        o_bias = s.sb("o_bias", [P, D])
        b_ent = s.sb("b_ent", [P, 1])
        gate = s.sb("gate", [P, 3, GU])
        summed = s.sb("summed", [P, D])
        w_loaded, spread2_ready, rooted2, gate_in, gate_exp = (
            s.sem(k) for k in ("w_loaded", "spread2_ready", "rooted2", "gate_in", "gate_exp"))
        a.v_gated = s.sem("v_gated")
        LOADS = 9
        with nc.Block() as block:
            @block.sync
            def _(sync):
                sync.dma_start(w_qkv[:, :, 0:3 * D], dram["L0_attn_w_qkv"].rearrange("(c p) n -> p c n", p=P)
                               ).then_inc(w_loaded, 16)
                for c in range(DC):
                    sync.dma_start(w_qkv[:, c, 3 * D:], dram["L0_attn_w_ent"][c * P:(c + 1) * P, :]).then_inc(w_loaded, 16)
                sync.dma_start(w_out[:, :, :], dram["L0_attn_w_out"].rearrange("(c p) n -> p c n", p=P)
                               ).then_inc(w_loaded, 16)
                sync.dma_start(ln[:, 0, :], dram["L0_attn_ln_g_col"]).then_inc(w_loaded, 16)
                sync.dma_start(ln[:, 1, :], dram["L0_attn_ln_b_col"]).then_inc(w_loaded, 16)
                sync.dma_start(qk_bias[:, :, :], dram["L0_attn_b_qkv_col"][:, 0:4].rearrange("p (a c) -> p a c", a=2)
                               ).then_inc(w_loaded, 16)
                load_rows(sync, v_bias[0:T, :], dram["L0_attn_b_qkv"][2 * D:3 * D], w_loaded)
                load_rows(sync, o_bias[0:T, :], dram["L0_attn_b_out"], w_loaded)
                load_rows(sync, b_ent[0:T, :], dram["L0_attn_b_ent"], w_loaded)

            @block.gpsimd
            def _(pool):
                norm_root_pool(pool, n, minus_half)
                pool.wait_ge(spread2_ready, 1)
                pool.tensor_tensor(spread2[0:T, 2, :], spread2[0:T, 1, :], minus_half[0:T, :], ALU.pow).then_inc(rooted2, 1)
                attention_constants_pool(pool, a)
                attention_pool(pool, a)

            @block.scalar
            def _(act):
                act.wait_ge(w_loaded, 16 * (LOADS + 1))
                act.wait_ge(a.step, 1)
                norm_group_act(act, n, 0, a.ps_o, scale=ln[:, 0, :], shift=ln[:, 1, :])

                def group(g, last):
                    queries_keys_act(act, a, g, qk_bias[:, 0, :], qk_bias[:, 1, :])
                    if not last:
                        act.wait_ge(a.v_done, GU * (g + 1))
                        norm_group_act(act, n, g + 1, a.ps_o, scale=ln[:, 0, :], shift=ln[:, 1, :])
                    act.wait_ge(gate_in, g + 1)
                    act.activation(gate[0:T, 1, :], gate[0:T, 0, :], ACT.Exp, scale=-1.0).then_inc(gate_exp, 1)

                over_groups(act, group)
                attention_act(act, a)

            @block.tensor
            def _(pe):
                pe.wait_ge(w_loaded, 16 * (LOADS + 1))
                norm_group_pe(pe, n, 0, a.ps_o, ident)
                over_groups(pe, lambda g, last: project_group_pe(pe, a, n, g, last, w_qkv, D + 1, ident))
                pe.wait_ge(a.const_ready, attention_constants_ready(a))
                attention_pe(pe, a, ident, ident16, w_out)

            @block.vector
            def _(dve):
                attention_constants_dve(dve, a, ident)
                norm_statistics_dve(dve, n, hidden, EPS)
                steps = Chain(dve, n.step, 6)
                var, scaled_var = spread2[0:T, 0, :], spread2[0:T, 1, :]
                steps.link(dve.tensor_tensor(var, n.stat[0:T, :, 2], n.stat[0:T, :, 5], ALU.add))
                steps.link(dve.tensor_scalar(var, var, 1.0 / D, None, ALU.mult))
                steps.link(dve.scalar_tensor_tensor(var, n.tmp[0:T, 3, :], 0.25, var, ALU.mult, ALU.add))
                steps.link(dve.tensor_tensor(var, var, n.rstd[0:T, :], ALU.mult))
                steps.link(dve.tensor_tensor(var, var, n.rstd[0:T, :], ALU.mult))
                dve.tensor_scalar(scaled_var, var, 1.0, EPS2, ALU.mult, ALU.add).then_inc(spread2_ready, 1)
                dve.wait_ge(rooted2, 1)
                steps.link(dve.tensor_tensor(n.rstd[0:T, :], n.rstd[0:T, :], spread2[0:T, 2, :], ALU.mult))
                dve.wait_ge(w_loaded, 16 * (LOADS + 1))
                dve.wait_ge(a.step, 1)
                steps = GroupSteps(dve, a.step, 1, 7)
                norm_group_dve(dve, n, 0, hidden)

                def group(g, last):
                    steps.begin(g)
                    if not last:
                        norm_group_dve(dve, n, g + 1, hidden)
                    for u in range(GU):
                        dve.wait_ge(a.v_done, GU * g + u + 1)
                        steps.link(dve.tensor_tensor(gate[0:T, 0, u:u + 1], a.ps_g[0:T, u % 2, D:D + 1], b_ent[0:T, :],
                                                     ALU.add))
                        dve.tensor_tensor(a.v[0:T, GU * g + u, :, 0:HD],
                                          a.ps_g[0:T, u % 2, 0:D].rearrange("p (h e) -> p h e", h=HEADS),
                                          v_bias[0:T, :].rearrange("p (h e) -> p h e", h=HEADS),
                                          ALU.add).then_inc(a.v_ready, 1)
                    dve.sem_inc(gate_in, 1)
                    dve.wait_ge(gate_exp, g + 1)
                    steps.link(dve.tensor_scalar(gate[0:T, 1, :], gate[0:T, 1, :], 1.0, None, ALU.add))
                    steps.link(dve.reciprocal(gate[0:T, 2, :], gate[0:T, 1, :]))
                    steps.link(dve.tensor_scalar(gate[0:T, 2, :], gate[0:T, 2, :], 0.1, 2.0, ALU.max, ALU.min))
                    dve.wait_ge(a.v_ready, GU * g + GU)
                    for u in range(GU):
                        dve.tensor_scalar(a.v[0:T, GU * g + u, :, 0:HD], a.v[0:T, GU * g + u, :, 0:HD], gate[0:T, 2, u:u + 1],
                                          None, ALU.mult).then_inc(a.v_gated, 1)
                    steps.end()

                over_groups(dve, group)
                steps = GroupSteps(dve, a.step, 1 + 7 * G, 2)

                def context(b, buf):
                    outputs = a.ps_o[0:T, buf, 0:HEADS * (HD + 1)].rearrange("p (h e) -> p h e", h=HEADS)
                    steps.link(dve.reciprocal(a.rden[0:T, 0, :], outputs[:, :, HD]))
                    steps.link(dve.tensor_tensor(a.ctx[0:T, buf, :].rearrange("p (h e) -> p h e", h=HEADS),
                                                 outputs[:, :, 0:HD],
                                                 a.rden[0:T, 0, :].unsqueeze(2).broadcast_to([T, HEADS, HD]), ALU.mult))
                    dve.sem_inc(a.ctx_ready, 1)
                    dve.sem_inc(a.outputs_read, 1)

                def add(b):
                    dve.wait_ge(a.out_done, b + 1)
                    dve.tensor_tensor(summed[0:T, :], a.ps_g[0:T, 0, 0:D], o_bias[0:T, :], ALU.add).then_inc(a.biased, 1)
                    dve.wait_ge(a.biased, b + 1)
                    dve.scalar_tensor_tensor(hidden[0:T, b, :], summed[0:T, :], OUT_SCALE, hidden[0:T, b, :], ALU.mult,
                                             ALU.add).then_inc(a.added, 1)

                dve.wait_ge(a.const_ready, attention_constants_ready(a))
                attention_dve(dve, a, steps, context, add, shared=shared)





def quantised_linear(nc, shared, dram):
    hidden, ident, ident16, minus_half = (shared[k] for k in ("hidden", "ident", "ident16", "minus_half"))
    TE = T + 1
    with Scope(nc, "quant") as s:
        n = Norm(s, shared["stat"])
        x1 = s.sb("x1", [P, B, D])
        w_int = s.sb("w_int", [P, DC, D // 4], mybir.dt.int32)
        w = s.sb("w", [P, DC, D], BF16)
        w_scale = s.sb("w_scale", [P, D])
        bias = s.sb("bias", [P, D])
        largest = s.sb("largest", [P, B])
        most = s.sb("most", [P, 2])
        x_scale = s.sb("x_scale", [P, 2])
        xs = s.sb("xs", [P, GU, D])
        xq = s.sb("xq", [P, GU, D], BF16)
        xqT = s.sb("xqT", [P, GU * DC * TE], BF16)
        scaled = s.sb("scaled", [P, GU, D])
        ps_t = s.ps("turned", [P, 512])
        ps_y = s.ps("product", [P, GU, D])
        w_loaded, w_ready, x1_ready, found, most_ready, step, rounded, xq_turned, xqT_ready, multiplied, scaled_ready, added = (
            s.sem(k) for k in ("w_loaded", "w_ready", "x1_ready", "found", "most_ready", "step", "rounded", "xq_turned",
                               "xqT_ready", "multiplied", "scaled_ready", "added"))
        with nc.Block() as block:
            @block.sync
            def _(sync):
                sync.dma_start(w_int[:, :, :], dram["L0_ffn_weight_int8"].rearrange("(c p) n -> p c n", p=P)
                               ).then_inc(w_loaded, 16)
                load_rows(sync, w_scale[0:T, :], dram["L0_ffn_weight_scale"].rearrange("n a -> (n a)"), w_loaded)
                load_rows(sync, bias[0:T, :], dram["L0_ffn_bias"], w_loaded)

            @block.gpsimd
            def _(pool):
                pool.memset(most[:, :], 0.0).then_inc(most_ready, 1)
                norm_root_pool(pool, n, minus_half)
                pool.wait_ge(found, 1)
                pool.partition_all_reduce(most[:, 1:2], most[:, 0:1], P, bass.bass_isa.ReduceOp.max).then_inc(most_ready, 1)

            @block.scalar
            def _(act):
                with act.Fori(0, G) as g:
                    act.wait_ge(xq_turned, g + 1)
                    act.wait_ge(multiplied, g)
                    act.activation(xqT[:, :], ps_t[:, :].bitcast(BF16)[:, 0:GU * DC * TE], ACT.Copy).then_inc(xqT_ready, 1)

            @block.tensor
            def _(pe):
                def turn(g):
                    pe.wait_ge(rounded, g + 1)
                    for k in range(GU * DC):
                        mm = pe.transpose(ps_t[:, :].bitcast(BF16)[:, k * TE:k * TE + T],
                                          xq[0:T, k // DC, k % DC * P:(k % DC + 1) * P], ident16[0:T, 0:T])
                    mm.then_inc(xq_turned, 1)

                def group(g, last):
                    pe.wait_ge(xqT_ready, g + 1)
                    if not last:
                        turn(g + 1)
                    pe.wait_ge(scaled_ready, g)
                    for u in range(GU):
                        for c in range(DC):
                            k = DC * u + c
                            mm = pe.matmul(ps_y[0:T, u, :], xqT[:, k * TE:k * TE + T], w[:, c, :], start=(c == 0),
                                           stop=(c == DC - 1), skip_group_check=True)
                    mm.then_inc(multiplied, 1)

                pe.wait_ge(w_ready, 1)
                turn(0)
                over_groups(pe, group)

            @block.vector
            def _(dve):
                norm_statistics_dve(dve, n, hidden, 1e-5)
                with dve.Fori(0, G) as g:
                    for u in range(GU):
                        b = GU * g + u
                        dve.tensor_scalar(x1[0:T, b, :], hidden[0:T, b, :], n.mean[0:T, bass.ds(b, 1)],
                                          n.rstd[0:T, bass.ds(b, 1)], ALU.subtract, ALU.mult).then_inc(x1_ready, 1)
                    dve.wait_ge(x1_ready, GU * g + GU)
                    at = bass.ds(GU * g, GU)
                    dve.tensor_reduce(largest[0:T, at], x1[0:T, at, :], AX.X, ALU.max, apply_absolute_value=True).then_inc(step, 1)
                dve.wait_ge(w_loaded, 48)
                for c in range(DC):
                    ins = dve.tensor_copy(w[:, c, :], w_int[:, c, :].bitcast(I8))
                ins.then_inc(w_ready, 1)
                dve.wait_ge(step, G)
                dve.wait_ge(most_ready, 1)
                dve.tensor_reduce(most[0:T, 0:1], largest[0:T, :], AX.X, ALU.max).then_inc(found, 1)
                dve.wait_ge(most_ready, 2)
                steps = Chain(dve, step, G)
                steps.link(dve.tensor_scalar(x_scale[:, 0:1], most[:, 1:2], 1.0 / 127.0, 1e-5, ALU.mult, ALU.max))
                steps.link(dve.reciprocal(x_scale[:, 1:2], x_scale[:, 0:1]))
                steps = GroupSteps(dve, step, G + 2, 2)
                wide = [T, GU, D]

                def quantise(g):
                    steps.begin(g)
                    dve.wait_ge(rounded, g)
                    x = xs[0:T, :, :]
                    steps.link(dve.tensor_scalar(x, x1[0:T, bass.ds(GU * g, GU), :], x_scale[0:T, 1:2], -128.0, ALU.mult, ALU.max))
                    steps.link(dve.tensor_scalar(x, x, 127.0, ROUND, ALU.min, ALU.add))
                    steps.end()
                    dve.wait_ge(xq_turned, g)
                    dve.tensor_scalar(xq[0:T, :, :], x, ROUND, None, ALU.subtract).then_inc(rounded, 1)

                def group(g, last):
                    if not last:
                        quantise(g + 1)
                    y = scaled[0:T, :, :]
                    dve.wait_ge(multiplied, g + 1)
                    dve.scalar_tensor_tensor(y, ps_y[0:T, :, :], x_scale[0:T, 0:1], w_scale[0:T, :].unsqueeze(1).broadcast_to(wide),
                                             ALU.mult, ALU.mult).then_inc(scaled_ready, 1)
                    dve.wait_ge(scaled_ready, g + 1)
                    dve.tensor_tensor(y, y, bias[0:T, :].unsqueeze(1).broadcast_to(wide), ALU.add).then_inc(added, 1)
                    dve.wait_ge(added, 2 * g + 1)
                    at = bass.ds(GU * g, GU)
                    dve.tensor_tensor(hidden[0:T, at, :], hidden[0:T, at, :], y, ALU.add).then_inc(added, 1)
                    for u in range(GU):
                        measure_dve(dve, shared, GU * g + u, added, 2 * g + 2)

                quantise(0)
                over_groups(dve, group)



def frequency_linear(nc, shared, dram):
    hidden, ident, minus_half = (shared[k] for k in ("hidden", "ident", "minus_half"))
    with Scope(nc, "freq") as s:
        n = Norm(s, shared["stat"])
        dft = s.sb("dft", [P, 2, DC, D])
        minus_sin = s.sb("minus_sin", [P, DC, D])
        back = s.sb("back", [P, 2, DC, D])
        w_freq = s.sb("w_freq", [P, 2, DC, D])
        folded = s.sb("folded", [P, 2, DC, D])
        m = s.sb("m", [P, DC, D])
        bias = s.sb("bias", [P, D])
        summed = s.sb("summed", [P, 2, D])
        ps_t = s.ps("turned", [P, 2, 512])
        ps_y = s.ps("product", [P, 2, 512])
        w_loaded, prepared, fold_done, fold_ready, y_done, step, added = (
            s.sem(k) for k in ("w_loaded", "prepared", "fold_done", "fold_ready", "y_done", "step", "added"))
        with nc.Block() as block:
            @block.sync
            def _(sync):
                for k in range(2):
                    sync.dma_start(dft[:, k, :, :], dram["dft"][k].rearrange("(c p) n -> p c n", p=P)).then_inc(w_loaded, 16)
                for k, name in enumerate(("L1_ffn_w_freq_real", "L1_ffn_w_freq_imag")):
                    sync.dma_start(w_freq[:, k, :, :], dram[name].rearrange("(c p) n -> p c n", p=P)).then_inc(w_loaded, 16)
                load_rows(sync, bias[0:T, :], dram["L1_ffn_bias"], w_loaded)

            @block.gpsimd
            def _(pool):
                norm_root_pool(pool, n, minus_half)

            @block.scalar
            def _(act):
                act.wait_ge(w_loaded, 80)
                act.activation(minus_sin[:, :, :], dft[:, 1, :, :], ACT.Copy, scale=-1.0).then_inc(prepared, 1)
                act.activation(back[:, 0, :, :], dft[:, 0, :, :], ACT.Copy, scale=1.0 / D).then_inc(prepared, 1)
                act.activation(back[:, 1, :, :], dft[:, 1, :, :], ACT.Copy, scale=-1.0 / D).then_inc(prepared, 1)
                for k in range(4):
                    act.wait_ge(fold_done, k + 1)
                    act.activation(folded[:, k // 2, k % 2, :], ps_y[:, k % 2, 0:D], ACT.Copy).then_inc(fold_ready, 1)
                for k in range(2):
                    act.wait_ge(fold_done, 5 + k)
                    act.activation(m[:, k, :], ps_y[:, k, 0:D], ACT.Copy).then_inc(fold_ready, 1)
                with act.Fori(0, G) as g:
                    act.wait_ge(y_done, GU * g)
                    norm_group_act(act, n, g, ps_t)

            @block.tensor
            def _(pe):
                pe.wait_ge(w_loaded, 80)
                pe.wait_ge(prepared, 3)
                for k, terms in enumerate((((0, dft[:, 0]), (1, dft[:, 1])), ((1, dft[:, 0]), (0, minus_sin)))):
                    for row in range(DC):
                        if k:
                            pe.wait_ge(fold_ready, row + 1)
                        for t, (part, right) in enumerate(terms):
                            for c in range(DC):
                                mm = pe.matmul(ps_y[:, row, 0:D], w_freq[:, part, c, row * P:(row + 1) * P], right[:, c, :],
                                               start=(t == 0 and c == 0), stop=(t == 1 and c == DC - 1))
                        mm.then_inc(fold_done, 1)
                pe.wait_ge(fold_ready, 4)
                for row in range(DC):
                    for t in range(2):
                        for c in range(DC):
                            mm = pe.matmul(ps_y[:, row, 0:D], folded[:, t, c, row * P:(row + 1) * P], back[:, t, c, :],
                                           start=(t == 0 and c == 0), stop=(t == 1 and c == DC - 1))
                    mm.then_inc(fold_done, 1)
                pe.wait_ge(fold_ready, 6)
                norm_group_pe(pe, n, 0, ps_t, ident)

                def group(g, last):
                    pe.wait_ge(n.xT_ready, 2 * g + 2)
                    for u in range(GU):
                        if u == GU - 1 and not last:
                            norm_group_pe(pe, n, g + 1, ps_t, ident)
                        if u < 2:
                            pe.wait_ge(added, GU * g)
                        else:
                            pe.wait_ge(added, GU * g + u - 1)
                        for c in range(DC):
                            mm = pe.matmul(ps_y[0:T, u % 2, 0:D], n.xT[:, c, u * T:(u + 1) * T], m[:, c, :],
                                           start=(c == 0), stop=(c == DC - 1))
                        mm.then_inc(y_done, 1)

                over_groups(pe, group)

            @block.vector
            def _(dve):
                norm_statistics_dve(dve, n, hidden, 1e-5, True)
                dve.wait_ge(w_loaded, 80)
                steps = GroupSteps(dve, step, 0, GU)
                norm_group_dve(dve, n, 0, hidden)

                def group(g, last):
                    steps.begin(g)
                    if not last:
                        norm_group_dve(dve, n, g + 1, hidden)
                    for u in range(GU):
                        dve.wait_ge(y_done, GU * g + u + 1)
                        steps.link(dve.tensor_tensor(summed[0:T, u % 2, :], ps_y[0:T, u % 2, 0:D], bias[0:T, :], ALU.add))
                        dve.tensor_tensor(hidden[0:T, GU * g + u, :], hidden[0:T, GU * g + u, :], summed[0:T, u % 2, :],
                                          ALU.add).then_inc(added, 1)
                        if u:
                            measure_dve(dve, shared, GU * g + u - 1, added, GU * g + u)
                    measure_dve(dve, shared, GU * g + GU - 1, added, GU * g + GU)
                    steps.end()

                over_groups(dve, group)



def reshaped_projection(nc, shared, dram):
    hidden, ident, minus_half = (shared[k] for k in ("hidden", "ident", "minus_half"))
    with Scope(nc, "rproj") as s:
        n = Norm(s, shared["stat"])
        w_qkv = s.sb("w_qkv", [P, DC, 3 * D])
        bias = s.sb("bias", [P, 3 * D])
        rows = s.sb("rows", [P, 2, 3, D])
        ps_t = s.ps("xturned", [P, 2, 512])
        ps_y = s.ps("product", [P, 2, 2, 512])
        w_loaded, y_done, y_copied = (s.sem(k) for k in ("w_loaded", "y_done", "y_copied"))
        stored = [s.sem(f"stored{j}") for j in range(2)]
        qkv = shared["qkv"]
        with nc.Block() as block:
            @block.sync
            def _(sync):
                sync.dma_start(w_qkv[:, :, :], dram["L1_attn_Wqkv"].rearrange("(c p) n -> p c n", p=P)).then_inc(w_loaded, 16)
                load_rows(sync, bias[0:T, :], dram["L1_attn_bqkv"], w_loaded)
                with sync.Fori(0, B // 2) as i:
                    for j in range(2):
                        sync.wait_ge(y_copied, 4 * i + 2 * j + 2)
                        sync.dma_start(qkv[bass.ds(2 * i + j, 1), :, :, :].rearrange("b a t d -> t (b a) d"),
                                       rows[0:T, j, :, :]).then_inc(stored[j], 16)
                for j in range(2):
                    sync.wait_ge(stored[j], 16 * (B // 2))

            @block.gpsimd
            def _(pool):
                norm_root_pool(pool, n, minus_half)

            @block.scalar
            def _(act):
                with act.Fori(0, G) as g:
                    act.wait_ge(y_done, GU * g)
                    norm_group_act(act, n, g, ps_t)

            @block.tensor
            def _(pe):
                pe.wait_ge(w_loaded, 32)
                norm_group_pe(pe, n, 0, ps_t, ident)

                def group(g, last):
                    pe.wait_ge(n.xT_ready, 2 * g + 2)
                    for u in range(GU):
                        if u == GU - 1 and not last:
                            norm_group_pe(pe, n, g + 1, ps_t, ident)
                        if u < 2:
                            pe.wait_ge(y_copied, 2 * GU * g)
                        else:
                            pe.wait_ge(y_copied, 2 * (GU * g + u - 1))
                        for bank, (at, size) in enumerate(((0, 2 * D), (2 * D, D))):
                            for c in range(DC):
                                mm = pe.matmul(ps_y[0:T, u % 2, bank, 0:size], n.xT[:, c, u * T:(u + 1) * T],
                                               w_qkv[:, c, at:at + size], start=(c == 0), stop=(c == DC - 1))
                        mm.then_inc(y_done, 1)

                over_groups(pe, group)

            @block.vector
            def _(dve):
                norm_statistics_dve(dve, n, hidden, 1e-5, True)
                dve.wait_ge(w_loaded, 32)
                norm_group_dve(dve, n, 0, hidden)

                def group(g, last):
                    if not last:
                        norm_group_dve(dve, n, g + 1, hidden)
                    for u in range(GU):
                        dve.wait_ge(y_done, GU * g + u + 1)
                        if u < 2:
                            dve.wait_ge(stored[u], 32 * g)
                        else:
                            dve.wait_ge(stored[u % 2], 32 * g + 16)
                        dve.tensor_tensor(rows[0:T, u % 2, 0:2, :].rearrange("p a d -> p (a d)"), ps_y[0:T, u % 2, 0, 0:2 * D],
                                          bias[0:T, 0:2 * D], ALU.add).then_inc(y_copied, 1)
                        dve.tensor_tensor(rows[0:T, u % 2, 2, :], ps_y[0:T, u % 2, 1, 0:D], bias[0:T, 2 * D:],
                                          ALU.add).then_inc(y_copied, 1)

                over_groups(dve, group)


def reshaped_attention(nc, shared, dram):
    hidden, ident, ident16 = (shared[k] for k in ("hidden", "ident", "ident16"))
    with Scope(nc, "rattn") as s:
        a = Attention(s, HEADS, True, 1.0 / math.sqrt(HD))
        w_out = s.sb("w_out", [P, DC, D])
        o_bias = s.sb("o_bias", [P, D])
        heads = s.sb("heads", [P, 2, GU, 3, D])
        summed = s.sb("summed", [P, D])
        w_loaded = s.sem("w_loaded")
        heads_loaded = [s.sem(f"heads_loaded{j}") for j in range(2)]
        heads_used = s.sem("heads_used")
        LOADS = 2
        source = shared["qkv"].rearrange("b a t d -> b a (t d)").rearrange("b a (h t e) -> b t a h e", h=HEADS, e=HD)
        with nc.Block() as block:
            @block.sync
            def _(sync):
                sync.dma_start(w_out[:, :, :], dram["L1_attn_Wproj"].rearrange("(c p) n -> p c n", p=P)).then_inc(w_loaded, 16)
                load_rows(sync, o_bias[0:T, :], dram["L1_attn_bproj"], w_loaded)
                with sync.Fori(0, G // 2) as i:
                    for j in range(2):
                        sync.wait_ge(heads_used, 2 * i + j + 1)
                        for u in range(GU):
                            for part in range(3):
                                sync.dma_start(heads[0:T, j, u, part, :].rearrange("p (h e) -> p h e", h=HEADS),
                                               source[bass.ds(2 * GU * i + GU * j + u, 1), :, part, :, :].rearrange(
                                                   "b t h e -> (b t) h e")).then_inc(heads_loaded[j], 16)

            @block.gpsimd
            def _(pool):
                attention_constants_pool(pool, a)
                attention_pool(pool, a)

            @block.scalar
            def _(act):
                with act.Fori(0, G) as g:
                    queries_keys_act(act, a, g, None, None)
                attention_act(act, a)

            @block.tensor
            def _(pe):
                pe.wait_ge(w_loaded, 16 * LOADS)
                with pe.Fori(0, G // 2) as i:
                    for j in range(2):
                        g = 2 * i + j
                        pe.wait_ge(heads_loaded[j], 16 * 3 * GU * (i + 1))
                        for what, (bank, done, read) in enumerate(((a.ps_s, a.q_done, a.q_ready), (a.ps_t, a.k_done, a.k_ready))):
                            for m in range(DC):
                                pe.wait_ge(read, DC * g)
                                for u in range(GU):
                                    mm = pe.transpose(bank[:, m, u * T:(u + 1) * T],
                                                      heads[0:T, j, u, what, m * P:(m + 1) * P], ident[0:T, 0:T])
                                mm.then_inc(done, 1)
                pe.wait_ge(a.const_ready, attention_constants_ready(a))
                attention_pe(pe, a, ident, ident16, w_out)

            @block.vector
            def _(dve):
                dve.sem_inc(heads_used, 2)
                attention_constants_dve(dve, a, ident)
                dve.wait_ge(w_loaded, 16 * LOADS)
                dve.wait_ge(a.step, 1)
                with dve.Fori(0, G // 2) as i:
                    for j in range(2):
                        g = 2 * i + j
                        dve.wait_ge(heads_loaded[j], 16 * 3 * GU * (i + 1))
                        dve.wait_ge(a.k_done, 2 * g + 2)
                        for u in range(GU):
                            dve.tensor_copy(a.v[0:T, GU * g + u, :, 0:HD],
                                            heads[0:T, j, u, 2, :].rearrange("p (h e) -> p h e", h=HEADS)).then_inc(a.v_ready, 1)
                        dve.wait_ge(a.v_ready, GU * g + GU)
                        dve.sem_inc(heads_used, 1)
                steps = GroupSteps(dve, a.step, 1, 2)

                def context(b, buf):
                    outputs = a.ps_o[0:T, buf, 0:HEADS * (HD + 1)].rearrange("p (h e) -> p h e", h=HEADS)
                    steps.link(dve.reciprocal(a.rden[0:T, 0, :], outputs[:, :, HD]))
                    steps.link(dve.tensor_tensor(a.ctx[0:T, buf, :].rearrange("p (h e) -> p h e", h=HEADS),
                                                 outputs[:, :, 0:HD],
                                                 a.rden[0:T, 0, :].unsqueeze(2).broadcast_to([T, HEADS, HD]), ALU.mult))
                    dve.sem_inc(a.ctx_ready, 1)
                    dve.sem_inc(a.outputs_read, 1)

                def add(b):
                    dve.wait_ge(a.out_done, b + 1)
                    dve.tensor_tensor(summed[0:T, :], a.ps_g[0:T, 0, 0:D], o_bias[0:T, :], ALU.add).then_inc(a.biased, 1)
                    dve.wait_ge(a.biased, b + 1)
                    dve.tensor_tensor(hidden[0:T, b, :], hidden[0:T, b, :], summed[0:T, :], ALU.add).then_inc(a.added, 1)

                dve.wait_ge(a.const_ready, attention_constants_ready(a))
                attention_dve(dve, a, steps, context, add, shared=shared)



def differential_attention(nc, shared, dram):
    hidden, ident, ident16, minus_half = (shared[k] for k in ("hidden", "ident", "ident16", "minus_half"))
    LAMBDA_INIT, EPS = 0.8 - 0.6 * math.exp(0.0), 1e-5
    MAPS = 2 * HEADS
    with Scope(nc, "dattn") as s:
        n = Norm(s, shared["stat"])
        a = Attention(s, MAPS, True, 1.0 / (D // MAPS))
        w_qkv = s.sb("w_qkv", [P, DC, 3 * D])
        w_out = s.sb("w_out", [P, DC, D])
        lam = s.sb("lam", [P, 4, 8])
        lam_s = s.sb("lam_s", [P, 6])
        gamma = s.sb("gamma", [P, 2])
        diff = s.sb("diff", [P, 2, D])
        square = s.sb("square", [P, 3, HEADS])
        w_loaded, lam_summed, lam_exp, gamma_ready, ms_ready, rms_ready = (
            s.sem(k) for k in ("w_loaded", "lam_summed", "lam_exp", "gamma_ready", "ms_ready", "rms_ready"))
        LOADS = 6 + P // HD
        with nc.Block() as block:
            @block.sync
            def _(sync):
                sync.dma_start(w_qkv[:, :, :], dram["L2_attn_w_attn"].rearrange("(c p) n -> p c n", p=P)).then_inc(w_loaded, 16)
                sync.dma_start(w_out[:, :, :], dram["L2_attn_w_proj"].rearrange("(c p) n -> p c n", p=P)).then_inc(w_loaded, 16)
                for k, name in enumerate(("q1", "k1", "q2", "k2")):
                    load_rows(sync, lam[0:T, k, :], dram[f"L2_attn_lambda_{name}"], w_loaded)
                for k in range(P // HD):
                    sync.dma_start(gamma[k * HD:(k + 1) * HD, 0:1], dram["L2_attn_gamma"].rearrange("(e a) -> e a", a=1)
                                   ).then_inc(w_loaded, 16)

            @block.gpsimd
            def _(pool):
                norm_root_pool(pool, n, minus_half)
                attention_constants_pool(pool, a)

                def root(b):
                    pool.wait_ge(ms_ready, b + 1)
                    pool.tensor_tensor(square[0:T, 2, :], square[0:T, 1, :], minus_half[0:T, 0:HEADS],
                                       ALU.pow).then_inc(rms_ready, 1)

                attention_pool(pool, a, root)

            @block.scalar
            def _(act):
                act.wait_ge(w_loaded, 16 * LOADS)
                act.activation(gamma[:, 1:2], gamma[:, 0:1], ACT.Copy, scale=1.0 - LAMBDA_INIT).then_inc(gamma_ready, 1)
                act.wait_ge(lam_summed, 2)
                act.activation(lam_s[0:T, 2:4], lam_s[0:T, 0:2], ACT.Exp).then_inc(lam_exp, 1)
                act.wait_ge(gamma_ready, 1)
                act.wait_ge(a.step, 1)
                norm_group_act(act, n, 0, a.ps_o)

                def group(g, last):
                    queries_keys_act(act, a, g, None, None)
                    if not last:
                        act.wait_ge(a.v_done, GU * (g + 1))
                        norm_group_act(act, n, g + 1, a.ps_o)

                over_groups(act, group)
                attention_act(act, a, ctx_scale=gamma[:, 1:2])

            @block.tensor
            def _(pe):
                pe.wait_ge(w_loaded, 16 * LOADS)
                norm_group_pe(pe, n, 0, a.ps_o, ident)
                over_groups(pe, lambda g, last: project_group_pe(pe, a, n, g, last, w_qkv, D, ident))
                pe.wait_ge(a.const_ready, attention_constants_ready(a))
                attention_pe(pe, a, ident, ident16, w_out)

            @block.vector
            def _(dve):
                attention_constants_dve(dve, a, ident)
                norm_statistics_dve(dve, n, hidden, 1e-5, True)
                dve.wait_ge(w_loaded, 16 * LOADS)
                dve.wait_ge(a.step, 1)
                steps = Chain(dve, a.step, 1)
                for k in range(2):
                    steps.link(dve.tensor_tensor(lam[0:T, 2 * k, :], lam[0:T, 2 * k, :], lam[0:T, 2 * k + 1, :], ALU.mult))
                    dve.tensor_reduce(lam_s[0:T, k:k + 1], lam[0:T, 2 * k, :], AX.X, ALU.add).then_inc(lam_summed, 1)
                dve.wait_ge(lam_exp, 1)
                steps.link(dve.tensor_tensor(lam_s[0:T, 4:5], lam_s[0:T, 3:4], lam_s[0:T, 2:3], ALU.subtract))
                steps.link(dve.tensor_scalar(lam_s[0:T, 5:6], lam_s[0:T, 4:5], LAMBDA_INIT, None, ALU.subtract))
                minus_lambda = lam_s[0:T, 5:6]
                norm_group_dve(dve, n, 0, hidden)

                def group(g, last):
                    if not last:
                        norm_group_dve(dve, n, g + 1, hidden)
                    for u in range(GU):
                        dve.wait_ge(a.v_done, GU * g + u + 1)
                        dve.tensor_copy(a.v[0:T, GU * g + u, :, 0:HD],
                                        a.ps_g[0:T, u % 2, 0:D].rearrange("p (h e) -> p h e", h=HEADS)).then_inc(a.v_ready, 1)

                over_groups(dve, group)
                steps = GroupSteps(dve, a.step, 5, 6)
                d0, d1 = (diff[0:T, k, :].rearrange("p (h e) -> p h e", h=HEADS) for k in range(2))
                wide = lambda x: x.unsqueeze(2).broadcast_to([T, HEADS, HD])

                def context(b, buf):
                    first, second = (a.ps_o[0:T, k, 0:HEADS * (HD + 1)].rearrange("p (h e) -> p h e", h=HEADS)
                                     for k in range(2))
                    dve.reciprocal(a.rden[0:T, 0, :], first[:, :, HD])
                    steps.link(dve.reciprocal(a.rden[0:T, 1, :], second[:, :, HD]))
                    steps.link(dve.tensor_scalar(a.rden[0:T, 1, :], a.rden[0:T, 1, :], minus_lambda, None, ALU.mult))
                    dve.tensor_tensor(d0, first[:, :, 0:HD], wide(a.rden[0:T, 0, :]), ALU.mult)
                    dve.tensor_tensor(d1, second[:, :, 0:HD], wide(a.rden[0:T, 1, :]), ALU.mult).then_inc(a.outputs_read, 1)
                    dve.wait_ge(a.outputs_read, b + 2)
                    steps.link(dve.tensor_tensor(d0, d0, d1, ALU.add))
                    steps.link(dve.tensor_tensor(d1, d0, d0, ALU.mult))
                    steps.link(dve.tensor_reduce(square[0:T, 0, :], d1, AX.X, ALU.add))
                    steps.link(dve.tensor_scalar(square[0:T, 1, :], square[0:T, 0, :], 1.0 / HD, EPS, ALU.mult, ALU.add))
                    dve.sem_inc(ms_ready, 1)

                def finish(b, buf):
                    dve.wait_ge(rms_ready, b + 1)
                    dve.tensor_tensor(a.ctx[0:T, buf, :].rearrange("p (h e) -> p h e", h=HEADS), d0,
                                      wide(square[0:T, 2, :]), ALU.mult).then_inc(a.ctx_ready, 1)

                def add(b):
                    dve.wait_ge(a.out_done, b + 1)
                    dve.tensor_tensor(hidden[0:T, b, :], a.ps_g[0:T, 0, 0:D], hidden[0:T, b, :], ALU.add).then_inc(a.added, 1)

                dve.wait_ge(a.const_ready, attention_constants_ready(a))
                attention_dve(dve, a, steps, context, add, finish, shared)


def layer1_attention(nc, shared, dram):
    shared["qkv"] = nc.dram_tensor("qkv_rows", (B, 3, T, D), F32, kind="Internal").ap()
    reshaped_projection(nc, shared, dram)
    reshaped_attention(nc, shared, dram)



def choose_two_dve(dve, steps, score, rows, wide_shape, restart, work, chosen):
    top, hit, rank, first = work["top"], work["hit"], work["rank"], work["first"]
    flat = lambda x: x[rows, :, :].rearrange("p b e -> p (b e)")
    left = score
    for k in range(2):
        steps.link(dve.tensor_reduce(top[rows, :], left[rows, :, :], AX.X, ALU.max))
        steps.link(dve.tensor_tensor(hit[rows, :, :], left[rows, :, :],
                                     top[rows, :].unsqueeze(2).broadcast_to(wide_shape), ALU.is_equal))
        steps.link(dve.tensor_tensor_scan(flat(rank), flat(restart), flat(hit), 0.0, ALU.mult, ALU.add))
        steps.link(dve.scalar_tensor_tensor(first[k][rows, :, :], rank[rows, :, :], 1.0, hit[rows, :, :],
                                            ALU.is_equal, ALU.mult))
        if k == 0:
            steps.link(dve.scalar_tensor_tensor(work["left"][rows, :, :], first[0][rows, :, :], MASKED,
                                                left[rows, :, :], ALU.mult, ALU.add))
            left = work["left"]
    steps.link(dve.tensor_tensor(chosen[rows, :, :], first[0][rows, :, :], first[1][rows, :, :], ALU.add))


def choice_buffers(s, sets, experts):
    work = {k: s.sb(f"choice_{k}", [P, sets, experts]) for k in ("hit", "rank", "left", "first0", "first1")}
    work["first"] = [work["first0"], work["first1"]]
    work["top"] = s.sb("choice_top", [P, sets])
    return work



def split_products(pe, out, w, x, start, stop):
    (w_high, w_low), (x_high, x_low) = w, x
    pe.matmul(out, w_high, x_high, start=start, stop=False)
    pe.matmul(out, w_high, x_low, start=False, stop=False)
    return pe.matmul(out, w_low, x_high, start=False, stop=stop)


def mixture(nc, shared, dram):
    hidden, ident, minus_half = (shared[k] for k in ("hidden", "ident", "minus_half"))
    E, F = 8, 1024
    FC = F // P
    PAIRS = FC // 2
    with Scope(nc, "moe") as s:
        n = Norm(s, shared["stat"])
        x_part = [s.sb(f"x_part{k}", [P, DC, B * T], BF16) for k in range(2)]
        w_router = s.sb("w_router", [P, DC, E])
        w1_in = s.sb("w1_in", [P, DC, F])
        w2_in = s.sb("w2_in", [P, FC, D])
        w1 = [s.sb(f"w1_part{k}", [P, 2, DC, F], BF16) for k in range(2)]
        w2 = [s.sb(f"w2_part{k}", [P, 2, FC, D], BF16) for k in range(2)]
        gelu = s.sb("gelu", [P, 2, 2, GT])
        act1 = [s.sb(f"act1_part{k}", [P, FC, GT], BF16) for k in range(2)]
        token_weight = s.sb("token_weight", [P, 2, GT])
        weighted = s.sb("weighted", [P, DC, GT])
        total_out = s.sb("total_out", [P, DC, B * T])
        logits = s.sb("logits", [P, B, E])
        prob = s.sb("prob", [P, B, E])
        chosen = s.sb("chosen", [P, B, E])
        weight = s.sb("weight", [P, B, E])
        weightT = s.sb("weightT", [P, 2, T])
        restart = s.sb("restart", [P, B, E])
        one = s.sb("one", [P, 1])
        total = s.sb("total", [P, 2, B])
        work = choice_buffers(s, B, E)
        ps_h = s.ps("hidden", [P, 4, 512])
        ps_y = s.ps("product", [P, 4, 512])
        ps_out = ps_h[:, :, :].rearrange("p b (u d) -> p (b u) d", d=D)
        names = ("router_loaded restart_ready x_high_ready x_low_ready routed logits_ready step prob_in prob_exp weight_ready "
                 "weight_turned weightT_ready weight_stored w_loaded w_split expert_ready h_done high_ready low_ready y_done y_read "
                 "summed_up expert_used outT_ready out_turned out_added").split()
        sem = {k: s.sem(k) for k in names}
        (router_loaded, restart_ready, x_high_ready, x_low_ready, routed, logits_ready, step, prob_in, prob_exp, weight_ready,
         weight_turned, weightT_ready, weight_stored, w_loaded, w_split, expert_ready, h_done, high_ready, low_ready, y_done, y_read,
         summed_up, expert_used, outT_ready, out_turned, out_added) = (sem[k] for k in names)
        token_weight_loaded = [s.sem(f"token_weight_loaded{j}") for j in range(2)]
        scratch = nc.dram_tensor("token_weights", (B, E, T), F32, kind="Internal").ap()
        with nc.Block() as block:
            @block.sync
            def _(sync):
                sync.dma_start(w_router[:, :, :], dram["L2_ffn_Wr"].rearrange("(c p) n -> p c n", p=P)).then_inc(router_loaded, 16)
                sync.wait_ge(weightT_ready, 1)
                for k in range(2):
                    sync.dma_start(scratch[k * B // 2:(k + 1) * B // 2, :, :].rearrange("b e t -> (b e) t"),
                                   weightT[:, k, :]).then_inc(weight_stored, 16)
                sync.wait_ge(weight_stored, 32)
                with sync.Fori(0, E) as e:
                    with sync.Fori(0, G // 2) as i:
                        for j in range(2):
                            sync.wait_ge(y_read, e * G + 2 * i + j + 1)
                            sync.dma_start(token_weight[:, j, :].rearrange("p (u t) -> p u t", u=GU),
                                           scratch[bass.ds(2 * GU * i + GU * j, GU), bass.ds(e, 1), :].rearrange(
                                               "b e t -> (b e) t").partition_broadcast(P)).then_inc(token_weight_loaded[j], 16)

            @block.gpsimd
            def _(pool):
                pool.memset(restart[:, :, :], 1.0).then_inc(restart_ready, 1)
                pool.wait_ge(restart_ready, 1)
                pool.memset(restart[:, :, 0:1], 0.0).then_inc(restart_ready, 1)
                norm_root_pool(pool, n, minus_half)
                pool.memset(one[:, :], 1.0).then_inc(restart_ready, 1)
                pool.wait_ge(restart_ready, 3)
                pool.memset(total_out[:, :, :], 0.0).then_inc(summed_up, 1)
                with pool.Fori(0, E // 2) as i:
                    for j in range(2):
                        e = 2 * i + j
                        pool.dma_start(w1_in[:, :, :], dram["L2_ffn_W1"][bass.ds(e, 1), :, :].rearrange(
                            "e (c p) n -> p (e c) n", p=P)).then_inc(w_loaded, 16)
                        pool.dma_start(w2_in[:, :, :], dram["L2_ffn_W2"][bass.ds(e, 1), :, :].rearrange(
                            "e (c p) n -> p (e c) n", p=P)).then_inc(w_loaded, 16)
                        pool.wait_ge(w_loaded, 32 * (e + 1))
                        pool.wait_ge(expert_used, e + 1)
                        for source, parts in ((w1_in, w1), (w2_in, w2)):
                            pool.tensor_tensor(parts[0][:, j, :, :], source[:, :, :],
                                               one[:, :].unsqueeze(2).broadcast_to(source.shape), ALU.mult).then_inc(w_split, 1)
                        pool.wait_ge(w_split, 2 * e + 2)
                        for source, parts in ((w1_in, w1), (w2_in, w2)):
                            pool.tensor_tensor(parts[1][:, j, :, :], source[:, :, :], parts[0][:, j, :, :],
                                               ALU.subtract).then_inc(expert_ready, 1)
                        pool.wait_ge(expert_ready, 2 * e + 2)

            @block.scalar
            def _(act):
                with act.Fori(0, G) as g:
                    act.wait_ge(routed, GU * g)
                    act.wait_ge(x_low_ready, g)
                    norm_group_act(act, n, g, ps_h)
                    act.activation(x_part[0][:, :, bass.ds(g * GT, GT)], ps_h[:, 0:DC, 0:GT], ACT.Copy).then_inc(x_high_ready, 1)
                act.wait_ge(prob_in, 1)
                act.activation(prob[0:T, :, :], logits[0:T, :, :], ACT.Exp).then_inc(prob_exp, 1)
                act.wait_ge(weight_turned, 1)
                act.activation(weightT[:, :, :], ps_y[:, 0:2, 0:T], ACT.Copy).then_inc(weightT_ready, 1)
                with act.Fori(0, E * G) as r:
                    act.wait_ge(y_done, r)
                    for k in range(PAIRS):
                        act.wait_ge(h_done, PAIRS * r + k + 1)
                        act.wait_ge(low_ready, PAIRS * r + k + 1)
                        act.activation(gelu[:, k % 2, :, :], ps_h[:, 2 * (k % 2):2 * (k % 2) + 2, 0:GT], ACT.Gelu)
                        act.activation(act1[0][:, 2 * k:2 * k + 2, :], ps_h[:, 2 * (k % 2):2 * (k % 2) + 2, 0:GT],
                                       ACT.Gelu).then_inc(high_ready, 1)
                act.wait_ge(summed_up, E * G + 1)
                with act.Fori(0, G // 2) as i:
                    for j, fixed in enumerate((n.xT, weighted)):
                        g = 2 * i + j
                        act.wait_ge(out_turned, g + 1)
                        act.activation(fixed[:, :, :], total_out[:, :, bass.ds(g * GT, GT)], ACT.Copy).then_inc(outT_ready, 1)

            @block.tensor
            def _(pe):
                pe.wait_ge(router_loaded, 16)
                norm_group_pe(pe, n, 0, ps_h, ident)

                def route(g, last):
                    pe.wait_ge(n.xT_ready, 2 * g + 2)
                    pe.wait_ge(logits_ready, g)
                    for u in range(GU):
                        for c in range(DC):
                            mm = pe.matmul(ps_y[0:T, 0, u * E:(u + 1) * E], n.xT[:, c, u * T:(u + 1) * T], w_router[:, c, :],
                                           start=(c == 0), stop=(c == DC - 1))
                        mm.then_inc(routed, 1)
                    if not last:
                        pe.wait_ge(x_high_ready, g + 1)
                        norm_group_pe(pe, n, g + 1, ps_h, ident)

                over_groups(pe, route)
                pe.wait_ge(weight_ready, 1)
                for k in range(2):
                    mm = pe.transpose(ps_y[:, k, 0:T], weight[0:T, k * B // 2:(k + 1) * B // 2, :].rearrange("p b e -> p (b e)"),
                                      ident[0:T, 0:T])
                mm.then_inc(weight_turned, 1)
                pe.wait_ge(weightT_ready, 1)
                pe.wait_ge(x_low_ready, G)
                with pe.Fori(0, E // 2) as i:
                    for j in range(2):
                        with pe.Fori(0, G // 2) as h:
                            for odd in range(2):
                                g = 2 * h + odd
                                r = (2 * i + j) * G + g
                                pe.wait_ge(expert_ready, 2 * (2 * i + j) + 2)
                                for k in range(PAIRS):
                                    pe.wait_ge(high_ready, PAIRS * r + k + 1)
                                    for f in (2 * k, 2 * k + 1):
                                        for c in range(DC):
                                            mm = split_products(pe, ps_h[:, f % 4, 0:GT],
                                                                [w[:, j, c, f * P:(f + 1) * P] for w in w1],
                                                                [part[:, c, bass.ds(g * GT, GT)] for part in x_part],
                                                                c == 0, c == DC - 1)
                                    mm.then_inc(h_done, 1)
                                pe.wait_ge(y_read, r + 1)
                                for f in range(FC):
                                    if f % 2 == 0:
                                        pe.wait_ge(low_ready, PAIRS * r + f // 2 + 3)
                                    for m in range(DC):
                                        mm = split_products(pe, ps_y[:, 2 * odd + m, 0:GT],
                                                            [w[:, j, f, m * P:(m + 1) * P] for w in w2],
                                                            [part[:, f, :] for part in act1], f == 0, f == FC - 1)
                                mm.then_inc(y_done, 1)
                with pe.Fori(0, G // 2) as i:
                    for j, fixed in enumerate((n.xT, weighted)):
                        pe.wait_ge(outT_ready, 2 * i + j + 1)
                        pe.wait_ge(out_added, 2 * i + j + 1)
                        for u in range(GU):
                            for c in range(DC):
                                mm = pe.transpose(ps_out[0:T, GU * j + u, c * P:(c + 1) * P], fixed[:, c, u * T:(u + 1) * T],
                                                  ident[:, :])
                        mm.then_inc(out_turned, 1)

            @block.vector
            def _(dve):
                dve.sem_inc(expert_used, 2)
                dve.sem_inc(high_ready, 2)
                dve.sem_inc(low_ready, 2)
                dve.sem_inc(y_read, 2)
                dve.sem_inc(out_turned, 2)
                dve.sem_inc(out_added, 2)
                norm_statistics_dve(dve, n, hidden, 1e-5, True)
                norm_group_dve(dve, n, 0, hidden)

                def route(g, last):
                    if not last:
                        norm_group_dve(dve, n, g + 1, hidden)
                    dve.wait_ge(x_high_ready, g + 1)
                    dve.tensor_tensor(x_part[1][:, :, bass.ds(g * GT, GT)], n.xT[:, :, :], x_part[0][:, :, bass.ds(g * GT, GT)],
                                      ALU.subtract).then_inc(x_low_ready, 1)
                    dve.wait_ge(routed, GU * g + GU)
                    dve.tensor_copy(logits[0:T, bass.ds(GU * g, GU), :],
                                    ps_y[0:T, 0, 0:GU * E].rearrange("p (u e) -> p u e", e=E)).then_inc(logits_ready, 1)

                over_groups(dve, route)
                dve.wait_ge(logits_ready, G)
                dve.wait_ge(restart_ready, 2)
                rows, wide = slice(0, T), [T, B, E]
                steps = Chain(dve, step)
                steps.link(dve.tensor_reduce(total[rows, 0, :], logits[rows, :, :], AX.X, ALU.max))
                dve.tensor_tensor(logits[rows, :, :], logits[rows, :, :], total[rows, 0, :].unsqueeze(2).broadcast_to(wide),
                                  ALU.subtract).then_inc(prob_in, 1)
                dve.wait_ge(prob_exp, 1)
                steps.link(dve.tensor_reduce(total[rows, 0, :], prob[rows, :, :], AX.X, ALU.add))
                steps.link(dve.reciprocal(total[rows, 1, :], total[rows, 0, :]))
                steps.link(dve.tensor_tensor(prob[rows, :, :], prob[rows, :, :],
                                             total[rows, 1, :].unsqueeze(2).broadcast_to(wide), ALU.mult))
                choose_two_dve(dve, steps, prob, rows, wide, restart, work, chosen)
                dve.tensor_tensor(weight[rows, :, :], prob[rows, :, :], chosen[rows, :, :], ALU.mult).then_inc(weight_ready, 1)
                dve.wait_ge(summed_up, 1)
                with dve.Fori(0, E) as e:
                    with dve.Fori(0, G // 2) as h:
                        for odd in range(2):
                            r = e * G + 2 * h + odd
                            for k in range(PAIRS):
                                dve.wait_ge(high_ready, PAIRS * r + k + 3)
                                dve.tensor_tensor(act1[1][:, 2 * k:2 * k + 2, :], gelu[:, k % 2, :, :], act1[0][:, 2 * k:2 * k + 2, :],
                                                  ALU.subtract).then_inc(low_ready, 1)
                            dve.wait_ge(token_weight_loaded[odd], 16 * (e * (G // 2) + h + 1))
                            dve.wait_ge(y_done, r + 1)
                            dve.wait_ge(summed_up, r + 1)
                            dve.tensor_tensor(weighted[:, :, :], ps_y[:, 2 * odd:2 * odd + 2, 0:GT],
                                              token_weight[:, odd, :].unsqueeze(1).broadcast_to([P, DC, GT]),
                                              ALU.mult).then_inc(y_read, 1)
                            dve.wait_ge(y_read, r + 3)
                            at = bass.ds((2 * h + odd) * GT, GT)
                            dve.tensor_tensor(total_out[:, :, at], total_out[:, :, at], weighted[:, :, :],
                                              ALU.add).then_inc(summed_up, 1)
                    dve.wait_ge(summed_up, (e + 1) * G + 1)
                    dve.sem_inc(expert_used, 1)
                with dve.Fori(0, G // 2) as i:
                    for j in range(2):
                        g = 2 * i + j
                        at = bass.ds(GU * g, GU)
                        dve.wait_ge(out_turned, g + 3)
                        dve.tensor_tensor(hidden[0:T, at, :], hidden[0:T, at, :], ps_out[0:T, GU * j:GU * (j + 1), :],
                                          ALU.add).then_inc(out_added, 1)
                        for u in range(GU):
                            measure_dve(dve, shared, GU * g + u, out_added, g + 3)



def over_pairs(eng, body):
    with eng.Fori(0, G // 2 - 1) as i:
        for j in range(2):
            body(2 * i + j, j, False)
    body(G - 2, 0, False)
    body(G - 1, 1, True)


def used(eng, sem, count):
    if not isinstance(count, int) or count > 0:
        eng.wait_ge(sem, count)


def state_space(nc, shared, dram):
    hidden, ident, minus_half = (shared[k] for k in ("hidden", "ident", "minus_half"))
    CH, N, TAPS, RANK = 512, 16, 4, 16
    CC = CH // P
    ROWS = RANK + 2 * N
    LN_EPS = 1e-5
    nodes = (np.cos(np.pi * (np.arange(64) + 0.5) / 64) + 1) / 18
    fit = np.polynomial.Chebyshev.fit(nodes, 2 * np.arctanh(np.sqrt(nodes)) / np.sqrt(nodes), 4, domain=[0, 1 / 9])
    ARTANH = [float(x) for x in fit.convert(kind=np.polynomial.Polynomial).coef]
    with Scope(nc, "ssm") as s:
        n = Norm(s, shared["stat"])
        w_in = s.sb("w_in", [P, DC, 2 * CH])
        w_x = s.sb("w_x", [P, CC, ROWS])
        w_dt = s.sb("w_dt", [RANK, CH])
        w_out = s.sb("w_out", [P, CC, D])
        taps = s.sb("taps", [P, CC, TAPS])
        cols = s.sb("cols", [P, 3, CC])
        decay = s.sb("decay", [P, CC, N])
        gamma = s.sb("gamma", [P, D])
        beta = s.sb("beta", [P, D])
        x_in = s.sb("x_in", [P, CC, GT])
        conv = s.sb("conv", [P, CC, GT])
        xc = s.sb("xc", [P, 2, CC, GT])
        gate = s.sb("gate", [P, 2, CC, GT])
        xns = [n.xn, s.sb("xn1", [P, GU, D])]
        two = s.sb("two", [P, 1])
        dbc = s.sb("dbc", [ROWS, GT])
        pos = s.sb("pos", [P, CC, GT])
        mag = s.sb("mag", [P, CC, GT])
        delta = s.sb("delta", [P, CC, GT])
        du = s.sb("du", [P, CC, GT])
        ratio, square = conv, x_in
        bc = s.sb("bc", [P, 2, 2, 2, GT])
        dA = s.sb("dA", [P, 2, CC, GU, T])
        dBx = s.sb("dBx", [P, 2, CC, GT])
        state = s.sb("state", [P, 2, CC, GT])
        hC = s.sb("hC", [P, 2, CC, GT])
        rstat = s.sb("rstat", [P, GU, 6])
        ragg = s.sb("ragg", [P, 3, GU])
        rroot = s.sb("rroot", [P, 2, GU])
        ps_a = s.ps("wide", [P, 4, 512])
        ps_b = s.ps("out", [P, 2, 512])
        ps_c = s.ps("ahead", [P, 2, 512])
        names = ("w_loaded dA_zeroed decay_exp decay_ready xz_done xz_ready conv_ready xc_ready dbc_done dbc_ready "
                 "dbc_stored delta_done relu_ready exp_ready ln_ready recip_ready mag_ready ratio_ready square_ready "
                 "sp_ready delta_ready du_ready dA_ready dbx_ready scanned hc_ready y_acc y_taken yT_ready out_done "
                 "step_ahead step spread2 rooted2 group_done").split()
        sem = {k: s.sem(k) for k in names}
        (w_loaded, dA_zeroed, decay_exp, decay_ready, xz_done, xz_ready, conv_ready, xc_ready, dbc_done, dbc_ready,
         dbc_stored, delta_done, relu_ready, exp_ready, ln_ready, recip_ready, mag_ready, ratio_ready, square_ready,
         sp_ready, delta_ready, du_ready, dA_ready, dbx_ready, scanned, hc_ready, y_acc, y_taken, yT_ready,
         out_done, step_ahead, step, spread2, rooted2, group_done) = (sem[k] for k in names)
        bc_loaded = [s.sem(f"bc_loaded{j}") for j in range(2)]
        scratch = nc.dram_tensor("dbc_rows", (G, ROWS, GT), F32, kind="Internal").ap()
        LOADS = 11
        with nc.Block() as block:
            @block.sync
            def _(sync):
                for tile, name in ((w_in, "L3_attn_W_in"), (w_x, "L3_attn_W_x"), (w_out, "L3_attn_W_out"),
                                   (taps, "L3_attn_conv_w"), (decay, "L3_attn_A_log")):
                    sync.dma_start(tile[:, :, :], dram[name].rearrange("(c p) n -> p c n", p=P)).then_inc(w_loaded, 16)
                sync.dma_start(w_dt[:, :], dram["L3_attn_W_dt"]).then_inc(w_loaded, 16)
                for k, name in enumerate(("conv_b", "b_dt", "D")):
                    sync.dma_start(cols[:, k, :], dram[f"L3_attn_{name}_col"]).then_inc(w_loaded, 16)
                load_rows(sync, gamma[0:T, :], dram["L3_attn_gamma"], w_loaded)
                load_rows(sync, beta[0:T, :], dram["L3_attn_beta"], w_loaded)

                def store(g):
                    sync.wait_ge(dbc_ready, g + 1)
                    sync.dma_start(scratch[bass.ds(g, 1), :, :].rearrange("g r t -> (g r) t"), dbc[:, :]).then_inc(dbc_stored, 16)

                def group(g, last):
                    sync.wait_ge(dbc_stored, 16 * (g + 1))
                    for q in range(N // 2):
                        sync.wait_ge(hc_ready, N * g + (2 * q + 2))
                        for k in range(2):
                            r = RANK + k * N + 2 * q
                            sync.dma_start(bc[:, q % 2, k, :, :].rearrange("p r t -> p (r t)"),
                                           scratch[bass.ds(g, 1), r:r + 2, :].rearrange("g r t -> (g r t)").partition_broadcast(P)
                                           ).then_inc(bc_loaded[q % 2], 16)
                    if not last:
                        store(g + 1)

                store(0)
                over_groups(sync, group)

            @block.gpsimd
            def _(pool):
                norm_root_pool(pool, n, minus_half)
                pool.memset(two[:, :], 2.0).then_inc(dA_zeroed, 1)
                pool.memset(rroot[:, :, :], 1.0).then_inc(spread2, 1)
                pool.memset(dA[:, :, :, :, :], 0.0).then_inc(dA_zeroed, 1)

                def group(g, j, last):
                    pool.wait_ge(sp_ready, g + 1)
                    pool.wait_ge(dA_ready, N * g)
                    pool.tensor_tensor(delta[:, :, :], pos[:, :, :], mag[:, :, :], ALU.add).then_inc(delta_ready, 1)
                    pool.wait_ge(delta_ready, g + 1)
                    pool.tensor_tensor(du[:, :, :], delta[:, :, :], xc[:, j, :, :], ALU.mult).then_inc(du_ready, 1)
                    root(g)
                    pool.wait_ge(du_ready, g + 1)
                    for k in range(N):
                        q = k // 2
                        pool.wait_ge(bc_loaded[q % 2], 32 * (N // 4) * g + 32 * (q // 2 + 1))
                        pool.wait_ge(scanned, N * g + k + 1)
                        pool.tensor_tensor(dBx[:, k % 2, :, :], du[:, :, :],
                                           bc[:, q % 2, 0, k % 2, :].unsqueeze(1).broadcast_to([P, CC, GT]),
                                           ALU.mult).then_inc(dbx_ready, 1)

                def root(g):
                    pool.wait_ge(spread2, g + 1)
                    pool.tensor_tensor(rroot[0:T, 1, :], rroot[0:T, 0, :], minus_half[0:T, 0:GU], ALU.pow).then_inc(rooted2, 1)

                over_pairs(pool, group)
                root(G)

            @block.scalar
            def _(act):
                act.wait_ge(w_loaded, 16 * LOADS)
                act.activation(decay[:, :, :], decay[:, :, :], ACT.Exp).then_inc(decay_exp, 1)
                act.wait_ge(decay_ready, 1)
                act.wait_ge(dA_zeroed, 2)

                def ahead(g, j, k):
                    if k == 3:
                        act.wait_ge(xz_done, 8 * g)
                        norm_group_act(act, n, g, ps_c)
                    if 5 <= k <= 8:
                        if k == 5:
                            act.wait_ge(sp_ready, g)
                            act.wait_ge(conv_ready, CC * g)
                            used(act, yT_ready, g - 1)
                        for m in (2 * k - 10, 2 * k - 9):
                            act.wait_ge(xz_done, 8 * g + m + 1)
                            act.activation(x_in[:, m, :] if m < CC else gate[:, j, m - CC, :], ps_c[:, m % 2, 0:GT],
                                           ACT.Copy).then_inc(xz_ready, 1)
                    if k == 10:
                        act.wait_ge(conv_ready, CC * g + CC)
                        used(act, out_done, GU * (g - 1))
                        act.activation(xc[:, j, :, :], conv[:, :, :], ACT.Silu)
                        act.wait_ge(xz_ready, 8 * g + 8)
                        act.activation(gate[:, j, :, :], gate[:, j, :, :], ACT.Silu).then_inc(xc_ready, 1)
                    if k == 12:
                        act.wait_ge(dbc_done, g + 1)
                        act.wait_ge(dbc_stored, 16 * g)
                        act.activation(dbc[:, :], ps_c[0:ROWS, 0, 0:GT], ACT.Copy).then_inc(dbc_ready, 1)
                    if k in (14, 15):
                        act.wait_ge(delta_ready, g)
                        for c in (2 * k - 28, 2 * k - 27):
                            act.wait_ge(delta_done, CC * g + c + 1)
                            act.activation(mag[:, c, :], ps_c[:, c % 2, 0:GT], ACT.Abs, bias=cols[:, 1, c:c + 1])
                            act.activation(pos[:, c, :], ps_c[:, c % 2, 0:GT], ACT.Relu, bias=cols[:, 1, c:c + 1]).then_inc(relu_ready, 1)
                    if k == 15:
                        act.wait_ge(relu_ready, CC * g + CC)
                        act.activation(mag[:, :, :], mag[:, :, :], ACT.Exp, scale=-1.0).then_inc(exp_ready, 1)
                        act.wait_ge(exp_ready, g + 1)
                        act.activation(ratio[:, :, :], mag[:, :, :], ACT.Ln, bias=two[:, 0:1]).then_inc(ln_ready, 1)
                        act.wait_ge(ln_ready, g + 1)
                        act.activation(ratio[:, :, :], ratio[:, :, :], ACT.Exp, scale=-1.0).then_inc(recip_ready, 1)
                        act.wait_ge(ratio_ready, g + 1)
                        act.activation(square[:, :, :], ratio[:, :, :], ACT.Square).then_inc(square_ready, 1)

                def group(g, j, last):
                    act.wait_ge(delta_ready, g + 1)
                    for k in range(N):
                        act.wait_ge(scanned, N * g + k + 1)
                        for c in range(CC):
                            ins = act.activation(dA[:, k % 2, c, :, 1:],
                                                 delta[:, c, :].rearrange("p (u t) -> p u t", u=GU)[:, :, 1:], ACT.Exp,
                                                 scale=decay[:, c, k:k + 1])
                        ins.then_inc(dA_ready, 1)
                        if not last:
                            ahead(g + 1, 1 - j, k)

                for k in range(N):
                    ahead(0, 0, k)
                over_pairs(act, group)

            @block.tensor
            def _(pe):
                pe.wait_ge(w_loaded, 16 * LOADS)

                def ahead(g, j, k):
                    if k == 0:
                        n.xn = xns[j]
                        pe.wait_ge(relu_ready, CC * g)
                        norm_group_pe(pe, n, g, ps_c, ident)
                    if 2 <= k <= 5:
                        for m in (2 * k - 4, 2 * k - 3):
                            if m < 2:
                                pe.wait_ge(n.xT_ready, 2 * g + 2)
                            else:
                                pe.wait_ge(xz_ready, 8 * g + m - 1)
                            for c in range(DC):
                                mm = pe.matmul(ps_c[:, m % 2, 0:GT], w_in[:, c, m * P:(m + 1) * P], n.xT[:, c, :],
                                               start=(c == 0), stop=(c == DC - 1))
                            mm.then_inc(xz_done, 1)
                    if k == 8:
                        pe.wait_ge(xc_ready, g + 1)
                        for c in range(CC):
                            mm = pe.matmul(ps_c[0:ROWS, 0, 0:GT], w_x[:, c, :], xc[:, j, c, :], start=(c == 0), stop=(c == CC - 1))
                        mm.then_inc(dbc_done, 1)
                    if k in (10, 12):
                        pe.wait_ge(dbc_ready, g + 1)
                        for c in (k - 10, k - 9):
                            if c >= 2:
                                pe.wait_ge(relu_ready, CC * g + c - 1)
                            pe.matmul(ps_c[:, c % 2, 0:GT], w_dt[:, c * P:(c + 1) * P], dbc[0:RANK, :], start=True,
                                      stop=True).then_inc(delta_done, 1)

                def group(g, j, last):
                    pe.wait_ge(y_taken, CC * g)
                    for k in range(N):
                        pe.wait_ge(hc_ready, N * g + (k + 5))
                        for c in range(CC):
                            mm = pe.matmul(ps_a[:, c, 0:GT], ident[:, :], hC[:, k % 2, c, :], start=(k == 0),
                                           stop=(k == N - 1))
                        mm.then_inc(y_acc, 1)
                        if not last:
                            ahead(g + 1, 1 - j, k)
                    pe.wait_ge(yT_ready, g + 1)
                    pe.wait_ge(group_done, g)
                    for u in range(GU):
                        for c in range(CC):
                            mm = pe.matmul(ps_b[0:T, u // 2, u % 2 * D:(u % 2 + 1) * D], xc[:, j, c, u * T:(u + 1) * T],
                                           w_out[:, c, :], start=(c == 0), stop=(c == CC - 1), skip_group_check=True)
                        mm.then_inc(out_done, 1)

                for k in range(N):
                    ahead(0, 0, k)
                over_pairs(pe, group)

            @block.vector
            def _(dve):
                dve.sem_inc(scanned, 2)
                dve.sem_inc(y_acc, 2)
                dve.sem_inc(hc_ready, 4)
                norm_statistics_dve(dve, n, hidden, 1e-5, True)
                dve.wait_ge(w_loaded, 16 * LOADS)
                dve.wait_ge(decay_exp, 1)
                dve.tensor_scalar(decay[:, :, :], decay[:, :, :], -1.0, None, ALU.mult).then_inc(decay_ready, 1)
                steps_ahead = GroupSteps(dve, step_ahead, 0, 3 * CC + 4)
                steps = GroupSteps(dve, step, 0, 4 + 6 + 4 + 2)
                by_utterance = lambda x: x.rearrange("p (u t) -> p u t", u=GU)
                flat = lambda x: x[:, :, :].rearrange("p c t -> p (c t)")

                def ahead(g, j, k):
                    if k == 0:
                        n.xn = xns[j]
                        steps_ahead.begin(g)
                        used(dve, group_done, g - 1)
                        norm_group_dve(dve, n, g, hidden)
                    if k in (5, 6):
                        for c in (2 * k - 10, 2 * k - 9):
                            dve.wait_ge(xz_ready, 8 * g + c + 1)
                            if k == 5:
                                dve.wait_ge(xc_ready, g)
                                dve.wait_ge(square_ready, g)
                            steps_ahead.link(dve.tensor_scalar(conv[:, c, :], x_in[:, c, :], taps[:, c, TAPS - 1:TAPS],
                                                               cols[:, 0, c:c + 1], ALU.mult, ALU.add))
                            for back in range(1, TAPS):
                                to = by_utterance(conv[:, c, :])[:, :, back:]
                                ins = dve.scalar_tensor_tensor(to, by_utterance(x_in[:, c, :])[:, :, 0:T - back],
                                                               taps[:, c, TAPS - 1 - back:TAPS - back], to, ALU.mult, ALU.add)
                                if back < TAPS - 1:
                                    steps_ahead.link(ins)
                                else:
                                    ins.then_inc(conv_ready, 1)

                def logarithm(g):
                    dve.wait_ge(recip_ready, g + 1)
                    dve.tensor_tensor(ratio[:, :, :], mag[:, :, :], ratio[:, :, :], ALU.mult).then_inc(ratio_ready, 1)
                    dve.wait_ge(square_ready, g + 1)
                    steps_ahead.link(dve.tensor_scalar(mag[:, :, :], square[:, :, :], ARTANH[-1], None, ALU.mult))
                    for coefficient in ARTANH[-2:0:-1]:
                        steps_ahead.link(dve.scalar_tensor_tensor(flat(mag), flat(mag), coefficient, flat(square), ALU.add, ALU.mult))
                    dve.scalar_tensor_tensor(flat(mag), flat(mag), ARTANH[0], flat(ratio), ALU.add, ALU.mult).then_inc(sp_ready, 1)
                    steps_ahead.end()

                def group(g, j, last):
                    for k in range(N):
                        q = k // 2
                        dve.wait_ge(dA_ready, N * g + k + 1)
                        dve.wait_ge(dbx_ready, N * g + k + 1)
                        dve.wait_ge(hc_ready, N * g + (3 + k))
                        dve.tensor_tensor_scan(state[:, k % 2, :, :].rearrange("p c t -> p (c t)"),
                                               dA[:, k % 2, :, :, :].rearrange("p c u t -> p (c u t)"),
                                               dBx[:, k % 2, :, :].rearrange("p c t -> p (c t)"), 0.0, ALU.mult,
                                               ALU.add).then_inc(scanned, 1)
                        dve.wait_ge(scanned, N * g + (k + 3))
                        dve.wait_ge(y_acc, N * g + k + 1)
                        dve.tensor_tensor(hC[:, k % 2, :, :], state[:, k % 2, :, :],
                                          bc[:, q % 2, 1, k % 2, :].unsqueeze(1).broadcast_to([P, CC, GT]),
                                          ALU.mult).then_inc(hc_ready, 1)
                        if not last:
                            ahead(g + 1, 1 - j, k)
                    dve.wait_ge(y_acc, N * g + (2 + N))
                    dve.wait_ge(du_ready, g + 1)
                    for c in range(CC):
                        dve.scalar_tensor_tensor(xc[:, j, c, :], xc[:, j, c, :], cols[:, 2, c:c + 1], ps_a[:, c, 0:GT], ALU.mult,
                                                 ALU.add).then_inc(y_taken, 1)
                    dve.wait_ge(y_taken, CC * g + CC)
                    dve.tensor_tensor(xc[:, j, :, :], xc[:, j, :, :], gate[:, j, :, :], ALU.mult).then_inc(yT_ready, 1)
                    if not last:
                        logarithm(g + 1)
                    steps.begin(g)
                    res = xns[j]
                    for half in range(2):
                        dve.wait_ge(out_done, GU * g + 2 * half + 2)
                        rows = res[0:T, 2 * half:2 * half + 2, :].rearrange("p u d -> p (u d)")
                        steps.link(dve.tensor_tensor(rows, ps_b[0:T, half, :], rows, ALU.add))
                        for u in (2 * half, 2 * half + 1):
                            ins = dve.bn_stats(rstat[0:T, u, :], res[0:T, u, :])
                        steps.link(ins)
                    mean_e, m2_e, mean_o, m2_o = (rstat[0:T, :, k] for k in (1, 2, 4, 5))
                    mean, apart, both = (ragg[0:T, k, :] for k in range(3))
                    steps.link(dve.tensor_tensor(mean, mean_e, mean_o, ALU.add))
                    steps.link(dve.tensor_tensor(apart, mean_e, mean_o, ALU.subtract))
                    steps.link(dve.tensor_tensor(both, m2_e, m2_o, ALU.add))
                    steps.link(dve.tensor_scalar(mean, mean, 0.5, None, ALU.mult))
                    steps.link(dve.tensor_tensor(apart, apart, apart, ALU.mult))
                    steps.link(dve.tensor_scalar(both, both, 1.0 / D, LN_EPS, ALU.mult, ALU.add))
                    dve.scalar_tensor_tensor(rroot[0:T, 0, :], apart, 0.25, both, ALU.mult, ALU.add).then_inc(spread2, 1)
                    dve.wait_ge(rooted2, g + 2)
                    for u in range(GU):
                        steps.link(dve.tensor_scalar(res[0:T, u, :], res[0:T, u, :], ragg[0:T, 0, u:u + 1], rroot[0:T, 1, u:u + 1],
                                                     ALU.subtract, ALU.mult))
                    steps.link(dve.tensor_tensor(res[0:T, :, :], res[0:T, :, :],
                                                 gamma[0:T, :].unsqueeze(1).broadcast_to([T, GU, D]), ALU.mult))
                    steps.link(dve.tensor_tensor(res[0:T, :, :], res[0:T, :, :],
                                                 beta[0:T, :].unsqueeze(1).broadcast_to([T, GU, D]), ALU.add))
                    at = bass.ds(GU * g, GU)
                    dve.tensor_tensor(hidden[0:T, at, :], hidden[0:T, at, :], res[0:T, :, :], ALU.add).then_inc(group_done, 1)
                    steps.end()

                for k in range(N):
                    ahead(0, 0, k)
                logarithm(0)
                over_pairs(dve, group)



def expert_attention(nc, shared, dram):
    hidden, ident, ident16, minus_half = (shared[k] for k in ("hidden", "ident", "ident16", "minus_half"))
    E, R, GH = 8, 16, 64
    Q, K, V, O = range(4)
    with Scope(nc, "eattn") as s:
        n = Norm(s)
        a = Attention(s, HEADS, False, 1.0 / math.sqrt(HD))
        w = s.sb("w", [P, DC, 4 * D])
        up = s.sb("up", [P, 4, D])
        down = s.sb("down", [P, DC, 4, P])
        strength = s.sb("strength", [P, 4])
        gated = s.sb("gated", [P, 4, B])
        qk_bias = s.sb("qk_bias", [P, 2, DC])
        v_bias = s.sb("v_bias", [P, D])
        o_bias = s.sb("o_bias", [P, D])
        gw1 = s.sb("gw1", [P, DC, GH])
        gw2 = s.sb("gw2", [GH, E])
        gb1 = s.sb("gb1", [GH, 1])
        gb2 = s.sb("gb2", [P, E])
        one = s.sb("one", [P, 1])
        pooled = s.sb("pooled", [P, DC, B])
        gate_h = s.sb("gate_h", [GH, B])
        score = s.sb("score", [P, 1, E])
        gate_e = s.sb("gate_e", [P, 1, E])
        chosen = s.sb("chosen", [P, 1, E])
        restart = s.sb("restart", [P, 1, E])
        total = s.sb("total", [P, 3])
        wide = s.sb("wide", [P, E, R])
        work = choice_buffers(s, 1, E)
        ranks = s.sb("ranks", [P, 3, GT])
        ranks_o = s.sb("ranks_o", [P, T])
        summed = s.sb("summed", [P, D])
        (w_loaded, restart_ready, pooled_ready, gates_done, gate_h_ready, gate_in, gate_exp, wide_ready, gated_ready,
         down_done, ranks_in, down_o_done) = (s.sem(k) for k in (
             "w_loaded", "restart_ready", "pooled_ready", "gates_done", "gate_h_ready", "gate_in", "gate_exp",
             "wide_ready", "gated_ready", "down_done", "ranks_in", "down_o_done"))
        a.ranks_ready = s.sem("ranks_ready")
        LOADS = 4 * 4 + 2 + 2 + 4
        with nc.Block() as block:
            @block.sync
            def _(sync):
                for k, name in enumerate("qkvo"):
                    sync.dma_start(w[:, :, k * D:(k + 1) * D], dram[f"L3_ffn_{name}Wm"].rearrange("(c p) n -> p c n", p=P)
                                   ).then_inc(w_loaded, 16)
                    sync.dma_start(up[:, k, :], dram[f"L3_ffn_{name}U"]).then_inc(w_loaded, 16)
                    sync.dma_start(down[:, :, k, :], dram[f"L3_ffn_{name}V"].rearrange("(c p) n -> p c n", p=P)
                                   ).then_inc(w_loaded, 16)
                    sync.dma_start(strength[:, k:k + 1], dram[f"L3_ffn_{name}S"].rearrange("(e a) -> e a", a=1)
                                   ).then_inc(w_loaded, 16)
                for k, name in enumerate("qk"):
                    sync.dma_start(qk_bias[:, k, :], dram[f"L3_ffn_{name}b_col"]).then_inc(w_loaded, 16)
                load_rows(sync, v_bias[0:T, :], dram["L3_ffn_vb"], w_loaded)
                load_rows(sync, o_bias[0:T, :], dram["L3_ffn_ob"], w_loaded)
                sync.dma_start(gw1[:, :, :], dram["L3_ffn_gw1"].rearrange("(c p) n -> p c n", p=P)).then_inc(w_loaded, 16)
                sync.dma_start(gw2[:, :], dram["L3_ffn_gw2"]).then_inc(w_loaded, 16)
                sync.dma_start(gb1[:, :], dram["L3_ffn_gb1"].rearrange("(e a) -> e a", a=1)).then_inc(w_loaded, 16)
                load_rows(sync, gb2[0:B, :], dram["L3_ffn_gb2"], w_loaded, rows=B)

            @block.gpsimd
            def _(pool):
                pool.memset(restart[:, :, :], 1.0).then_inc(restart_ready, 1)
                pool.wait_ge(restart_ready, 1)
                pool.memset(restart[:, :, 0:1], 0.0).then_inc(restart_ready, 1)
                pool.memset(one[:, :], 1.0).then_inc(restart_ready, 1)
                norm_root_pool(pool, n, minus_half)
                attention_constants_pool(pool, a)
                attention_pool(pool, a)

            @block.scalar
            def _(act):
                act.wait_ge(w_loaded, 16 * LOADS)
                act.wait_ge(n.turned, B)
                act.activation(pooled[:, :, :], a.ps_s[:, 1, 0:DC * B], ACT.Copy).then_inc(pooled_ready, 1)
                act.wait_ge(gates_done, 1)
                act.activation(gate_h[:, :], a.ps_s[0:GH, 0, 0:B], ACT.Relu, scale=1.0 / T, bias=gb1[:, 0:1]
                               ).then_inc(gate_h_ready, 1)
                act.wait_ge(gate_in, 1)
                act.activation(gate_e[0:B, 0, :], score[0:B, 0, :], ACT.Exp).then_inc(gate_exp, 1)
                act.wait_ge(gated_ready, 4)
                norm_group_act(act, n, G, a.ps_o)

                def group(g, last):
                    for k in range(3):
                        act.wait_ge(down_done, 3 * g + k + 1)
                        for u in range(GU):
                            ins = act.activation(ranks[:, k, u * T:(u + 1) * T], a.ps_g[:, (k + 1) % 2, u * T:(u + 1) * T],
                                                 ACT.Copy, scale=gated[:, k, bass.ds(GU * g + u, 1)])
                        ins.then_inc(ranks_in, 1)
                    queries_keys_act(act, a, g, qk_bias[:, 0, :], qk_bias[:, 1, :])
                    if not last:
                        act.wait_ge(a.v_done, GU * (g + 1))
                        norm_group_act(act, n, g + (G + 1), a.ps_o)

                over_groups(act, group)

                def ranks_out(b):
                    act.wait_ge(down_o_done, b + 1)
                    act.activation(ranks_o[:, :], a.ps_g[:, 1, 0:T], ACT.Copy,
                                   scale=gated[:, O, bass.ds(b, 1)]).then_inc(a.ranks_ready, 1)

                attention_act(act, a, extra=ranks_out)

            @block.tensor
            def _(pe):
                pe.wait_ge(w_loaded, 16 * LOADS)
                pe.wait_ge(restart_ready, 3)
                with pe.Fori(0, G) as g:
                    for u in range(GU):
                        b = GU * g + u
                        pe.wait_ge(n.normed, b + 1)
                        for c in range(DC):
                            mm = pe.matmul(a.ps_s[:, 1, bass.ds(c * B + b, 1)], n.xn[0:T, u, c * P:(c + 1) * P], one[0:T, :],
                                           start=True, stop=True, skip_group_check=True)
                        mm.then_inc(n.turned, 1)
                pe.wait_ge(pooled_ready, 1)
                for c in range(DC):
                    mm = pe.matmul(a.ps_s[0:GH, 0, 0:B], gw1[:, c, :], pooled[:, c, :], start=(c == 0), stop=(c == DC - 1))
                mm.then_inc(gates_done, 1)
                pe.wait_ge(gate_h_ready, 1)
                pe.matmul(a.ps_t[0:B, 0, 0:E], gate_h[:, :], gw2[:, :], start=True, stop=True).then_inc(gates_done, 1)
                pe.wait_ge(wide_ready, 1)
                pe.transpose(a.ps_t[:, 1, 0:B], wide[0:B, :, :], ident[0:B, 0:B]).then_inc(gates_done, 1)
                pe.wait_ge(gated_ready, 4)
                norm_group_pe(pe, n, G, a.ps_o, ident)

                def group(g, last):
                    pe.wait_ge(n.xT_ready, 2 * g + 2)
                    for k in range(3):
                        if k < 2:
                            pe.wait_ge(a.v_ready, GU * g)
                        else:
                            pe.wait_ge(ranks_in, 3 * g + 1)
                        for c in range(DC):
                            mm = pe.matmul(a.ps_g[:, (k + 1) % 2, 0:GT], down[:, c, k, :], n.xT[:, c, :], start=(c == 0),
                                           stop=(c == DC - 1))
                        mm.then_inc(down_done, 1)
                    for k, bank, done, read in ((Q, a.ps_s, a.q_done, a.q_ready), (K, a.ps_t, a.k_done, a.k_ready)):
                        pe.wait_ge(read, DC * g)
                        for m in range(DC):
                            at = k * D + m * P
                            for c in range(DC):
                                pe.matmul(bank[:, m, 0:GT], w[:, c, at:at + P], n.xT[:, c, :], start=(c == 0), stop=False)
                            pe.wait_ge(ranks_in, 3 * g + 1 + k)
                            pe.matmul(bank[:, m, 0:GT], up[:, k, m * P:(m + 1) * P], ranks[:, k, :], start=False,
                                      stop=True).then_inc(done, 1)
                    if not last:
                        norm_group_pe(pe, n, g + (G + 1), a.ps_o, ident)
                    pe.wait_ge(ranks_in, 3 * g + 3)
                    for u in range(GU):
                        values_free_pe(pe, a, g, u)
                        for c in range(DC):
                            pe.matmul(a.ps_g[0:T, u % 2, 0:D], n.xT[:, c, u * T:(u + 1) * T], w[:, c, V * D:(V + 1) * D],
                                      start=(c == 0), stop=False)
                        pe.matmul(a.ps_g[0:T, u % 2, 0:D], ranks[:, V, u * T:(u + 1) * T], up[:, V, :], start=False,
                                  stop=True).then_inc(a.v_done, 1)

                over_groups(pe, group)

                def ranks_of_output(b):
                    for c in range(DC):
                        mm = pe.matmul(a.ps_g[:, 1, 0:T], down[:, c, O, :], a.ctxT[:, c, :], start=(c == 0),
                                       stop=(c == DC - 1))
                    mm.then_inc(down_o_done, 1)

                def add_experts(b):
                    pe.wait_ge(a.ranks_ready, b + 1)
                    return pe.matmul(a.ps_g[0:T, 0, 0:D], ranks_o[:, :], up[:, O, :], start=False, stop=True)

                pe.wait_ge(a.const_ready, attention_constants_ready(a))
                attention_pe(pe, a, ident, ident16, w[:, :, O * D:(O + 1) * D], ranks_of_output, add_experts)

            @block.vector
            def _(dve):
                attention_constants_dve(dve, a, ident)
                norm_statistics_dve(dve, n, hidden, 1e-5)
                with dve.Fori(0, G) as g:
                    norm_group_dve(dve, n, g, hidden)
                dve.wait_ge(w_loaded, 16 * LOADS)
                dve.wait_ge(a.step, 1)
                dve.wait_ge(restart_ready, 2)
                dve.wait_ge(gates_done, 2)
                steps = Chain(dve, a.step, 1)
                rows = slice(0, B)
                steps.link(dve.tensor_tensor(score[rows, 0, :], a.ps_t[rows, 0, 0:E], gb2[rows, :], ALU.add))
                choose_two_dve(dve, steps, score, rows, [B, 1, E], restart, work, chosen)
                steps.link(dve.tensor_reduce(total[rows, 0:1], score[rows, 0, :], AX.X, ALU.max))
                dve.tensor_scalar(score[rows, 0, :], score[rows, 0, :], total[rows, 0:1], None, ALU.subtract).then_inc(gate_in, 1)
                dve.wait_ge(gate_exp, 1)
                steps.link(dve.tensor_tensor(gate_e[rows, 0, :], gate_e[rows, 0, :], chosen[rows, 0, :], ALU.mult))
                steps.link(dve.tensor_reduce(total[rows, 1:2], gate_e[rows, 0, :], AX.X, ALU.add))
                steps.link(dve.reciprocal(total[rows, 2:3], total[rows, 1:2]))
                dve.tensor_scalar(wide[rows, :, :], gate_e[rows, 0, :].unsqueeze(2).broadcast_to([B, E, R]), total[rows, 2:3],
                                  None, ALU.mult).then_inc(wide_ready, 1)
                dve.wait_ge(gates_done, 3)
                for k in range(4):
                    dve.tensor_scalar(gated[:, k, :], a.ps_t[:, 1, 0:B], strength[:, k:k + 1], None,
                                      ALU.mult).then_inc(gated_ready, 1)
                base = steps.base
                norm_group_dve(dve, n, 0, hidden, 1)

                def group(g, last):
                    if not last:
                        norm_group_dve(dve, n, g + 1, hidden, 1)
                    for u in range(GU):
                        dve.wait_ge(a.v_done, GU * g + u + 1)
                        dve.tensor_tensor(a.v[0:T, GU * g + u, :, 0:HD],
                                          a.ps_g[0:T, u % 2, 0:D].rearrange("p (h e) -> p h e", h=HEADS),
                                          v_bias[0:T, :].rearrange("p (h e) -> p h e", h=HEADS),
                                          ALU.add).then_inc(a.v_ready, 1)

                over_groups(dve, group)
                steps = GroupSteps(dve, a.step, base, 2)

                def context(b, buf):
                    outputs = a.ps_o[0:T, buf, 0:HEADS * (HD + 1)].rearrange("p (h e) -> p h e", h=HEADS)
                    steps.link(dve.reciprocal(a.rden[0:T, 0, :], outputs[:, :, HD]))
                    steps.link(dve.tensor_tensor(a.ctx[0:T, buf, :].rearrange("p (h e) -> p h e", h=HEADS),
                                                 outputs[:, :, 0:HD],
                                                 a.rden[0:T, 0, :].unsqueeze(2).broadcast_to([T, HEADS, HD]), ALU.mult))
                    dve.sem_inc(a.ctx_ready, 1)
                    dve.sem_inc(a.outputs_read, 1)

                def add(b):
                    dve.wait_ge(a.out_done, b + 1)
                    dve.tensor_tensor(summed[0:T, :], a.ps_g[0:T, 0, 0:D], o_bias[0:T, :], ALU.add).then_inc(a.biased, 1)
                    dve.wait_ge(a.biased, b + 1)
                    dve.tensor_tensor(hidden[0:T, b, :], hidden[0:T, b, :], summed[0:T, :], ALU.add).then_inc(a.added, 1)

                dve.wait_ge(a.const_ready, attention_constants_ready(a))
                attention_dve(dve, a, steps, context, add)


LAYERS = (tokenizer, gated_attention, quantised_linear, layer1_attention, frequency_linear, differential_attention,
          mixture, state_space, expert_attention)



def audio_tower(nc, dram, out):
    with Scope(nc, "top") as top:
        shared = {"hidden": top.sb("hidden", [P, B, D])}
        constants(nc, top, shared)
        for layer in LAYERS:
            layer(nc, shared, dram)
        written = top.sem("written")
        with nc.Block() as block:
            @block.sync
            def _(sync):
                sync.dma_start(out.rearrange("b t d -> t b d"), shared["hidden"][0:T, :, :]).then_inc(written, 16)
                sync.wait_ge(written, 16)



def laid_out(inputs):
    a = {k: np.asarray(v) for k, v in inputs.items()}
    out = {}
    frames = np.zeros((B, (T + 1) * STRIDE, BANDS), a["x"].dtype)
    frames[:, :FRAMES] = a.pop("x")
    out["frames"] = frames.reshape(B, T + 1, STRIDE * BANDS).transpose(2, 0, 1)
    for k, v in a.items():
        out[k.replace("L0_tok", "tok")] = v
    out["tok_W1"] = out["tok_W1"].reshape(2, STRIDE * BANDS, D)
    for k in ("L0_attn_w_qkv", "L0_attn_w_ent", "L0_attn_w_out", "L0_ffn_weight_int8", "L3_ffn_gw1", "L3_ffn_gw2",
              "L3_ffn_qWm", "L3_ffn_kWm", "L3_ffn_vWm", "L3_ffn_oWm"):
        out[k] = out[k].T
    for p in "qkvo":
        U, V, S = (out[f"L3_ffn_{p}{m}"] for m in "UVS")
        out[f"L3_ffn_{p}U"] = U.transpose(0, 2, 1).reshape(-1, D)
        out[f"L3_ffn_{p}V"] = V.reshape(-1, D).T
        out[f"L3_ffn_{p}S"] = S.reshape(-1)
    for k, v in list(out.items()):
        if v.ndim == 1 and v.size % P == 0:
            out[k + "_col"] = v.reshape(-1, P).T
    n = np.arange(D)
    angle = 2.0 * np.pi * (np.outer(n, n) % D) / D
    out["dft"] = np.stack([np.cos(angle), np.sin(angle)]).astype(np.float32)
    out = {k: np.ascontiguousarray(v) for k, v in out.items()}
    out["L0_ffn_weight_int8"] = out["L0_ffn_weight_int8"].view(np.int32)
    return out


def kernel(**inputs):
    import concourse.bacc as bacc
    from concourse.bass_utils import run_bass_kernel_spmd as run

    nc = bacc.Bacc("TRN2", target_bir_lowering=False, num_devices=1)
    arrays, dram = {}, {}
    for name, a in laid_out(inputs).items():
        arrays[f"in_{name}"] = a
        dram[name] = nc.dram_tensor(f"in_{name}", a.shape, mybir.dt.from_np(a.dtype), kind="ExternalInput").ap()
    out = nc.dram_tensor("out", (B, T, D), F32, kind="ExternalOutput").ap()
    audio_tower(nc, dram, out)
    return run(nc, [arrays], core_ids=[0]).results[0]["out"]
```
